# Optimizing a Trainium2 kernel written in Bass

```python
import numpy as np
import jax
import jax.numpy as jnp

def _softmax(x, axis=-1):
    return jax.nn.softmax(x, axis=axis)

def _gelu(x):
    return jax.nn.gelu(x, approximate=True)

def _silu(x):
    return jax.nn.silu(x)

def _sigmoid(x):
    return jax.nn.sigmoid(x)

def _layernorm(x, axis=-1, eps=1e-05):
    m = jnp.mean(x, axis=axis, keepdims=True)
    v = jnp.var(x, axis=axis, keepdims=True)
    return (x - m) / jnp.sqrt(v + eps)

def _scatter_add(tgt, idx, src, axis=0):
    return tgt.at[idx].add(src)

def _segment_sum(src, seg, n):
    return jax.ops.segment_sum(src, seg, n)
kernel_name = 'mk_audio_tower_d1_tok_audfeat2048_r4_b63ad5'

def setup_inputs(seed: int=0):
    np.random.seed(seed)
    _w = jnp.asarray

    def _rec_inputs():
        import jax
        import jax.numpy as jnp
        _rk = jax.random.key(seed)
        x = -0.000392918 + 0.999932 * jax.random.normal(jax.random.fold_in(_rk, 1), (128, 375, 64), jnp.float32)
        return x
    x = _rec_inputs()

    def _L0_tok_setup():
        import jax, jax.numpy as jnp
        import numpy as np
        TIN = 16
        FEAT = 64
        IN_DIM = TIN * FEAT
        HDIM = 512
        EPS = 1e-06

        def layer_norm(x, gamma, beta, eps):
            mu = jnp.mean(x, axis=-1, keepdims=True)
            var = jnp.mean(jnp.square(x - mu), axis=-1, keepdims=True)
            return (x - mu) * jax.lax.rsqrt(var + eps) * gamma + beta
        key = jax.random.key(seed)
        ks = jax.random.split(key, 4)
        x = jax.random.normal(ks[0], (64, 1024, FEAT), dtype=jnp.float32)
        W = jax.random.normal(ks[1], (IN_DIM, HDIM), dtype=jnp.float32) / np.sqrt(IN_DIM)
        b = jnp.zeros((HDIM,), dtype=jnp.float32)
        g1 = jnp.ones((IN_DIM,), dtype=jnp.float32)
        b1 = jnp.zeros((IN_DIM,), dtype=jnp.float32)
        g2 = jnp.ones((HDIM,), dtype=jnp.float32)
        b2 = jnp.zeros((HDIM,), dtype=jnp.float32)
        return {'x': x, 'W': W, 'b': b, 'g1': g1, 'b1': b1, 'g2': g2, 'b2': b2}
    _L0_tok_all = _L0_tok_setup()
    _L0_tok_in = {k: v for k, v in _L0_tok_all.items() if k in ('W', 'b', 'g1', 'b1', 'g2', 'b2')}
    del _L0_tok_all

    def _L0_attn_setup():
        import jax, jax.numpy as jnp
        import numpy as np
        EPS = 1e-06
        N_REP = 4

        def _qk_norm(a):
            a32 = a.astype(jnp.float32)
            var = jnp.mean(jnp.square(a32), axis=-1, keepdims=True)
            return (a32 * jax.lax.rsqrt(var + EPS)).astype(a.dtype)
        key = jax.random.key(seed)
        ks = jax.random.split(key, 5)
        B, Tq, C, H, D, Hkv = (2, 512, 512, 16, 128, 4)
        s = 0.02
        return {'x_q': jax.random.normal(ks[0], (B, Tq, C), dtype=jnp.float32), 'Wq': jax.random.normal(ks[1], (C, H, D), dtype=jnp.float32) * s, 'Wk': jax.random.normal(ks[2], (C, Hkv, D), dtype=jnp.float32) * s, 'Wv': jax.random.normal(ks[3], (C, Hkv, D), dtype=jnp.float32) * s, 'Wo': jax.random.normal(ks[4], (H * D, C), dtype=jnp.float32) * s}
    _L0_attn_all = _L0_attn_setup()
    _L0_attn_in = {k: v for k, v in _L0_attn_all.items() if k in ('Wq', 'Wk', 'Wv', 'Wo')}
    del _L0_attn_all

    def _L0_ffn_setup():
        import jax, jax.numpy as jnp
        import numpy as np
        BS, SLEN, DIM, HID, E, TOPK = (4, 512, 512, 448, 8, 2)
        key = jax.random.key(seed)
        ks = jax.random.split(key, 9)
        s = 0.02
        return {'x': jax.random.normal(ks[0], (BS, SLEN, DIM), jnp.float32), 'gate_w': jax.random.normal(ks[1], (DIM, E), jnp.float32) * s, 'w1': jax.random.normal(ks[2], (E, DIM, HID), jnp.float32) * s, 'w2': jax.random.normal(ks[3], (E, HID, DIM), jnp.float32) * s, 'w3': jax.random.normal(ks[4], (E, DIM, HID), jnp.float32) * s, 'sw1': jax.random.normal(ks[5], (DIM, HID), jnp.float32) * s, 'sw2': jax.random.normal(ks[6], (HID, DIM), jnp.float32) * s, 'sw3': jax.random.normal(ks[7], (DIM, HID), jnp.float32) * s, 'expert_bias': jnp.zeros((E,), jnp.float32)}
    _L0_ffn_all = _L0_ffn_setup()
    _L0_ffn_in = {k: v for k, v in _L0_ffn_all.items() if k in ('gate_w', 'w1', 'w2', 'w3', 'sw1', 'sw2', 'sw3', 'expert_bias')}
    del _L0_ffn_all
    return {'x': x, 'L0_tok_W': _L0_tok_in['W'], 'L0_tok_b': _L0_tok_in['b'], 'L0_tok_g1': _L0_tok_in['g1'], 'L0_tok_b1': _L0_tok_in['b1'], 'L0_tok_g2': _L0_tok_in['g2'], 'L0_tok_b2': _L0_tok_in['b2'], 'L0_attn_Wq': _L0_attn_in['Wq'], 'L0_attn_Wk': _L0_attn_in['Wk'], 'L0_attn_Wv': _L0_attn_in['Wv'], 'L0_attn_Wo': _L0_attn_in['Wo'], 'L0_ffn_gate_w': _L0_ffn_in['gate_w'], 'L0_ffn_w1': _L0_ffn_in['w1'], 'L0_ffn_w2': _L0_ffn_in['w2'], 'L0_ffn_w3': _L0_ffn_in['w3'], 'L0_ffn_sw1': _L0_ffn_in['sw1'], 'L0_ffn_sw2': _L0_ffn_in['sw2'], 'L0_ffn_sw3': _L0_ffn_in['sw3'], 'L0_ffn_expert_bias': _L0_ffn_in['expert_bias']}

def reference(x, L0_tok_W, L0_tok_b, L0_tok_g1, L0_tok_b1, L0_tok_g2, L0_tok_b2, L0_attn_Wq, L0_attn_Wk, L0_attn_Wv, L0_attn_Wo, L0_ffn_gate_w, L0_ffn_w1, L0_ffn_w2, L0_ffn_w3, L0_ffn_sw1, L0_ffn_sw2, L0_ffn_sw3, L0_ffn_expert_bias):
    import jax
    import jax.numpy as jnp

    def _L0_tok_ref(x, W, b, g1, b1, g2, b2):
        import jax, jax.numpy as jnp
        import numpy as np
        TIN = 16
        FEAT = 64
        IN_DIM = TIN * FEAT
        HDIM = 512
        EPS = 1e-06

        def layer_norm(x, gamma, beta, eps):
            mu = jnp.mean(x, axis=-1, keepdims=True)
            var = jnp.mean(jnp.square(x - mu), axis=-1, keepdims=True)
            return (x - mu) * jax.lax.rsqrt(var + eps) * gamma + beta
        bsz, T, F = x.shape
        n_patch = T // TIN
        x = x[:, :n_patch * TIN, :].reshape(bsz, n_patch, TIN * F)
        x = layer_norm(x, g1, b1, EPS)
        x = jnp.einsum('bpd,dh->bph', x, W) + b
        return layer_norm(x, g2, b2, EPS)

    def _L0_attn_ref(x_q, Wq, Wk, Wv, Wo):
        import jax, jax.numpy as jnp
        import numpy as np
        EPS = 1e-06
        N_REP = 4

        def _qk_norm(a):
            a32 = a.astype(jnp.float32)
            var = jnp.mean(jnp.square(a32), axis=-1, keepdims=True)
            return (a32 * jax.lax.rsqrt(var + EPS)).astype(a.dtype)
        B, Tq, C = x_q.shape
        D = Wq.shape[-1]
        q = jnp.einsum('btc,chd->bthd', x_q, Wq)
        k = jnp.einsum('btc,chd->bthd', x_q, Wk)
        v = jnp.einsum('btc,chd->bthd', x_q, Wv)
        q = _qk_norm(q)
        k = _qk_norm(k)
        k = jnp.repeat(k, N_REP, axis=2)
        v = jnp.repeat(v, N_REP, axis=2)
        scale = jnp.asarray(1.0 / np.sqrt(D), dtype=q.dtype)
        logits = jnp.einsum('bqhd,bkhd->bhqk', q, k) * scale
        attn = jax.nn.softmax(logits, axis=-1)
        out = jnp.einsum('bhqk,bkhd->bqhd', attn, v)
        out = out.reshape(B, Tq, -1)
        return out @ Wo

    def _L0_ffn_ref(x, gate_w, w1, w2, w3, sw1, sw2, sw3, expert_bias):
        import jax, jax.numpy as jnp
        import numpy as np
        BS, SLEN, DIM, HID, E, TOPK = (4, 512, 512, 448, 8, 2)
        bs, slen, dim = x.shape
        T = bs * slen
        xf = x.reshape(T, dim)
        scores = jax.nn.softmax((xf @ gate_w).astype(jnp.float32), axis=-1)
        _, sel = jax.lax.top_k(scores + expert_bias[None, :], TOPK)
        top_scores = jnp.take_along_axis(scores, sel, axis=1)
        flat_sel = sel.reshape(-1)
        counts = jnp.bincount(flat_sel, length=E).astype(jnp.int32)
        order = jnp.argsort(flat_sel, stable=True)
        top_scores_sorted = top_scores.reshape(-1)[order]
        token_idx = order // TOPK
        routed_in = xf[token_idx] * top_scores_sorted[:, None]
        h = jax.nn.silu(jax.lax.ragged_dot(routed_in, w1, counts)) * jax.lax.ragged_dot(routed_in, w3, counts)
        routed_out = jax.lax.ragged_dot(h, w2, counts)
        out = jax.nn.silu(xf @ sw1) * (xf @ sw3) @ sw2
        out = out.at[token_idx].add(routed_out)
        return out.reshape(bs, slen, dim)
    h = _L0_tok_ref(x, L0_tok_W, L0_tok_b, L0_tok_g1, L0_tok_b1, L0_tok_g2, L0_tok_b2)
    h = h + _L0_attn_ref(_layernorm(h, axis=-1), L0_attn_Wq, L0_attn_Wk, L0_attn_Wv, L0_attn_Wo)
    h = h + _L0_ffn_ref(_layernorm(h, axis=-1), L0_ffn_gate_w, L0_ffn_w1, L0_ffn_w2, L0_ffn_w3, L0_ffn_sw1, L0_ffn_sw2, L0_ffn_sw3, L0_ffn_expert_bias)
    return h

_drawn_inputs = setup_inputs


def setup_inputs(seed=0):
    import zlib

    import numpy as np

    out = dict(_drawn_inputs(seed))
    spreads = {'L0_tok_b': (0.0, 0.1),
     'L0_tok_g1': (1.0, 0.2),
     'L0_tok_b1': (0.0, 0.1),
     'L0_tok_g2': (1.0, 0.2),
     'L0_tok_b2': (0.0, 0.1),
     'L0_ffn_expert_bias': (0.0, 0.8)}
    factors = {'L0_ffn_gate_w': 8.0,
     'L0_ffn_w1': 8.0,
     'L0_ffn_w2': 8.0,
     'L0_ffn_w3': 8.0,
     'L0_ffn_sw1': 8.0,
     'L0_ffn_sw2': 8.0,
     'L0_ffn_sw3': 8.0}
    for name, (base, spread) in spreads.items():
        noise = np.random.default_rng([zlib.crc32(name.encode()), seed]).standard_normal(out[name].shape)
        drawn = base * np.exp(spread * noise) if base else spread * noise
        out[name] = jnp.asarray(drawn.astype(out[name].dtype))
    for name, factor in factors.items():
        out[name] = (out[name] * factor).astype(out[name].dtype)
    return out
```

```python
from contextlib import ExitStack
import numpy as np
import concourse.bass as bass
from concourse import mybir

ALU = mybir.AluOpType
ACT = mybir.ActivationFunctionType
AX = mybir.AxisListType
F32 = mybir.dt.float32
F32R = mybir.dt.float32r
U32 = mybir.dt.uint32

P = 128
BATCH, FRAMES, FEAT, TIN = 128, 375, 64, 16
NPATCH = FRAMES // TIN
IN_DIM = TIN * FEAT
DIM = 512
TOK = BATCH * NPATCH
WSEQ = 16
WT = WSEQ * NPATCH
WIN = TOK // WT
ROWS = [128, 128, WT - 256]
TPW = len(ROWS)
KC = DIM // P
XC = IN_DIM // P
EPS_TOK = 1e-6
EPS_LN = 1e-5


def pieces(j):
    out, n, end = [], 128 * j, 128 * j + ROWS[j]
    while n < end:
        s, p = divmod(n, NPATCH)
        whole = (end - n) // NPATCH if p == 0 else 0
        k = whole * NPATCH if whole else min(NPATCH - p, end - n)
        out.append((n - 128 * j, s, p, whole, k))
        n += k
    return out


TPU = 2 * TPW
UNITS = WIN // 2


def rows_of(i):
    return ROWS[i % TPW]


def run_steps(eng, turns, per, lag, step):
    for i in range(per):
        step(0, i)
    with eng.Fori(1, turns) as u:
        for i in range(per):
            step(u, i)
    for i in range(lag):
        step(turns + i // per, i % per)


def earlier(u, i, n, turns, per):
    d, i = divmod(i - n, per)
    if isinstance(u, int) and not 0 <= u + d < turns:
        return None
    return u + d, i


def tile_steps(eng, lag, step):
    run_steps(eng, UNITS, TPU, lag, step)


def back(u, i, n):
    return earlier(u, i, n, UNITS, TPU)


def number(at):
    return at[0] * TPU + at[1]


def first(at, n):
    return isinstance(at[0], int) and number(at) < n


def tokenise(nc, x, W, b, g1, b1, g2, b2, ident, h_sb, normed_t):
    with ExitStack() as ctx:
        def sb(name, shape, dt=F32):
            return ctx.enter_context(nc.sbuf_tensor(name, shape, dt))

        def sem(name):
            return ctx.enter_context(nc.semaphore(name))

        w_raw = sb("w_raw", [P, XC, DIM])
        w_hi = sb("w_hi", [P, XC, DIM], F32R)
        w_lo = sb("w_lo", [P, XC, DIM], F32R)
        g1_col = sb("g1_col", [P, XC])
        b1_col = sb("b1_col", [P, XC])
        zeros = sb("zeros", [P, P])
        b1_wide = sb("b1_wide", [P, XC, P])
        g2_row = sb("g2_row", [P, DIM])
        b2_row = sb("b2_row", [P, DIM])
        bias_row = sb("bias_row", [P, DIM])
        turnstile = sb("turnstile", [P, 1])
        minus_half = sb("minus_half", [P, 1])
        xin = sb("xin", [P, 3, IN_DIM])
        xt_hi = sb("xt_hi", [P, 2, XC, P], F32R)
        xt_lo = sb("xt_lo", [P, 2, XC, P], F32R)
        proj = sb("proj", [P, 2, DIM])
        norm3 = sb("norm3", [P, 2, DIM])
        ht = sb("ht", [P, 3, 2, KC, P], F32R)
        st = [sb(f"st{i}", [P, 3, 2, 6]) for i in range(3)]
        mv = [sb(f"mv{i}", [P, 3, 2]) for i in range(3)]
        ve = [sb(f"ve{i}", [P, 3]) for i in range(3)]
        rstd = [sb(f"rstd{i}", [P, 3]) for i in range(3)]
        xt_ps = ctx.enter_context(nc.psum_tensor("xt_ps", [P, 4, KC, P], F32))
        acc = ctx.enter_context(nc.psum_tensor("acc", [P, 2, DIM], F32))
        ht_ps = ctx.enter_context(nc.psum_tensor("ht_ps", [P, 2, KC, P], F32))

        consts_in = sem("consts_in")
        w_in = sem("w_in")
        x_in = [sem(f"x_in{j}") for j in range(TPW)]
        b1_spread = sem("b1_spread")
        w_scaled = sem("w_scaled")
        w_hi_ready = sem("w_hi_ready")
        w_ready = sem("w_ready")
        bias_mm = sem("bias_mm")
        bias_ready = sem("bias_ready")
        consts_set = sem("consts_set")
        stats_done = [sem(f"stats_done{i}") for i in range(3)]
        mv_done = [sem(f"mv_done{i}") for i in range(3)]
        var_ready = [sem(f"var_ready{i}") for i in range(3)]
        rstd_ready = [sem(f"rstd_ready{i}") for i in range(3)]
        xhat_ready = sem("xhat_ready")
        xt_done = sem("xt_done")
        xt_hi_done = sem("xt_hi_done")
        xt_lo_done = sem("xt_lo_done")
        acc_done = sem("acc_done")
        proj_ready = sem("proj_ready")
        centred = sem("centred")
        h_ready = sem("h_ready")
        norm3_ready = sem("norm3_ready")
        ht_done = sem("ht_done")
        ht_hi_done = sem("ht_hi_done")
        ht_lo_done = sem("ht_lo_done")
        ht_stored = [sem(f"ht_stored{k}") for k in range(3)]

        flat = x.rearrange("b t f -> b (t f)")
        XHAT, PROJ, LN2, LN3, HT = 1, 3, 4, 5, 6
        block = ctx.enter_context(nc.Block())

        @block.sync
        def _(sp):
            sp.dma_start(w_raw[:], W.rearrange("(c p) n -> p c n", p=P)).then_inc(w_in, 16)
            with nc.allow_non_contiguous_dma("columns of two short vectors"):
                sp.dma_start(g1_col[:], g1.rearrange("(c p) -> p c", p=P)).then_inc(consts_in, 16)
                sp.dma_start(b1_col[:], b1.rearrange("(c p) -> p c", p=P)).then_inc(consts_in, 16)
            for row, vector in ((g2_row, g2), (b2_row, b2), (bias_row, b)):
                sp.dma_start(row[:], vector.partition_broadcast(P)).then_inc(consts_in, 16)

            def load(at):
                (u, i), j = at, at[1] % TPW
                if not first(at, 3):
                    sp.wait_ge(xt_done, 2 * (number(at) - 2))
                seq = u * 2 * WSEQ + i // TPW * WSEQ
                for row, s, p, whole, k in pieces(j):
                    src = flat[bass.ds(seq + s, whole or 1), p * IN_DIM:(p + (NPATCH if whole else k)) * IN_DIM]
                    sp.dma_start(xin[row:row + k, i % 3, :], src.rearrange("s (p d) -> s p d", d=IN_DIM))\
                        .then_inc(x_in[j], 16)

            def step(u, i):
                if at := back(u, i, 0):
                    load(at)
            tile_steps(sp, 0, step)
            for stored in ht_stored:
                sp.wait_ge(stored, 16 * UNITS * TPU // 3)

        @block.gpsimd
        def _(pool):
            pool.memset(minus_half[:], -0.5).then_inc(consts_set, 1)
            pool.memset(zeros[:], 0.0).then_inc(consts_set, 1)
            pool.wait_ge(consts_set, 2)
            pool.wait_ge(consts_in, 16 * 5)
            for c in range(XC):
                pool.tensor_scalar(b1_wide[:, c, :], zeros[:], b1_col[:, c:c + 1], None, ALU.add)\
                    .then_inc(b1_spread, 1)

            def power(n, at):
                i, R = at[1] % 3, rows_of(at[1])
                pool.wait_ge(var_ready[n], number(at) + 1)
                pool.tensor_tensor(rstd[n][0:R, i:i + 1], ve[n][0:R, i:i + 1], minus_half[0:R, :],
                                   ALU.pow).then_inc(rstd_ready[n], 1)

            def store(at):
                (u, i), j = at, at[1] % TPW
                pool.wait_ge(ht_lo_done, number(at) + 1)
                pool.dma_start(normed_t[u * 2 + i // TPW, :, :, :, 128 * j:128 * j + ROWS[j]],
                             ht[:, i % 3, :, :, 0:ROWS[j]].bitcast(F32)).then_inc(ht_stored[i % 3], 16)

            def step(u, i):
                for n, lag in enumerate((0, PROJ, LN2)):
                    if at := back(u, i, lag):
                        power(n, at)
                if at := back(u, i, HT):
                    store(at)
            tile_steps(pool, HT, step)

        @block.scalar
        def _(act):
            act.wait_ge(w_scaled, XC)
            act.copy(w_hi[:], w_raw[:]).then_inc(w_hi_ready, 1)

            def patches_high(at):
                i, R = at[1], rows_of(at[1])
                if not first(at, 2):
                    act.wait_ge(acc_done, number(at) - 1)
                for half in range(2):
                    act.wait_ge(xt_done, 2 * number(at) + half + 1)
                    act.copy(xt_hi[:, i % 2, half * KC:half * KC + KC, 0:R],
                             xt_ps[:, 2 * (i % 2) + half, :, 0:R]).then_inc(xt_hi_done, 1)

            def h_high(at):
                i, R = at[1], rows_of(at[1])
                act.wait_ge(ht_done, number(at) + 1)
                if not first(at, 3):
                    act.wait_ge(ht_stored[i % 3], 16 * (at[0] * 2 + i // 3))
                act.copy(ht[:, i % 3, 0, :, 0:R], ht_ps[:, i % 2, :, 0:R]).then_inc(ht_hi_done, 1)

            def step(u, i):
                if at := back(u, i, XHAT):
                    patches_high(at)
                if at := back(u, i, LN3):
                    h_high(at)
            tile_steps(act, LN3, step)

        @block.tensor
        def _(pe):
            pe.wait_ge(b1_spread, XC)
            pe.wait_ge(w_in, 16)
            for c in range(XC):
                mm = pe.matmul(acc[:, 0, :], b1_wide[:, c, :], w_raw[:, c, :], start=c == 0, stop=c == XC - 1)
            mm.then_inc(bias_mm, 1)

            def patches_t(at):
                i, R = at[1], rows_of(at[1])
                pe.wait_ge(xhat_ready, number(at) + 1)
                for half in range(2):
                    if not first(at, 2):
                        pe.wait_ge(xt_lo_done, 2 * (number(at) - 2) + half + 1)
                    for c in range(KC):
                        k = half * KC + c
                        mm = pe.transpose(xt_ps[:, 2 * (i % 2) + half, c, 0:R],
                                          xin[0:R, i % 3, k * P:k * P + P], ident[0:R, 0:R])
                    mm.then_inc(xt_done, 1)

            def project(at):
                i, R = at[1], rows_of(at[1])
                pe.wait_ge(xt_lo_done, 2 * number(at) + 2)
                if first(at, 1):
                    pe.wait_ge(w_ready, 1)
                    pe.wait_ge(bias_ready, 1)
                if not first(at, 2):
                    pe.wait_ge(proj_ready, number(at) - 1)
                for c in range(XC):
                    for lhs, rhs in ((xt_hi, w_hi), (xt_lo, w_hi), (xt_hi, w_lo)):
                        mm = pe.matmul(acc[0:R, i % 2, :], lhs[:, i % 2, c, 0:R], rhs[:, c, :],
                                       start=c == 0 and lhs is xt_hi and rhs is w_hi,
                                       stop=c == XC - 1 and rhs is w_lo)
                mm.then_inc(acc_done, 1)

            def h_t(at):
                i, R = at[1], rows_of(at[1])
                pe.wait_ge(norm3_ready, number(at) + 1)
                if not first(at, 2):
                    pe.wait_ge(ht_lo_done, number(at) - 1)
                for c in range(KC):
                    mm = pe.transpose(ht_ps[:, i % 2, c, 0:R], norm3[0:R, i % 2, c * P:c * P + P],
                                      ident[0:R, 0:R])
                mm.then_inc(ht_done, 1)

            def step(u, i):
                if at := back(u, i, XHAT):
                    patches_t(at)
                if at := back(u, i, XHAT + 1):
                    project(at)
                if at := back(u, i, LN3):
                    h_t(at)
            tile_steps(pe, LN3, step)

        @block.vector
        def _(dve):
            dve.wait_ge(consts_in, 16 * 5)
            dve.wait_ge(w_in, 16)
            dve.wait_ge(bias_mm, 1)
            dve.tensor_tensor(bias_row[:], acc[:, 0, :], bias_row[:], ALU.add).then_inc(bias_ready, 1)
            for c in range(XC):
                dve.tensor_scalar(w_raw[:, c, :], w_raw[:, c, :], g1_col[:, c:c + 1], None, ALU.mult)\
                    .then_inc(w_scaled, 1)
            dve.wait_ge(w_scaled, XC)
            dve.wait_ge(w_hi_ready, 1)
            dve.tensor_tensor(w_lo[:], w_raw[:], w_hi[:].bitcast(F32), ALU.subtract).then_inc(w_ready, 1)
            dve.wait_ge(bias_ready, 1)

            def statistics(n, at, source, eps):
                i, R = at[1] % 3, rows_of(at[1])
                halves = source.shape[-1] // DIM
                dve.memset(turnstile[:], 0.0)
                for k in range(halves):
                    dve.bn_stats(st[n][0:R, i, k, :], source[:, k * DIM:k * DIM + DIM]).then_inc(stats_done[n], 1)
                dve.wait_ge(stats_done[n], halves * (number(at) + 1))
                dve.memset(turnstile[:], 0.0)
                dve.bn_aggr(mv[n][0:R, i, :], st[n][0:R, i, 0:halves, :].rearrange("p a b -> p (a b)"))\
                    .then_inc(mv_done[n], 1)
                dve.wait_ge(mv_done[n], number(at) + 1)
                dve.tensor_scalar(ve[n][0:R, i:i + 1], mv[n][0:R, i, 1:2], eps, None, ALU.add)\
                    .then_inc(var_ready[n], 1)

            def step(u, i):
                if at := back(u, i, XHAT):
                    k, R = at[1] % 3, rows_of(at[1])
                    dve.wait_ge(rstd_ready[0], number(at) + 1)
                    dve.tensor_scalar(xin[0:R, k, :], xin[0:R, k, :], mv[0][0:R, k, 0:1], rstd[0][0:R, k:k + 1],
                                      ALU.subtract, ALU.mult).then_inc(xhat_ready, 1)
                if at := back(u, i, XHAT + 1):
                    k, R = at[1] % 2, rows_of(at[1])
                    for half in range(2):
                        dve.wait_ge(xt_hi_done, 2 * number(at) + half + 1)
                        chunks = slice(half * KC, half * KC + KC)
                        dve.tensor_tensor(xt_lo[:, k, chunks, 0:R], xt_ps[:, 2 * k + half, :, 0:R],
                                          xt_hi[:, k, chunks, 0:R].bitcast(F32), ALU.subtract)\
                            .then_inc(xt_lo_done, 1)
                if at := back(u, i, PROJ):
                    k, R = at[1] % 2, rows_of(at[1])
                    dve.wait_ge(acc_done, number(at) + 1)
                    dve.tensor_tensor(proj[0:R, k, :], acc[0:R, k, :], bias_row[0:R, :], ALU.add)\
                        .then_inc(proj_ready, 1)
                    dve.wait_ge(proj_ready, number(at) + 1)
                    statistics(1, at, proj[0:R, k, :], EPS_TOK)
                if at := back(u, i, 0):
                    j, R = at[1] % TPW, rows_of(at[1])
                    whole_windows = at[0] * 2 + at[1] // TPW
                    dve.wait_ge(x_in[j], 16 * len(pieces(j)) * (whole_windows + 1))
                    statistics(0, at, xin[0:R, at[1] % 3, :], EPS_TOK)
                if at := back(u, i, LN2):
                    k, s, R = at[1] % 2, at[1] % 3, rows_of(at[1])
                    h = h_sb[0:R, number(at), :]
                    dve.wait_ge(rstd_ready[1], number(at) + 1)
                    dve.scalar_tensor_tensor(proj[0:R, k, :], proj[0:R, k, :], mv[1][0:R, s, 0:1], g2_row[0:R, :],
                                             ALU.subtract, ALU.mult).then_inc(centred, 1)
                    dve.wait_ge(centred, number(at) + 1)
                    dve.scalar_tensor_tensor(h, proj[0:R, k, :], rstd[1][0:R, s:s + 1], b2_row[0:R, :],
                                             ALU.mult, ALU.add).then_inc(h_ready, 1)
                    dve.wait_ge(h_ready, number(at) + 1)
                    statistics(2, at, h, EPS_LN)
                if at := back(u, i, LN3):
                    k, s, R = at[1] % 2, at[1] % 3, rows_of(at[1])
                    dve.wait_ge(rstd_ready[2], number(at) + 1)
                    dve.tensor_scalar(norm3[0:R, k, :], h_sb[0:R, number(at), :], mv[2][0:R, s, 0:1],
                                      rstd[2][0:R, s:s + 1], ALU.subtract, ALU.mult).then_inc(norm3_ready, 1)
                if at := back(u, i, HT):
                    k, R = at[1], rows_of(at[1])
                    dve.wait_ge(ht_hi_done, number(at) + 1)
                    dve.tensor_tensor(ht[:, k % 3, 1, :, 0:R], ht_ps[:, k % 2, :, 0:R],
                                      ht[:, k % 3, 0, :, 0:R].bitcast(F32), ALU.subtract).then_inc(ht_lo_done, 1)
            tile_steps(dve, HT, step)


HEADS, KV_HEADS, HD = 16, 4, 128
REP = HEADS // KV_HEADS
GSEQ = 4
GT = GSEQ * NPATCH
GPW = WSEQ // GSEQ
QW = REP * HD
WCOLS = QW + 2 * HD + DIM
WPART = WCOLS // 2
EPS_QK = 1e-6
MASKED = -16384.0
BF16 = mybir.dt.bfloat16
TURNS = KV_HEADS * WIN // 2
TURNS_HEAD = WIN // 2


def attend(nc, Wq, Wk, Wv, Wo, ident, h_sb, normed_t):
    with ExitStack() as ctx:
        def sb(name, shape, dt=F32):
            return ctx.enter_context(nc.sbuf_tensor(name, shape, dt))

        def sem(name):
            return ctx.enter_context(nc.semaphore(name))

        w_raw = sb("aw_raw", [P, WPART])
        w_hi = sb("aw_hi", [P, 2, KC, WCOLS], F32R)
        w_lo = sb("aw_lo", [P, 2, KC, WCOLS], F32R)
        hn = sb("hn", [P, 2, 2, KC, WT], F32R)
        squares = sb("squares", [P, QW])
        normed = sb("normed", [P, 2, QW])
        ssq = sb("ssq", [P, 4, REP])
        var = sb("var", [P, 4, REP])
        rs = sb("rs", [P, 4, REP])
        minus_half = sb("aminus_half", [P, REP])
        q_t = sb("q_t", [P, 2, REP, WT], F32R)
        k_t = sb("k_t", [P, 2, WT], F32R)
        v = sb("v", [GT, 2, GPW, HD], F32R)
        e = sb("e", [GT, 2, REP * GT])
        p_hi = sb("p_hi", [GT, 2, REP * GT], F32R)
        p_lo = sb("p_lo", [GT, 2, REP * GT], F32R)
        rden = sb("rden", [P, REP * GT])
        o_norm = sb("o_norm", [P, REP * GT])
        o_t = sb("o_t", [P, 2, REP, WT], F32R)
        ident_b = sb("ident_b", [GT, GT], BF16)
        mask = sb("mask", [GT, REP, GT], BF16)
        ones = sb("ones", [GT, 2], F32R)
        rden_col = sb("rden_col", [GT, REP])
        kv_ps = ctx.enter_context(nc.psum_tensor("kv_ps", [P, GPW, 2 * HD], F32))
        proj_ps = ctx.enter_context(nc.psum_tensor("proj_ps", [P, 2, DIM], F32))
        turn_ps = ctx.enter_context(nc.psum_tensor("turn_ps", [P, 2, DIM], F32))
        o_ps = ctx.enter_context(nc.psum_tensor("o_ps", [P, DIM], F32))
        den_ps = ctx.enter_context(nc.psum_tensor("den_ps", [P, DIM], F32))

        consts = sem("aconsts")
        mask_steps = sem("mask_steps")
        w_in = sem("aw_in")
        w_hi_done = sem("aw_hi_done")
        w_lo_done = sem("aw_lo_done")
        hn_in = [sem(f"hn_in{i}") for i in range(2)]
        raw_done = sem("raw_done")
        squared = sem("squared")
        summed = sem("summed")
        var_ready = sem("avar_ready")
        rs_ready = sem("rs_ready")
        normalised = sem("normalised")
        turned = sem("turned")
        turned_hi = sem("turned_hi")
        turned_lo = sem("turned_lo")
        v_hi_done = sem("v_hi_done")
        v_lo_done = sem("v_lo_done")
        scores_done = sem("scores_done")
        exp_done = sem("exp_done")
        p_hi_done = sem("p_hi_done")
        p_lo_done = sem("p_lo_done")
        pv_done = sem("pv_done")
        den_done = sem("den_done")
        rden_ready = sem("rden_ready")
        rden_spread = sem("rden_spread")
        rden_taken = sem("rden_taken")
        o_norm_ready = sem("o_norm_ready")
        o_hi_done = sem("o_hi_done")
        o_lo_done = sem("o_lo_done")
        out_done = sem("out_done")
        h_added = sem("h_added")

        K = GPW - 1

        def count(at):
            return at[0] * 2 + at[1]

        def first_step(at, n=1):
            return isinstance(at[0], int) and count(at) < n

        def steps(eng, step):
            def both(u, i):
                step(earlier(u, i, 0, TURNS, 2), earlier(u, i, 1, TURNS, 2))
            run_steps(eng, TURNS, 2, 1, both)

        def slot(at):
            return at[0] // TURNS_HEAD % 2

        def part_source(head, c, half):
            rows = bass.ds(c * P, P)
            if half == 0:
                return [(0, Wq[rows, bass.ds(head * REP, REP), :].rearrange("p h d -> p (h d)"), QW),
                        (QW, Wk[rows, bass.ds(head, 1), :].rearrange("p h d -> p (h d)"), HD)]
            return [(0, Wv[rows, bass.ds(head, 1), :].rearrange("p h d -> p (h d)"), HD),
                    (HD, Wo[bass.ds((head * REP + c) * P, P), :], DIM)]

        def next_part(at):
            u, i = at
            return (u // TURNS_HEAD + 1) % 2, u % TURNS_HEAD, slice(i * WPART, i * WPART + WPART)

        block = ctx.enter_context(nc.Block())

        @block.sync
        def _(sp):
            def load_hn(at):
                u, i = at
                if not first_step(at, 2):
                    sp.wait_ge(raw_done, 4 * (count(at) - 1))
                sp.dma_start(hn[:, i, :, :, :].bitcast(F32), normed_t[bass.ds((u % TURNS_HEAD) * 2 + i, 1)]
                             .rearrange("a p s c t -> (a p) s c t")).then_inc(hn_in[i], 16)

            def load_part(head, c, half):
                for col, src, n in part_source(head, c, half):
                    sp.dma_start(w_raw[:, col:col + n], src).then_inc(w_in, 16)

            load_hn((0, 0))
            for n in range(2 * KC):
                if n:
                    sp.wait_ge(w_lo_done, n)
                load_part(0, n // 2, n % 2)

            def step(front, rear):
                if front:
                    if not first_step(front):
                        load_hn(front)
                    u, i = front
                    sp.wait_ge(w_lo_done, 2 * KC + count(front))
                    load_part((u // TURNS_HEAD + 1) % KV_HEADS, u % TURNS_HEAD, i)
            steps(sp, step)

        @block.gpsimd
        def _(pool):
            pool.memset(minus_half[:], -0.5).then_inc(consts, 1)
            pool.memset(ones[:].bitcast(F32), 1.0).then_inc(consts, 1)
            pool.tensor_copy(ident_b[:], ident[0:GT, 0:GT]).then_inc(consts, 1)
            pool.memset(mask[:], 0.0).then_inc(mask_steps, 1)
            for j in range(GSEQ):
                part = mask[:, :, j * NPATCH:j * NPATCH + NPATCH]
                for side, (base, sign) in enumerate(((-j * NPATCH, 1), (j * NPATCH + NPATCH - 1, -1))):
                    pool.wait_ge(mask_steps, 1 + 2 * j + side)
                    pool.affine_select(out=part, in_=part, compare_op=ALU.is_ge, fill=MASKED, base=base,
                                       pattern=[[0, REP], [0, NPATCH]], channel_multiplier=sign)\
                        .then_inc(mask_steps, 1)
            pool.wait_ge(consts, 3)

            def step(front, rear):
                if front:
                    for s in range(4):
                        R = GT if s == K else ROWS[s]
                        pool.wait_ge(var_ready, 4 * count(front) + s + 1)
                        pool.tensor_tensor(rs[0:R, s, :], var[0:R, s, :], minus_half[0:R, :], ALU.pow)\
                            .then_inc(rs_ready, 1)
            steps(pool, step)

        @block.scalar
        def _(act):
            for n in range(2 * KC):
                act.wait_ge(w_in, 32 * (n + 1))
                act.copy(w_hi[:, 0, n // 2, n % 2 * WPART:n % 2 * WPART + WPART], w_raw[:]).then_inc(w_hi_done, 1)

            def step(front, rear):
                f, r = front and count(front), rear and count(rear)

                def exponent(g):
                    act.wait_ge(scores_done, 4 * r + g + 1)
                    if g >= 2 or not first_step(rear):
                        act.wait_ge(p_lo_done, 4 * r + g - 1)
                    act.activation(e[:, g % 2, :], turn_ps[0:GT, g % 2, 0:REP * GT], ACT.Exp,
                                   scale=float(HD) ** -0.5).then_inc(exp_done, 1)
                    if g >= 2 or not first_step(rear):
                        act.wait_ge(pv_done, 4 * r + g - 1)
                    act.wait_ge(exp_done, 4 * r + g + 1)
                    act.copy(p_hi[:, g % 2, :], e[:, g % 2, :]).then_inc(p_hi_done, 1)

                def square(s):
                    act.wait_ge(raw_done, 4 * f + s + 1)
                    if s or not first_step(front):
                        act.wait_ge(summed, 4 * f + s)
                    if s == K:
                        act.activation(squares[0:GT, :].rearrange("p (g d) -> p g d", g=GPW), kv_ps[0:GT, :, 0:HD],
                                       ACT.Square).then_inc(squared, 1)
                    else:
                        act.activation(squares[0:ROWS[s], :], proj_ps[0:ROWS[s], s % 2, :], ACT.Square)\
                            .then_inc(squared, 1)

                def values_high():
                    if rear:
                        act.wait_ge(pv_done, 4 * r + 4)
                    act.copy(v[:, 0], kv_ps[0:GT, :, HD:2 * HD]).then_inc(v_hi_done, 1)

                def take_reciprocals(g):
                    act.wait_ge(rden_spread, 4 * r + g + 1)
                    if g or not first_step(rear):
                        act.wait_ge(o_norm_ready, 4 * r + g)
                    act.copy(rden[:], den_ps[:, 0:REP * GT]).then_inc(rden_taken, 1)

                def out_high(g):
                    act.wait_ge(o_norm_ready, 4 * r + g + 1)
                    if g == 0 and not first_step(rear):
                        act.wait_ge(out_done, TPW * r)
                    act.copy(o_t[:, 0, :, g * GT:g * GT + GT], o_norm[:].rearrange("p (h t) -> p h t", h=REP))\
                        .then_inc(o_hi_done, 1)

                def turned_high(s):
                    act.wait_ge(turned, 4 * f + s + 1)
                    if rear:
                        act.wait_ge(scores_done, 4 * r + 4)
                    if s == K:
                        act.copy(k_t[:, 0, :], turn_ps[:, 1, 0:WT]).then_inc(turned_hi, 1)
                    else:
                        R = ROWS[s]
                        act.copy(q_t[:, 0, :, s * P:s * P + R],
                                 turn_ps[:, s % 2, 0:REP * R].rearrange("p (h t) -> p h t", h=REP))\
                            .then_inc(turned_hi, 1)

                if rear:
                    exponent(0)
                    exponent(1)
                if front:
                    square(0)
                if rear:
                    exponent(2)
                    take_reciprocals(0)
                    out_high(0)
                if front:
                    square(1)
                if rear:
                    exponent(3)
                    take_reciprocals(1)
                    out_high(1)
                if front:
                    square(2)
                if rear:
                    for g in (2, 3):
                        take_reciprocals(g)
                        out_high(g)
                if front:
                    square(K)
                    values_high()
                    for s in range(4):
                        turned_high(s)
                    into, c, cols = next_part(front)
                    act.wait_ge(w_in, 32 * (2 * KC + f + 1))
                    if rear:
                        act.wait_ge(out_done, TPW * (r + 1))
                    act.copy(w_hi[:, bass.ds(into, 1), bass.ds(c, 1), cols].rearrange("p a b n -> p (a b n)"), w_raw[:])\
                        .then_inc(w_hi_done, 1)
            steps(act, step)

        @block.tensor
        def _(pe):
            pe.wait_ge(mask_steps, 1 + 2 * GSEQ)
            pe.wait_ge(consts, 3)

            def products(out, pairs, start, stop):
                for n, (lhs, rhs) in enumerate(pairs):
                    mm = pe.matmul(out, lhs, rhs, start=start and n == 0, stop=stop and n == len(pairs) - 1)
                return mm

            def weights(at, c, cols):
                return [w[:, bass.ds(slot(at), 1), c, cols].rearrange("p a n -> p (a n)") for w in (w_hi, w_lo)]

            def step(front, rear):
                f, r = front and count(front), rear and count(rear)

                def query(j):
                    i, R = front[1], ROWS[j]
                    if j == 0:
                        pe.wait_ge(hn_in[i], 16 * (front[0] + 1))
                        pe.wait_ge(w_lo_done, 2 * KC + (front[0] // TURNS_HEAD) * WIN)
                    if j < 2 and rear and not first_step(rear):
                        pe.wait_ge(h_added, TPW * (r - 1) + 2 + j)
                    if j == 2:
                        pe.wait_ge(normalised, 4 * f + 1)
                    for c in range(KC):
                        hi, lo = (hn[:, i, k, c, j * P:j * P + R] for k in range(2))
                        w, wl = weights(front, c, slice(0, QW))
                        mm = products(proj_ps[0:R, j % 2, :], ((hi, w), (lo, w), (hi, wl)), c == 0, c == KC - 1)
                    mm.then_inc(raw_done, 1)

                def keys_values(groups):
                    i = front[1]
                    if groups[0] == 0 and rear:
                        pe.wait_ge(v_lo_done, f)
                        pe.wait_ge(normalised, 4 * f)
                    for g in groups:
                        for c in range(KC):
                            hi, lo = (hn[:, i, k, c, g * GT:g * GT + GT] for k in range(2))
                            w, wl = weights(front, c, slice(QW, QW + 2 * HD))
                            mm = products(kv_ps[0:GT, g, :], ((hi, w), (lo, w), (hi, wl)), c == 0, c == KC - 1)
                    if groups[-1] == K:
                        mm.then_inc(raw_done, 1)

                def turn(s):
                    R = GT if s == K else ROWS[s]
                    pe.wait_ge(normalised, 4 * f + s + 1)
                    if s < 2 and rear:
                        pe.wait_ge(exp_done, 4 * r + 3 + s)
                    if s >= 2:
                        pe.wait_ge(turned_lo, 4 * f + s - 1)
                    for n in range(REP):
                        mm = pe.transpose(turn_ps[:, s % 2, n * R:n * R + R], normed[0:R, s % 2, n * HD:n * HD + HD],
                                          ident[0:R, 0:R])
                    mm.then_inc(turned, 1)

                def scores(g):
                    if g == 0:
                        pe.wait_ge(turned_lo, 4 * r + 4)
                    if g >= 2:
                        pe.wait_ge(exp_done, 4 * r + g - 1)
                    out = turn_ps[0:GT, g % 2, 0:REP * GT]
                    pe.matmul(out, ident_b[:], mask[:].rearrange("p h t -> p (h t)"), start=True, stop=False)
                    k_hi, k_lo = (k_t[:, k, g * GT:g * GT + GT] for k in range(2))
                    q_hi, q_lo = (q_t[:, k, :, g * GT:g * GT + GT] for k in range(2))
                    products(out, ((k_hi, q_hi), (k_lo, q_hi), (k_hi, q_lo)), False, True).then_inc(scores_done, 1)

                def attended(g):
                    pe.wait_ge(p_lo_done, 4 * r + g + 1)
                    if g == 0:
                        pe.wait_ge(v_lo_done, r + 1)
                    if g or not first_step(rear):
                        pe.wait_ge(o_norm_ready, 4 * r + g)
                    hi, lo = p_hi[:, g % 2, :], p_lo[:, g % 2, :]
                    for n in range(REP):
                        head = slice(n * GT, n * GT + GT)
                        mm = products(den_ps[0:GT, REP * GT + 2 * n:REP * GT + 2 * n + 2],
                                      ((hi[:, head], ones[:]), (lo[:, head], ones[:])), True, True)
                    mm.then_inc(den_done, 1)
                    products(o_ps[:, 0:REP * GT], ((v[:, 0, g, :], hi), (v[:, 0, g, :], lo), (v[:, 1, g, :], hi)),
                             True, True).then_inc(pv_done, 1)

                def spread(g):
                    pe.wait_ge(rden_ready, 4 * r + g + 1)
                    for n in range(REP):
                        mm = pe.transpose(den_ps[:, n * GT:n * GT + GT],
                                          rden_col[:, n:n + 1].broadcast_to([GT, P]), ident[0:GT, 0:GT])
                    mm.then_inc(rden_spread, 1)

                def output(j):
                    R = ROWS[j]
                    if j == 0:
                        pe.wait_ge(o_lo_done, 4 * r + 4)
                    if j < 2 and front:
                        pe.wait_ge(normalised, 4 * f + 2 + j)
                    elif j < 2:
                        pe.wait_ge(h_added, TPW * r)
                    else:
                        pe.wait_ge(h_added, TPW * r + 1)
                    for c in range(REP):
                        hi, lo = (o_t[:, k, c, j * P:j * P + R] for k in range(2))
                        w, wl = weights(rear, c, slice(QW + 2 * HD, WCOLS))
                        mm = products(proj_ps[0:R, (j + 1) % 2, :], ((hi, w), (lo, w), (hi, wl)), c == 0, c == REP - 1)
                    mm.then_inc(out_done, 1)

                if rear:
                    scores(0)
                    scores(1)
                if front:
                    query(0)
                if rear:
                    attended(0)
                    scores(2)
                    spread(0)
                if front:
                    query(1)
                if rear:
                    attended(1)
                    scores(3)
                    spread(1)
                if front:
                    query(2)
                if rear:
                    attended(2)
                if front:
                    keys_values((0,))
                if rear:
                    spread(2)
                if front:
                    turn(0)
                    keys_values((1,))
                if rear:
                    attended(3)
                if front:
                    turn(1)
                    keys_values((2,))
                if rear:
                    spread(3)
                if front:
                    keys_values((3,))
                if rear:
                    output(0)
                if front:
                    turn(2)
                if rear:
                    output(1)
                if front:
                    turn(K)
                if rear:
                    output(2)
            steps(pe, step)

        @block.vector
        def _(dve):
            for n in range(2 * KC):
                cols = slice(n % 2 * WPART, n % 2 * WPART + WPART)
                dve.wait_ge(w_hi_done, n + 1)
                dve.tensor_tensor(w_lo[:, 0, n // 2, cols], w_raw[:], w_hi[:, 0, n // 2, cols].bitcast(F32),
                                  ALU.subtract).then_inc(w_lo_done, 1)

            def step(front, rear):
                f, r = front and count(front), rear and count(rear)

                def probs_low(g):
                    dve.wait_ge(p_hi_done, 4 * r + g + 1)
                    dve.tensor_tensor(p_lo[:, g % 2, :], e[:, g % 2, :], p_hi[:, g % 2, :].bitcast(F32), ALU.subtract)\
                        .then_inc(p_lo_done, 1)

                def sums(s):
                    R = GT if s == K else ROWS[s]
                    dve.wait_ge(squared, 4 * f + s + 1)
                    dve.tensor_reduce(ssq[0:R, s, :], squares[0:R, :].rearrange("p (h d) -> p h d", h=REP), AX.X,
                                      ALU.add).then_inc(summed, 1)
                    dve.wait_ge(summed, 4 * f + s + 1)
                    dve.tensor_scalar(var[0:R, s, :], ssq[0:R, s, :], 1.0 / HD, EPS_QK, ALU.mult, ALU.add)\
                        .then_inc(var_ready, 1)

                def normalise(s):
                    R = GT if s == K else ROWS[s]
                    dve.wait_ge(rs_ready, 4 * f + s + 1)
                    if s >= 2 or not first_step(front):
                        dve.wait_ge(turned, 4 * f + s - 1)
                    raw = kv_ps[0:GT, :, 0:HD] if s == K else \
                        proj_ps[0:R, s % 2, :].rearrange("p (h d) -> p h d", h=REP)
                    dve.tensor_tensor(normed[0:R, s % 2, :].rearrange("p (h d) -> p h d", h=REP), raw,
                                      rs[0:R, s, :].unsqueeze(2).broadcast_to([R, REP, HD]), ALU.mult)\
                        .then_inc(normalised, 1)

                def values_low():
                    dve.wait_ge(v_hi_done, f + 1)
                    dve.tensor_tensor(v[:, 1], kv_ps[0:GT, :, HD:2 * HD], v[:, 0].bitcast(F32), ALU.subtract)\
                        .then_inc(v_lo_done, 1)

                def reciprocals(g):
                    dve.wait_ge(den_done, 4 * r + g + 1)
                    if g or not first_step(rear):
                        dve.wait_ge(rden_spread, 4 * r + g)
                    dve.reciprocal(rden_col[:], den_ps[0:GT, REP * GT:REP * GT + 2 * REP:2]).then_inc(rden_ready, 1)

                def divide(g):
                    dve.wait_ge(pv_done, 4 * r + g + 1)
                    dve.wait_ge(rden_taken, 4 * r + g + 1)
                    if g or not first_step(rear):
                        dve.wait_ge(o_lo_done, 4 * r + g)
                    dve.tensor_tensor(o_norm[:], o_ps[:, 0:REP * GT], rden[:], ALU.mult).then_inc(o_norm_ready, 1)

                def out_low(g):
                    dve.wait_ge(o_hi_done, 4 * r + g + 1)
                    cols = slice(g * GT, g * GT + GT)
                    dve.tensor_tensor(o_t[:, 1, :, cols], o_norm[:].rearrange("p (h t) -> p h t", h=REP),
                                      o_t[:, 0, :, cols].bitcast(F32), ALU.subtract).then_inc(o_lo_done, 1)

                def turned_low(s):
                    dve.wait_ge(turned_hi, 4 * f + s + 1)
                    if s == K:
                        dve.tensor_tensor(k_t[:, 1, :], turn_ps[:, 1, 0:WT], k_t[:, 0, :].bitcast(F32),
                                          ALU.subtract).then_inc(turned_lo, 1)
                    else:
                        R = ROWS[s]
                        cols = slice(s * P, s * P + R)
                        dve.tensor_tensor(q_t[:, 1, :, cols],
                                          turn_ps[:, s % 2, 0:REP * R].rearrange("p (h t) -> p h t", h=REP),
                                          q_t[:, 0, :, cols].bitcast(F32), ALU.subtract).then_inc(turned_lo, 1)

                def add(j):
                    R = ROWS[j]
                    tile = h_sb[0:R, bass.ds((rear[0] % TURNS_HEAD) * TPU + rear[1] * TPW + j, 1), :]\
                        .rearrange("p a n -> p (a n)")
                    dve.wait_ge(out_done, TPW * r + j + 1)
                    dve.tensor_tensor(tile, proj_ps[0:R, (j + 1) % 2, :], tile, ALU.add).then_inc(h_added, 1)

                if rear:
                    probs_low(0)
                    probs_low(1)
                if front:
                    sums(0)
                if rear:
                    reciprocals(0)
                if front:
                    normalise(0)
                if rear:
                    probs_low(2)
                    divide(0)
                    out_low(0)
                if front:
                    sums(1)
                if rear:
                    reciprocals(1)
                if front:
                    normalise(1)
                if rear:
                    probs_low(3)
                    divide(1)
                    out_low(1)
                if front:
                    sums(2)
                if rear:
                    reciprocals(2)
                if rear:
                    divide(2)
                    out_low(2)
                if front:
                    normalise(2)
                if rear:
                    reciprocals(3)
                    divide(3)
                    out_low(3)
                if front:
                    sums(K)
                    values_low()
                    normalise(K)
                    turned_low(0)
                    turned_low(1)
                if rear:
                    add(0)
                if front:
                    turned_low(2)
                if rear:
                    add(1)
                if front:
                    turned_low(K)
                if rear:
                    add(2)
                if front:
                    into, c, cols = next_part(front)
                    dve.wait_ge(w_hi_done, 2 * KC + f + 1)
                    hi, lo = (w[:, bass.ds(into, 1), bass.ds(c, 1), cols].rearrange("p a b n -> p (a b n)")
                              for w in (w_hi, w_lo))
                    dve.tensor_tensor(lo, w_raw[:], hi.bitcast(F32), ALU.subtract).then_inc(w_lo_done, 1)
            steps(dve, step)


EXPERTS, HID = 8, 448
MC = 4
HC = HID // MC
TILES = WIN * TPW
SLOTS = 256
BLOCKS = (2 * TOK + EXPERTS * (SLOTS - 1)) // SLOTS
LIMITS = -(-TOK // SLOTS)


def route_and_share(nc, gate_w, bias, sw1, sw2, sw3, ident, h_sb, normed_t, rows, table, slots, expert_of):
    with ExitStack() as ctx:
        def sb(name, shape, dt=F32):
            return ctx.enter_context(nc.sbuf_tensor(name, shape, dt))

        def sem(name):
            return ctx.enter_context(nc.semaphore(name))

        gate = sb("gate", [P, KC, EXPERTS])
        gate_hi = sb("gate_hi", [P, KC, EXPERTS], F32R)
        gate_lo = sb("gate_lo", [P, KC, EXPERTS], F32R)
        bias_row = sb("fbias_row", [P, EXPERTS])
        minus_half = sb("fminus_half", [P, 1])
        st = sb("fst", [P, 3, 6])
        mv = sb("fmv", [P, 3, 2])
        ve = sb("fve", [P, 3])
        rstd = sb("frstd", [P, 3])
        turnstile = sb("fturnstile", [P, 1])
        norm = sb("norm", [P, 3, DIM])
        ht = sb("fht", [P, 3, 2, KC, P], F32R)
        grid = [P, TILES, EXPERTS]
        logits = sb("logits", grid)
        scores = sb("scores", grid)
        chosen = [sb(f"chosen{k}", grid) for k in range(2)]
        work = sb("work", grid)
        key = sb("key", grid)
        rank = sb("rank", grid)
        falling = sb("falling", [P, EXPERTS])
        valid = sb("valid", [P, TILES])
        best = sb("best", [P, TILES])
        both = sb("both", grid, BF16)
        below = sb("below", [P, P], BF16)
        ones_b = sb("ones_b", [P, P], BF16)
        per_row = sb("per_row", [P, EXPERTS], BF16)
        counts = sb("counts", [P, EXPERTS])
        limits = sb("limits", [P, LIMITS])
        over = sb("over", [P, EXPERTS, LIMITS])
        blocks = sb("blocks", [P, EXPERTS])
        upto = sb("upto", [P, EXPERTS])
        start = sb("start", [P, EXPERTS])
        block_no = sb("block_no", [P, BLOCKS])
        passed = sb("passed", [P, BLOCKS, EXPERTS])
        expert_f = sb("expert_f", [P, BLOCKS])
        payload = sb("payload", [P, TILES, 2, 2], U32)
        slot_f = sb("slot_f", [P, TILES])
        zero_table = sb("zero_table", [P, BLOCKS * SLOTS // P * 2], U32)
        raw = sb("sraw", [P, 2 * KC * HID])
        raw2 = sb("sraw2", [HC, MC, DIM])
        w13_hi = sb("sw13_hi", [P, 2, KC, HID], F32R)
        w13_lo = sb("sw13_lo", [P, 2, KC, HID], F32R)
        w2_hi = sb("sw2_hi", [HC, MC, DIM], F32R)
        w2_lo = sb("sw2_lo", [HC, MC, DIM], F32R)
        xt = sb("sxt", [P, 2, 2, KC, WT], F32R)
        gated = sb("gated", [HC, 2, WT])
        hidden = sb("hidden", [HC, 2, WT])
        hid_hi = sb("hid_hi", [HC, MC, WT], F32R)
        hid_lo = sb("hid_lo", [HC, MC, WT], F32R)

        ht_ps = ctx.enter_context(nc.psum_tensor("fht_ps", [P, 2, KC, P], F32))
        gu_ps = ctx.enter_context(nc.psum_tensor("gu_ps", [P, 2, 2, DIM], F32))
        y_ps = ctx.enter_context(nc.psum_tensor("y_ps", [P, 2, DIM], F32))

        consts_in = sem("fconsts_in")
        consts = sem("fconsts")
        valid_steps = sem("valid_steps")
        w_in = sem("sw_in")
        gate_hi_done = sem("gate_hi_done")
        gate_ready = sem("gate_ready")
        w_hi_done = sem("sw_hi_done")
        w_lo_done = sem("sw_lo_done")
        stats_done = sem("fstats_done")
        mv_done = sem("fmv_done")
        var_ready = sem("fvar_ready")
        rstd_ready = sem("frstd_ready")
        norm_ready = sem("fnorm_ready")
        rows_stored = [sem(f"rows_stored{k}") for k in range(3)]
        ht_done = sem("fht_done")
        ht_hi_done = sem("fht_hi_done")
        ht_lo_done = sem("fht_lo_done")
        ht_stored = [sem(f"fht_stored{k}") for k in range(3)]
        gate_done = sem("gate_done")
        logits_ready = sem("logits_ready")
        table_zeroed = sem("table_zeroed")
        routed = sem("routed")
        centred = sem("fcentred")
        exp_done = sem("fexp_done")
        counts_ready = sem("counts_ready")
        ranks_done = sem("ranks_done")
        counts_done = sem("counts_done")
        slots_ready = sem("slots_ready")
        scattered = sem("scattered")
        xt_in = [sem(f"sxt_in{k}") for k in range(2)]
        gu_done = sem("gu_done")
        silu_done = sem("silu_done")
        hidden_ready = sem("hidden_ready")
        hid_hi_done = sem("hid_hi_done")
        hid_lo_done = sem("hid_lo_done")
        y_done = sem("y_done")
        h_added = sem("fh_added")

        NORM, LOW, LOGITS = 1, 2, 3
        block = ctx.enter_context(nc.Block())

        @block.sync
        def _(sp):
            sp.dma_start(gate[:], gate_w.rearrange("(c p) e -> p c e", p=P)).then_inc(consts_in, 16)
            sp.dma_start(bias_row[:], bias.partition_broadcast(P)).then_inc(consts_in, 16)
            for k, w in enumerate((sw1, sw3)):
                sp.dma_start(raw[:, k * KC * HID:(k + 1) * KC * HID].rearrange("p (c n) -> p c n", c=KC),
                             w.rearrange("(c p) n -> p c n", p=P)).then_inc(w_in, 16)
            sp.dma_start(raw2[:], sw2.rearrange("(c p) n -> p c n", p=HC)).then_inc(w_in, 16)

            def store_rows(at):
                (u, i), j, R = at, at[1] % TPW, rows_of(at[1])
                sp.wait_ge(norm_ready, number(at) + 1)
                sp.dma_start(rows[bass.ds((u * 2 + i // TPW) * WT + P * j, R), :], norm[0:R, i % 3, :])\
                    .then_inc(rows_stored[i % 3], 16)

            def store_turned(at):
                (u, i), j, R = at, at[1] % TPW, rows_of(at[1])
                sp.wait_ge(ht_lo_done, number(at) + 1)
                sp.dma_start(normed_t[u * 2 + i // TPW, :, :, :, P * j:P * j + R],
                             ht[:, i % 3, :, :, 0:R].bitcast(F32)).then_inc(ht_stored[i % 3], 16)

            def step(u, i):
                if at := back(u, i, NORM):
                    store_rows(at)
                if at := back(u, i, LOW):
                    store_turned(at)
            tile_steps(sp, LOW, step)
            for k in range(3):
                sp.wait_ge(rows_stored[k], 16 * TILES // 3)
                sp.wait_ge(ht_stored[k], 16 * TILES // 3)

            def load(u, i):
                if not (isinstance(u, int) and u == 0):
                    sp.wait_ge(gu_done, MC * ((u - 1) * 2 + i + 1))
                sp.dma_start(xt[:, i].bitcast(F32), normed_t[bass.ds(u * 2 + i, 1)]
                             .rearrange("a p s c t -> (a p) s c t")).then_inc(xt_in[i], 16)
            run_steps(sp, WIN // 2, 2, 0, load)

        @block.gpsimd
        def _(pool):
            pool.memset(zero_table[:], 0).then_inc(consts, 1)
            pool.memset(minus_half[:], -0.5).then_inc(consts, 1)
            pool.memset(logits[:], 0.0).then_inc(consts, 1)
            pool.memset(ones_b[:], 1.0).then_inc(consts, 1)
            pool.memset(below[:], 1.0).then_inc(consts, 1)
            pool.memset(valid[:], 1.0).then_inc(consts, 1)
            for n in range(EXPERTS):
                pool.memset(falling[:, n:n + 1], float(EXPERTS - n)).then_inc(consts, 1)
            for n in range(LIMITS):
                pool.memset(limits[:, n:n + 1], float(n * SLOTS)).then_inc(consts, 1)
            for n in range(BLOCKS):
                pool.memset(block_no[:, n:n + 1], float(n)).then_inc(consts, 1)
            made = 6 + EXPERTS + LIMITS + BLOCKS
            pool.wait_ge(consts, made)
            pool.dma_start(table.rearrange("(p n) w -> p (n w)", p=P), zero_table[:]).then_inc(table_zeroed, 16)
            pool.affine_select(out=below[:], in_=below[:], compare_op=ALU.is_gt, fill=0.0, base=0, pattern=[[1, P]],
                               channel_multiplier=-1).then_inc(consts, 1)
            last = valid[:].rearrange("p (w j) -> p w j", j=TPW)[:, :, TPW - 1]
            pool.affine_select(out=last, in_=last, compare_op=ALU.is_gt, fill=0.0, base=ROWS[-1], pattern=[[0, WIN]],
                               channel_multiplier=-1).then_inc(consts, 1)
            for k in range(2):
                for j in range(TPW):
                    pool.iota(payload[:].rearrange("p (w j) k n -> p j k n w", j=TPW)[:, j, k, 0, :],
                              pattern=[[WT, WIN]], base=P * j, channel_multiplier=1).then_inc(consts, 1)

            def step(u, i):
                at = back(u, i, 0)
                if at:
                    k, R = at[1] % 3, rows_of(at[1])
                    pool.wait_ge(var_ready, number(at) + 1)
                    pool.tensor_tensor(rstd[0:R, k:k + 1], ve[0:R, k:k + 1], minus_half[0:R, :], ALU.pow)\
                        .then_inc(rstd_ready, 1)
            tile_steps(pool, 0, step)

            pool.wait_ge(table_zeroed, 16)
            pool.wait_ge(slots_ready, 4)
            for n in range(TILES):
                R = ROWS[n % TPW]
                for k in range(2):
                    pool.indirect_dma_start(out=table[:, :],
                                            out_offset=bass.IndirectOffsetOnAxis(ap=slots[0:R, k, n:n + 1], axis=0),
                                            in_=payload[0:R, n, k, :], in_offset=None).then_inc(scattered, 16)
            pool.wait_ge(scattered, 16 * 2 * TILES)

        @block.scalar
        def _(act):
            act.wait_ge(consts_in, 32)
            act.copy(gate_hi[:], gate[:]).then_inc(gate_hi_done, 1)

            def high(at):
                i, R = at[1], rows_of(at[1])
                act.wait_ge(ht_done, number(at) + 1)
                if not first(at, 3):
                    act.wait_ge(ht_stored[i % 3], 16 * (at[0] * 2 + i // 3))
                    act.wait_ge(gate_done, number(at) - 2)
                act.copy(ht[:, i % 3, 0, :, 0:R], ht_ps[:, i % 2, :, 0:R]).then_inc(ht_hi_done, 1)

            def step(u, i):
                if at := back(u, i, NORM):
                    high(at)
            tile_steps(act, NORM, step)

            act.wait_ge(w_in, 48)
            act.copy(w13_hi[:].rearrange("p k c n -> p (k c n)"), raw[:]).then_inc(w_hi_done, 1)
            act.copy(w2_hi[:], raw2[:]).then_inc(w_hi_done, 1)
            act.wait_ge(centred, 1)
            act.activation(scores[:], work[:], ACT.Exp).then_inc(exp_done, 1)

            def window(u, i):
                n = u * 2 + i
                for m in range(MC):
                    known = isinstance(u, int)
                    act.wait_ge(gu_done, MC * n + m + 1)
                    if not (known and MC * n + m < 2):
                        act.wait_ge(hidden_ready, MC * n + m - 1)
                    act.activation(gated[:, m % 2, :], gu_ps[0:HC, m % 2, 0, 0:WT], ACT.Silu).then_inc(silu_done, 1)
                    act.wait_ge(hidden_ready, MC * n + m + 1)
                    if m == 0 and not (known and n == 0):
                        act.wait_ge(y_done, TPW * n)
                    act.copy(hid_hi[:, m, :], hidden[:, m % 2, :]).then_inc(hid_hi_done, 1)
            run_steps(act, WIN // 2, 2, 0, window)

        @block.tensor
        def _(pe):
            pe.wait_ge(gate_ready, 1)

            def turn(at):
                i, R = at[1], rows_of(at[1])
                pe.wait_ge(norm_ready, number(at) + 1)
                if not first(at, 2):
                    pe.wait_ge(ht_lo_done, number(at) - 1)
                for c in range(KC):
                    mm = pe.transpose(ht_ps[:, i % 2, c, 0:R], norm[0:R, i % 3, c * P:c * P + P], ident[0:R, 0:R])
                mm.then_inc(ht_done, 1)

            def gates(at):
                i, R = at[1], rows_of(at[1])
                pe.wait_ge(ht_lo_done, number(at) + 1)
                if not first(at, 2):
                    pe.wait_ge(logits_ready, number(at) - 1)
                for c in range(KC):
                    hi, lo = (ht[:, i % 3, k, c, 0:R] for k in range(2))
                    for n, (lhs, rhs) in enumerate(((hi, gate_hi), (lo, gate_hi), (hi, gate_lo))):
                        mm = pe.matmul(y_ps[0:R, i % 2, 0:EXPERTS], lhs, rhs[:, c, :], start=c == 0 and n == 0,
                                       stop=c == KC - 1 and n == 2)
                mm.then_inc(gate_done, 1)

            def step(u, i):
                if at := back(u, i, NORM):
                    turn(at)
                if at := back(u, i, LOW):
                    gates(at)
            tile_steps(pe, LOW, step)

            pe.wait_ge(consts, 8 + EXPERTS + LIMITS + BLOCKS)
            pe.wait_ge(counts_ready, 2)
            ranks = gu_ps[:, 0, 0, 0:TILES * EXPERTS].rearrange("p (t e) -> p t e", e=EXPERTS)
            pe.matmul(ranks, below[:], both[:], start=True, stop=False)
            for t in range(TILES - 1):
                after = TILES - 1 - t
                mm = pe.matmul(ranks[:, t + 1:TILES, :], ones_b[:],
                               both[:, t, :].unsqueeze(1).broadcast_to([P, after, EXPERTS]), start=False,
                               stop=t == TILES - 2)
            mm.then_inc(ranks_done, 1)
            pe.matmul(gu_ps[:, 0, 1, 0:EXPERTS], ones_b[:], per_row[:], start=True, stop=True).then_inc(counts_done, 1)

            def window(u, i):
                n, known = u * 2 + i, isinstance(u, int)
                pe.wait_ge(xt_in[i], 16 * (u + 1))
                if known and n == 0:
                    pe.wait_ge(w_lo_done, 2)
                    pe.wait_ge(slots_ready, 4)
                for m in range(MC):
                    if not (known and MC * n + m < 2):
                        pe.wait_ge(hidden_ready, MC * n + m - 1)
                    cols = slice(m * HC, m * HC + HC)
                    for k in range(2):
                        for c in range(KC):
                            x_hi, x_lo = (xt[:, i, s, c, :] for s in range(2))
                            w, wl = w13_hi[:, k, c, cols], w13_lo[:, k, c, cols]
                            for q, (lhs, rhs) in enumerate(((w, x_hi), (wl, x_hi), (w, x_lo))):
                                mm = pe.matmul(gu_ps[0:HC, m % 2, k, 0:WT], lhs, rhs, start=c == 0 and q == 0,
                                               stop=c == KC - 1 and q == 2)
                    mm.then_inc(gu_done, 1)
                for j in range(TPW):
                    R = ROWS[j]
                    slot = (TPW * i + j) % 2
                    if not (known and TPW * n + j < 2):
                        pe.wait_ge(h_added, TPW * n + j - 1)
                    for c in range(MC):
                        if j == 0:
                            pe.wait_ge(hid_lo_done, MC * n + c + 1)
                        tok = slice(j * P, j * P + R)
                        h, hl = hid_hi[:, c, tok], hid_lo[:, c, tok]
                        for q, (lhs, rhs) in enumerate(((h, w2_hi), (hl, w2_hi), (h, w2_lo))):
                            mm = pe.matmul(y_ps[0:R, slot, :], lhs, rhs[:, c, :], start=c == 0 and q == 0,
                                           stop=c == MC - 1 and q == 2)
                    mm.then_inc(y_done, 1)
            run_steps(pe, WIN // 2, 2, 0, window)

        @block.vector
        def _(dve):
            dve.wait_ge(gate_hi_done, 1)
            dve.tensor_tensor(gate_lo[:], gate[:], gate_hi[:].bitcast(F32), ALU.subtract).then_inc(gate_ready, 1)
            dve.wait_ge(consts, 6)

            def step(u, i):
                if at := back(u, i, 0):
                    k, R = at[1] % 3, rows_of(at[1])
                    h = h_sb[0:R, bass.ds(number(at), 1), :].rearrange("p a n -> p (a n)")
                    dve.bn_stats(st[0:R, k, :], h).then_inc(stats_done, 1)
                    dve.wait_ge(stats_done, number(at) + 1)
                    dve.memset(turnstile[:], 0.0)
                    dve.bn_aggr(mv[0:R, k, :], st[0:R, k, :]).then_inc(mv_done, 1)
                    dve.wait_ge(mv_done, number(at) + 1)
                    dve.tensor_scalar(ve[0:R, k:k + 1], mv[0:R, k, 1:2], EPS_LN, None, ALU.add).then_inc(var_ready, 1)
                if at := back(u, i, NORM):
                    k, R = at[1] % 3, rows_of(at[1])
                    h = h_sb[0:R, bass.ds(number(at), 1), :].rearrange("p a n -> p (a n)")
                    if not first(at, 3):
                        dve.wait_ge(rows_stored[k], 16 * (at[0] * 2 + at[1] // 3))
                        dve.wait_ge(ht_done, number(at) - 2)
                    dve.wait_ge(rstd_ready, number(at) + 1)
                    dve.tensor_scalar(norm[0:R, k, :], h, mv[0:R, k, 0:1], rstd[0:R, k:k + 1], ALU.subtract,
                                      ALU.mult).then_inc(norm_ready, 1)
                if at := back(u, i, LOW):
                    k, R = at[1], rows_of(at[1])
                    dve.wait_ge(ht_hi_done, number(at) + 1)
                    dve.tensor_tensor(ht[:, k % 3, 1, :, 0:R], ht_ps[:, k % 2, :, 0:R],
                                      ht[:, k % 3, 0, :, 0:R].bitcast(F32), ALU.subtract).then_inc(ht_lo_done, 1)
                if at := back(u, i, LOGITS):
                    k, R = at[1], rows_of(at[1])
                    dve.wait_ge(gate_done, number(at) + 1)
                    dve.tensor_copy(logits[0:R, bass.ds(number(at), 1), :].rearrange("p a e -> p (a e)"),
                                    y_ps[0:R, k % 2, 0:EXPERTS]).then_inc(logits_ready, 1)
            tile_steps(dve, LOGITS, step)

            dve.wait_ge(logits_ready, TILES)
            dve.wait_ge(consts_in, 32)
            dve.wait_ge(consts, 14 + EXPERTS + LIMITS + BLOCKS)
            done = 0

            def over_experts(a):
                return a.unsqueeze(2).broadcast_to(grid)

            def over_tiles(a):
                return a.unsqueeze(1).broadcast_to(grid)

            def then(instruction):
                nonlocal done
                done += 1
                instruction.then_inc(routed, 1)
                dve.wait_ge(routed, done)

            then(dve.tensor_reduce(best[:], logits[:], AX.X, ALU.max))
            dve.tensor_tensor(work[:], logits[:], over_experts(best[:]), ALU.subtract).then_inc(centred, 1)
            dve.wait_ge(exp_done, 1)
            then(dve.tensor_reduce(best[:], scores[:], AX.X, ALU.add))
            then(dve.reciprocal(slot_f[:], best[:]))
            then(dve.tensor_tensor(scores[:], scores[:], over_experts(slot_f[:]), ALU.mult))
            then(dve.tensor_tensor(work[:], scores[:], over_tiles(bias_row[:]), ALU.add))
            for k in range(2):
                then(dve.tensor_reduce(best[:], work[:], AX.X, ALU.max))
                then(dve.tensor_tensor(key[:], work[:], over_experts(best[:]), ALU.is_equal))
                then(dve.tensor_tensor(key[:], key[:], over_tiles(falling[:]), ALU.mult))
                then(dve.tensor_reduce(best[:], key[:], AX.X, ALU.max))
                then(dve.tensor_tensor(chosen[k][:], key[:], over_experts(best[:]), ALU.is_equal))
                if k == 0:
                    then(dve.scalar_tensor_tensor(work[:], chosen[0][:], -3e38, work[:], ALU.mult, ALU.add))
                then(dve.tensor_tensor(chosen[k][:], chosen[k][:], over_experts(valid[:]), ALU.mult))
            then(dve.tensor_tensor(key[:], chosen[0][:], chosen[1][:], ALU.add))
            dve.tensor_copy(both[:], key[:]).then_inc(counts_ready, 1)
            then(dve.tensor_reduce(counts[:], key[:].rearrange("p t e -> p e t"), AX.X, ALU.add))
            dve.tensor_copy(per_row[:], counts[:]).then_inc(counts_ready, 1)
            for k in range(2):
                then(dve.tensor_tensor(work[:], chosen[k][:], scores[:], ALU.mult))
                then(dve.tensor_reduce(payload[:, :, k, 1].bitcast(F32), work[:], AX.X, ALU.add))
            dve.wait_ge(ranks_done, 1)
            dve.wait_ge(counts_done, 1)
            then(dve.tensor_copy(counts[:], gu_ps[:, 0, 1, 0:EXPERTS]))
            wide = [P, EXPERTS, LIMITS]
            then(dve.tensor_tensor(over[:], counts[:].unsqueeze(2).broadcast_to(wide),
                                   limits[:].unsqueeze(1).broadcast_to(wide), ALU.is_gt))
            then(dve.tensor_reduce(blocks[:], over[:], AX.X, ALU.add))
            then(dve.tensor_copy(upto[:], blocks[:]))
            for n in range(1, EXPERTS):
                then(dve.tensor_tensor(upto[:, n:n + 1], upto[:, n - 1:n], blocks[:, n:n + 1], ALU.add))
            then(dve.tensor_tensor(start[:], upto[:], blocks[:], ALU.subtract))
            then(dve.tensor_scalar(start[:], start[:], float(SLOTS), None, ALU.mult))
            then(dve.tensor_tensor(rank[:], gu_ps[:, 0, 0, 0:TILES * EXPERTS].rearrange("p (t e) -> p t e", e=EXPERTS),
                                   over_tiles(start[:]), ALU.add))
            for k in range(2):
                then(dve.tensor_tensor(work[:], chosen[k][:], rank[:], ALU.mult))
                then(dve.tensor_reduce(slot_f[:], work[:], AX.X, ALU.add))
                dve.tensor_copy(slots[:, k, :], slot_f[:]).then_inc(slots_ready, 1)
                dve.wait_ge(slots_ready, k + 1)
            wide = [P, BLOCKS, EXPERTS]
            then(dve.tensor_tensor(passed[:], block_no[:].unsqueeze(2).broadcast_to(wide),
                                   upto[:].unsqueeze(1).broadcast_to(wide), ALU.is_ge))
            then(dve.tensor_reduce(expert_f[:], passed[:], AX.X, ALU.add))
            dve.tensor_scalar(expert_of[:], expert_f[0:1, :], float(EXPERTS - 1), None, ALU.min).then_inc(slots_ready, 1)
            dve.tensor_scalar(turnstile[:], turnstile[:], 1.0, None, ALU.mult).then_inc(slots_ready, 1)

            dve.wait_ge(w_hi_done, 2)
            dve.tensor_tensor(w13_lo[:].rearrange("p k c n -> p (k c n)"), raw[:],
                              w13_hi[:].rearrange("p k c n -> p (k c n)").bitcast(F32), ALU.subtract)\
                .then_inc(w_lo_done, 1)
            dve.tensor_tensor(w2_lo[:], raw2[:], w2_hi[:].bitcast(F32), ALU.subtract).then_inc(w_lo_done, 1)

            def window(u, i):
                n, known = u * 2 + i, isinstance(u, int)

                def low(m):
                    dve.wait_ge(hid_hi_done, MC * n + m + 1)
                    dve.tensor_tensor(hid_lo[:, m, :], hidden[:, m % 2, :], hid_hi[:, m, :].bitcast(F32), ALU.subtract)\
                        .then_inc(hid_lo_done, 1)

                for m in range(MC):
                    dve.wait_ge(silu_done, MC * n + m + 1)
                    dve.tensor_tensor(hidden[:, m % 2, :], gu_ps[0:HC, m % 2, 1, 0:WT], gated[:, m % 2, :], ALU.mult)\
                        .then_inc(hidden_ready, 1)
                    low(m)
                for j in range(TPW):
                    R = ROWS[j]
                    tile = h_sb[0:R, bass.ds(n * TPW + j, 1), :].rearrange("p a n -> p (a n)")
                    dve.wait_ge(y_done, TPW * n + j + 1)
                    dve.tensor_tensor(tile, y_ps[0:R, (TPW * i + j) % 2, :], tile, ALU.add).then_inc(h_added, 1)
            run_steps(dve, WIN // 2, 2, 0, window)


def run_experts(nc, w1, w2, w3, ident, rows, table, expert_of, routed_out):
    with ExitStack() as ctx:
        def sb(name, shape, dt=F32):
            return ctx.enter_context(nc.sbuf_tensor(name, shape, dt))

        def sem(name):
            return ctx.enter_context(nc.semaphore(name))

        HALVES = SLOTS // P
        raw = sb("eraw", [P, KC, 2, HID])
        raw2 = sb("eraw2", [HC, MC, DIM])
        w13_hi = sb("ew13_hi", [P, 2, KC, 2, HID], F32R)
        w13_lo = sb("ew13_lo", [P, 2, KC, 2, HID], F32R)
        w2_hi = sb("ew2_hi", [HC, 2, MC, DIM], F32R)
        w2_lo = sb("ew2_lo", [HC, 2, MC, DIM], F32R)
        entry = sb("entry", [P, 2, HALVES, 2], U32)
        gathered = sb("gathered", [P, 2, HALVES, DIM])
        xt_hi = sb("ext_hi", [P, KC, SLOTS], F32R)
        xt_lo = sb("ext_lo", [P, KC, SLOTS], F32R)
        gated = sb("egated", [HC, 2, SLOTS])
        hidden = sb("ehidden", [HC, 2, SLOTS])
        hid_hi = sb("ehid_hi", [HC, MC, SLOTS], F32R)
        hid_lo = sb("ehid_lo", [HC, MC, SLOTS], F32R)
        y = sb("y", [P, HALVES, DIM])
        turnstile = sb("eturnstile", [P, 2])
        xt_ps = ctx.enter_context(nc.psum_tensor("ext_ps", [P, HALVES, KC, P], F32))
        gu_ps = ctx.enter_context(nc.psum_tensor("egu_ps", [P, MC, 2, SLOTS], F32))
        y_ps = ctx.enter_context(nc.psum_tensor("ey_ps", [P, HALVES, DIM], F32))

        w_in = [sem(f"ew_in{c}") for c in range(KC)]
        w_hi_done = sem("ew_hi_done")
        w_lo_done = sem("ew_lo_done")
        entry_in = sem("entry_in")
        turnstile_set = sem("turnstile_set")
        gathered_in = [sem(f"gathered_in{k}") for k in range(2)]
        scaled = sem("scaled")
        turned = sem("eturned")
        turned_hi = sem("eturned_hi")
        turned_lo = sem("eturned_lo")
        gu_done = sem("egu_done")
        silu_done = sem("esilu_done")
        hidden_ready = sem("ehidden_ready")
        hid_hi_done = sem("ehid_hi_done")
        hid_lo_done = sem("ehid_lo_done")
        y_done = sem("ey_done")
        y_taken = sem("y_taken")
        y_stored = [sem(f"y_stored{k}") for k in range(HALVES)]

        BTURNS = BLOCKS // 2
        assert BLOCKS % 2 == 0

        def steps(eng, step):
            def both(u, i):
                step(earlier(u, i, 0, BTURNS, 2), earlier(u, i, 1, BTURNS, 2))
            run_steps(eng, BTURNS, 2, 1, both)

        def count(at):
            return at[0] * 2 + at[1]

        def is_first(at, n=1):
            return isinstance(at[0], int) and count(at) < n

        block = ctx.enter_context(nc.Block())

        @block.sync
        def _(sp):
            def step(front, rear):
                if front:
                    f = count(front)
                    e = sp.value_load(expert_of[0:1, bass.ds(f, 1)], min_val=0, max_val=EXPERTS - 1)
                    for c in range(KC):
                        if not is_first(front):
                            sp.wait_ge(w_lo_done, KC * (f - 1) + c + 1)
                        for k, w in enumerate((w1, w3)):
                            sp.dma_start(raw[:, c, k, :], w[bass.ds(e, 1), c * P:c * P + P, :]
                                         .rearrange("a p n -> (a p) n")).then_inc(w_in[c], 16)
                        sp.dma_start(raw2[:, c, :], w2[bass.ds(e, 1), c * HC:c * HC + HC, :]
                                     .rearrange("a p n -> (a p) n")).then_inc(w_in[c], 16)
            steps(sp, step)

        @block.gpsimd
        def _(pool):
            pool.memset(turnstile[:], 0.0).then_inc(turnstile_set, 1)
            pool.wait_ge(turnstile_set, 1)

            def step(front, rear):
                if front:
                    (u, i), f = front, count(front)
                    if not is_first(front, 2):
                        pool.wait_ge(turned, HALVES * (f - 1))
                    pool.dma_start(entry[:, i], table[bass.ds(f * SLOTS, SLOTS), :]
                                   .rearrange("(h p) w -> p h w", p=P)).then_inc(entry_in, 16)
                    pool.wait_ge(entry_in, 16 * (f + 1))
                    if not is_first(front):
                        pool.wait_ge(turnstile_set, f + 1)
                    pool.tensor_tensor(turnstile[:, 0:1], turnstile[:, 1:2], turnstile[:, 1:2], ALU.mult)\
                        .then_inc(turnstile_set, 1)
                    for half in range(HALVES):
                        pool.indirect_dma_start(out=gathered[:, i, half, :], out_offset=None, in_=rows[:, :],
                                                in_offset=bass.IndirectOffsetOnAxis(ap=entry[:, i, half, 0:1], axis=0))\
                            .then_inc(gathered_in[i], 16)
            steps(pool, step)

        @block.scalar
        def _(act):
            def step(front, rear):
                f, r = front and count(front), rear and count(rear)

                def weights(c):
                    i = front[1]
                    act.wait_ge(w_in[c], 48 * (f + 1))
                    if c == 0 and not is_first(front, 2):
                        act.wait_ge(y_done, HALVES * (f - 1))
                    act.copy(w13_hi[:, i, c], raw[:, c]).then_inc(w_hi_done, 1)
                    act.copy(w2_hi[:, i, c, :], raw2[:, c, :]).then_inc(w_hi_done, 1)

                def rows_high(half):
                    act.wait_ge(turned, HALVES * f + half + 1)
                    act.copy(xt_hi[:, :, half * P:half * P + P], xt_ps[:, half]).then_inc(turned_hi, 1)

                def silu(m):
                    act.wait_ge(gu_done, MC * r + m + 1)
                    if m >= 2 or not is_first(rear):
                        act.wait_ge(hidden_ready, MC * r + m - 1)
                    act.activation(gated[:, m % 2, :], gu_ps[0:HC, m, 0, :], ACT.Silu).then_inc(silu_done, 1)

                def hidden_high(m):
                    act.wait_ge(hidden_ready, MC * r + m + 1)
                    if m == 0 and not is_first(rear):
                        act.wait_ge(y_done, HALVES * r)
                    act.copy(hid_hi[:, m, :], hidden[:, m % 2, :]).then_inc(hid_hi_done, 1)

                def take(half):
                    act.wait_ge(y_done, HALVES * r + half + 1)
                    if not is_first(rear):
                        act.wait_ge(y_stored[half], 16 * r)
                    act.copy(y[:, half, :], y_ps[:, half, :]).then_inc(y_taken, 1)

                def store(half):
                    act.wait_ge(y_taken, HALVES * r + half + 1)
                    act.dma_start(routed_out[bass.ds(r * SLOTS + half * P, P), :], y[:, half, :])\
                        .then_inc(y_stored[half], 16)

                for m in range(MC):
                    if rear:
                        silu(m)
                        hidden_high(m)
                    if front:
                        weights(m)
                if front:
                    for half in range(HALVES):
                        rows_high(half)
                if rear:
                    for half in range(HALVES):
                        take(half)
                        store(half)
            steps(act, step)
            for stored in y_stored:
                act.wait_ge(stored, 16 * BLOCKS)

        @block.tensor
        def _(pe):
            def step(front, rear):
                f, r = front and count(front), rear and count(rear)

                def gate_and_up(m):
                    i = rear[1]
                    if m == 0:
                        pe.wait_ge(turned_lo, HALVES * (r + 1))
                        pe.wait_ge(w_lo_done, KC * (r + 1))
                    if not is_first(rear):
                        pe.wait_ge(hidden_ready, MC * (r - 1) + m + 1)
                    cols = slice(m * HC, m * HC + HC)
                    for k in range(2):
                        for c in range(KC):
                            w, wl = w13_hi[:, i, c, k, cols], w13_lo[:, i, c, k, cols]
                            for q, (lhs, rhs) in enumerate(((w, xt_hi), (wl, xt_hi), (w, xt_lo))):
                                mm = pe.matmul(gu_ps[0:HC, m, k, :], lhs, rhs[:, c, :], start=c == 0 and q == 0,
                                               stop=c == KC - 1 and q == 2)
                    mm.then_inc(gu_done, 1)

                def turn(half):
                    i = front[1]
                    pe.wait_ge(scaled, HALVES * f + half + 1)
                    if rear:
                        pe.wait_ge(turned_lo, HALVES * (f - 1) + half + 1)
                    for c in range(KC):
                        mm = pe.transpose(xt_ps[:, half, c, :], gathered[:, i, half, c * P:c * P + P], ident[:])
                    mm.then_inc(turned, 1)

                def down(half):
                    i = rear[1]
                    if not is_first(rear):
                        pe.wait_ge(y_taken, HALVES * (r - 1) + half + 1)
                    for c in range(MC):
                        if half == 0:
                            pe.wait_ge(hid_lo_done, MC * r + c + 1)
                        tok = slice(half * P, half * P + P)
                        h, hl = hid_hi[:, c, tok], hid_lo[:, c, tok]
                        for q, (lhs, rhs) in enumerate(((h, w2_hi), (hl, w2_hi), (h, w2_lo))):
                            mm = pe.matmul(y_ps[:, half, :], lhs, rhs[:, i, c, :], start=c == 0 and q == 0,
                                           stop=c == MC - 1 and q == 2)
                    mm.then_inc(y_done, 1)

                if rear:
                    for m in range(MC):
                        gate_and_up(m)
                if front:
                    for half in range(HALVES):
                        turn(half)
                if rear:
                    for half in range(HALVES):
                        down(half)
            steps(pe, step)

        @block.vector
        def _(dve):
            def step(front, rear):
                f, r = front and count(front), rear and count(rear)

                def weights(c):
                    i = front[1]
                    dve.wait_ge(w_hi_done, 2 * (KC * f + c + 1))
                    dve.tensor_tensor(w13_lo[:, i, c], raw[:, c], w13_hi[:, i, c].bitcast(F32), ALU.subtract)
                    dve.tensor_tensor(w2_lo[:, i, c, :], raw2[:, c, :], w2_hi[:, i, c, :].bitcast(F32), ALU.subtract)\
                        .then_inc(w_lo_done, 1)

                def scale(half):
                    i = front[1]
                    if half == 0:
                        dve.wait_ge(gathered_in[i], 16 * HALVES * (front[0] + 1))
                    x = gathered[:, i, half, :]
                    dve.tensor_scalar(x, x, entry[:, i, half, 1:2].bitcast(F32), None, ALU.mult).then_inc(scaled, 1)

                def rows_low(half):
                    dve.wait_ge(turned_hi, HALVES * f + half + 1)
                    cols = slice(half * P, half * P + P)
                    dve.tensor_tensor(xt_lo[:, :, cols], xt_ps[:, half], xt_hi[:, :, cols].bitcast(F32),
                                      ALU.subtract).then_inc(turned_lo, 1)

                def multiply(m):
                    dve.wait_ge(silu_done, MC * r + m + 1)
                    dve.tensor_tensor(hidden[:, m % 2, :], gu_ps[0:HC, m, 1, :], gated[:, m % 2, :], ALU.mult)\
                        .then_inc(hidden_ready, 1)

                def hidden_low(m):
                    dve.wait_ge(hid_hi_done, MC * r + m + 1)
                    dve.tensor_tensor(hid_lo[:, m, :], hidden[:, m % 2, :], hid_hi[:, m, :].bitcast(F32),
                                      ALU.subtract).then_inc(hid_lo_done, 1)

                if front:
                    for half in range(HALVES):
                        scale(half)
                for m in range(MC):
                    if rear:
                        multiply(m)
                        hidden_low(m)
                    if front:
                        weights(m)
                if front:
                    for half in range(HALVES):
                        rows_low(half)
            steps(dve, step)


def combine(nc, h_sb, slots, routed_out, out):
    RING = 6
    flat = out.rearrange("b p d -> (b p) d")
    with ExitStack() as ctx:
        picked = ctx.enter_context(nc.sbuf_tensor("picked", [P, RING, 2, DIM], F32))
        picked_in = [ctx.enter_context(nc.semaphore(f"picked_in{k}")) for k in range(RING)]
        added = ctx.enter_context(nc.semaphore("added"))
        stored = ctx.enter_context(nc.semaphore("out_stored"))
        block = ctx.enter_context(nc.Block())

        @block.gpsimd
        def _(pool):
            for n in range(TILES):
                R = ROWS[n % TPW]
                if n >= RING:
                    pool.wait_ge(added, 2 * (n - RING + 1))
                for k in range(2):
                    pool.indirect_dma_start(out=picked[0:R, n % RING, k, :], out_offset=None, in_=routed_out[:, :],
                                            in_offset=bass.IndirectOffsetOnAxis(ap=slots[0:R, k, n:n + 1], axis=0))\
                        .then_inc(picked_in[n % RING], 16)

        @block.vector
        def _(dve):
            for n in range(TILES):
                R = ROWS[n % TPW]
                dve.wait_ge(picked_in[n % RING], 32 * (n // RING + 1))
                for k in range(2):
                    if k:
                        dve.wait_ge(added, 2 * n + 1)
                    dve.tensor_tensor(h_sb[0:R, n, :], h_sb[0:R, n, :], picked[0:R, n % RING, k, :], ALU.add)\
                        .then_inc(added, 1)

        @block.sync
        def _(sp):
            for n in range(TILES):
                w, j = divmod(n, TPW)
                sp.wait_ge(added, 2 * n + 2)
                sp.dma_start(flat[w * WT + P * j:w * WT + P * j + ROWS[j], :], h_sb[0:ROWS[j], n, :])\
                    .then_inc(stored, 16)
            sp.wait_ge(stored, 16 * TILES)


def build(nc, x, W, b, g1, b1, g2, b2, Wq, Wk, Wv, Wo, gate_w, w1, w2, w3, sw1, sw2, sw3, bias, out):
    normed_t = nc.dram_tensor("normed_t", (WIN, P, 2, KC, WT), F32).ap()
    rows = nc.dram_tensor("rows", (TOK, DIM), F32).ap()
    table = nc.dram_tensor("table", (BLOCKS * SLOTS, 2), U32).ap()
    routed_out = nc.dram_tensor("routed_out", (BLOCKS * SLOTS, DIM), F32).ap()
    with ExitStack() as ctx:
        ident = ctx.enter_context(nc.sbuf_tensor("ident", [P, P], F32))
        h_sb = ctx.enter_context(nc.sbuf_tensor("h_sb", [P, WIN * TPW, DIM], F32))
        constants(nc, ident)
        tokenise(nc, x, W, b, g1, b1, g2, b2, ident, h_sb, normed_t)
        attend(nc, Wq, Wk, Wv, Wo, ident, h_sb, normed_t)
        slots = ctx.enter_context(nc.sbuf_tensor("slots", [P, 2, TILES], U32))
        expert_of = ctx.enter_context(nc.sbuf_tensor("expert_of", [1, BLOCKS], U32))
        route_and_share(nc, gate_w, bias, sw1, sw2, sw3, ident, h_sb, normed_t, rows, table, slots, expert_of)
        run_experts(nc, w1, w2, w3, ident, rows, table, expert_of, routed_out)
        combine(nc, h_sb, slots, routed_out, out)


def constants(nc, ident):
    with nc.semaphore("cleared") as cleared, nc.Block() as block:
        @block.gpsimd
        def _(pool):
            pool.memset(ident[:], 0.0).then_inc(cleared, 1)
            pool.wait_ge(cleared, 1)
            pool.affine_select(out=ident[:], in_=ident[:], compare_op=ALU.not_equal, fill=1.0, base=0,
                               pattern=[[-1, P]], channel_multiplier=1)


_INS = ['x', 'L0_tok_W', 'L0_tok_b', 'L0_tok_g1', 'L0_tok_b1', 'L0_tok_g2', 'L0_tok_b2', 'L0_attn_Wq', 'L0_attn_Wk',
        'L0_attn_Wv', 'L0_attn_Wo', 'L0_ffn_gate_w', 'L0_ffn_w1', 'L0_ffn_w2', 'L0_ffn_w3', 'L0_ffn_sw1',
        'L0_ffn_sw2', 'L0_ffn_sw3', 'L0_ffn_expert_bias']


def kernel(**inputs):
    import numpy as _np
    import concourse.bacc as _bacc
    from concourse.bass_utils import run_bass_kernel_spmd as _run

    nc = _bacc.Bacc("TRN2", target_bir_lowering=False, num_devices=1)
    arrays, args = {}, []
    for name in _INS:
        a = _np.ascontiguousarray(inputs[name])
        arrays[f"in_{name}"] = a
        args.append(nc.dram_tensor(f"in_{name}", a.shape, mybir.dt.from_np(a.dtype), kind="ExternalInput").ap())
    args.append(nc.dram_tensor("out_dram", (BATCH, NPATCH, DIM), F32, kind="ExternalOutput").ap())
    build(nc, *args)
    return _run(nc, [arrays], core_ids=[0]).results[0]["out_dram"]
```

```python
from contextlib import ExitStack
import numpy as np
import concourse.bass as bass
from concourse import mybir

ALU = mybir.AluOpType
ACT = mybir.ActivationFunctionType
AX = mybir.AxisListType
F32 = mybir.dt.float32
F32R = mybir.dt.float32r
U32 = mybir.dt.uint32

P = 128
BATCH, FRAMES, FEAT, TIN = 128, 375, 64, 16
NPATCH = FRAMES // TIN
IN_DIM = TIN * FEAT
DIM = 512
TOK = BATCH * NPATCH
WSEQ = 16
WT = WSEQ * NPATCH
WIN = TOK // WT
ROWS = [128, 128, WT - 256]
TPW = len(ROWS)
KC = DIM // P
XC = IN_DIM // P
EPS_TOK = 1e-6
EPS_LN = 1e-5


def pieces(j):
    out, n, end = [], 128 * j, 128 * j + ROWS[j]
    while n < end:
        s, p = divmod(n, NPATCH)
        whole = (end - n) // NPATCH if p == 0 else 0
        k = whole * NPATCH if whole else min(NPATCH - p, end - n)
        out.append((n - 128 * j, s, p, whole, k))
        n += k
    return out


TPU = 2 * TPW
UNITS = WIN // 2


def rows_of(i):
    return ROWS[i % TPW]


def run_steps(eng, turns, per, lag, step, peeled=1):
    for n in range(peeled * per):
        step(n // per, n % per)
    with eng.Fori(peeled, turns) as u:
        for i in range(per):
            step(u, i)
    for i in range(lag):
        step(turns + i // per, i % per)


def earlier(u, i, n, turns, per):
    d, i = divmod(i - n, per)
    if isinstance(u, int) and not 0 <= u + d < turns:
        return None
    return u + d, i


def tile_steps(eng, lag, step):
    run_steps(eng, UNITS, TPU, lag, step)


def back(u, i, n):
    return earlier(u, i, n, UNITS, TPU)


def number(at):
    return at[0] * TPU + at[1]


def first(at, n):
    return isinstance(at[0], int) and number(at) < n


def tokenise(nc, x, W, b, g1, b1, g2, b2, ident, h_sb, normed_t):
    with ExitStack() as ctx:
        def sb(name, shape, dt=F32):
            return ctx.enter_context(nc.sbuf_tensor(name, shape, dt))

        def sem(name):
            return ctx.enter_context(nc.semaphore(name))

        w_raw = sb("w_raw", [P, XC, DIM])
        w_hi = sb("w_hi", [P, XC, DIM], F32R)
        w_lo = sb("w_lo", [P, XC, DIM], F32R)
        g1_col = sb("g1_col", [P, XC])
        b1_col = sb("b1_col", [P, XC])
        zeros = sb("zeros", [P, P])
        b1_wide = sb("b1_wide", [P, XC, P])
        g2_row = sb("g2_row", [P, DIM])
        b2_row = sb("b2_row", [P, DIM])
        bias_row = sb("bias_row", [P, DIM])
        turnstile = sb("turnstile", [P, 1])
        minus_half = sb("minus_half", [P, 1])
        minus_one = sb("minus_one", [P, 1])
        xin = sb("xin", [P, 3, IN_DIM])
        xt_hi = sb("xt_hi", [P, 2, XC, P], F32R)
        xt_lo = sb("xt_lo", [P, 2, XC, P], F32R)
        proj = sb("proj", [P, 2, DIM])
        norm3 = sb("norm3", [P, 2, DIM])
        ht = sb("ht", [P, 3, 2, KC, P], F32R)
        st = [sb(f"st{i}", [P, 3, 2, 6]) for i in range(3)]
        mv = [sb(f"mv{i}", [P, 3, 2]) for i in range(3)]
        ve = [sb(f"ve{i}", [P, 3]) for i in range(3)]
        rstd = [sb(f"rstd{i}", [P, 3]) for i in range(3)]
        shift = [sb(f"shift{i}", [P, 3]) for i in range(3)]
        xt_ps = ctx.enter_context(nc.psum_tensor("xt_ps", [P, 4, KC, P], F32))
        acc = ctx.enter_context(nc.psum_tensor("acc", [P, 2, DIM], F32))
        ht_ps = ctx.enter_context(nc.psum_tensor("ht_ps", [P, 2, KC, P], F32))

        consts_in = sem("consts_in")
        w_in = [sem(f"w_in{c}") for c in range(XC)]
        x_in = [sem(f"x_in{j}") for j in range(TPW)]
        b1_spread = sem("b1_spread")
        w_hi_ready = sem("w_hi_ready")
        w_ready = sem("w_ready")
        bias_mm = sem("bias_mm")
        bias_ready = sem("bias_ready")
        consts_set = sem("consts_set")
        stats_done = [sem(f"stats_done{i}") for i in range(3)]
        mv_done = [sem(f"mv_done{i}") for i in range(3)]
        var_ready = [sem(f"var_ready{i}") for i in range(3)]
        powered = [sem(f"powered{i}") for i in range(3)]
        rstd_ready = [sem(f"rstd_ready{i}") for i in range(3)]
        xhat_ready = sem("xhat_ready")
        xt_done = sem("xt_done")
        xt_hi_done = sem("xt_hi_done")
        xt_lo_done = sem("xt_lo_done")
        acc_done = sem("acc_done")
        proj_ready = sem("proj_ready")
        centred = sem("centred")
        h_ready = sem("h_ready")
        norm3_ready = sem("norm3_ready")
        ht_done = sem("ht_done")
        ht_hi_done = sem("ht_hi_done")
        ht_lo_done = sem("ht_lo_done")
        ht_stored = [sem(f"ht_stored{k}") for k in range(3)]

        flat = x.rearrange("b t f -> b (t f)")
        XHAT, PROJ, LN2, LN3, HT = 1, 3, 4, 5, 6
        block = ctx.enter_context(nc.Block())

        @block.sync
        def _(sp):
            with nc.allow_non_contiguous_dma("columns of two short vectors"):
                sp.dma_start(g1_col[:], g1.rearrange("(c p) -> p c", p=P)).then_inc(consts_in, 16)
                sp.dma_start(b1_col[:], b1.rearrange("(c p) -> p c", p=P)).then_inc(consts_in, 16)
            for row, vector in ((g2_row, g2), (b2_row, b2), (bias_row, b)):
                sp.dma_start(row[:], vector.partition_broadcast(P)).then_inc(consts_in, 16)

            def load_weights():
                for c in range(XC):
                    sp.dma_start(w_raw[:, c, :], W[c * P:c * P + P, :]).then_inc(w_in[c], 16)

            def load(at):
                (u, i), j = at, at[1] % TPW
                if not first(at, 3):
                    sp.wait_ge(xt_done, 2 * (number(at) - 2))
                seq = u * 2 * WSEQ + i // TPW * WSEQ
                for row, s, p, whole, k in pieces(j):
                    src = flat[bass.ds(seq + s, whole or 1), p * IN_DIM:(p + (NPATCH if whole else k)) * IN_DIM]
                    sp.dma_start(xin[row:row + k, i % 3, :], src.rearrange("s (p d) -> s p d", d=IN_DIM))\
                        .then_inc(x_in[j], 16)

            def step(u, i):
                if at := back(u, i, 0):
                    load(at)
                    if first(at, 1):
                        load_weights()
            tile_steps(sp, 0, step)
            for stored in ht_stored:
                sp.wait_ge(stored, 16 * UNITS * TPU // 3)

        @block.gpsimd
        def _(pool):
            pool.memset(minus_half[:], -0.5).then_inc(consts_set, 1)
            pool.memset(minus_one[:], -1.0).then_inc(consts_set, 1)
            pool.memset(zeros[:], 0.0).then_inc(consts_set, 1)
            pool.wait_ge(consts_set, 3)
            pool.wait_ge(consts_in, 16 * 5)
            for c in range(XC):
                pool.tensor_scalar(b1_wide[:, c, :], zeros[:], b1_col[:, c:c + 1], None, ALU.add)\
                    .then_inc(b1_spread, 1)

            def power(n, at):
                i, R = at[1] % 3, rows_of(at[1])
                pool.wait_ge(var_ready[n], number(at) + 1)
                power = pool.tensor_tensor(rstd[n][0:R, i:i + 1], ve[n][0:R, i:i + 1], minus_half[0:R, :], ALU.pow)
                if n == 1:
                    power.then_inc(rstd_ready[n], 1)
                    return
                power.then_inc(powered[n], 1)
                pool.tensor_tensor(shift[n][0:R, i:i + 1], mv[n][0:R, i, 0:1], minus_one[0:R, :], ALU.mult)\
                    .then_inc(powered[n], 1)
                pool.wait_ge(powered[n], 2 * number(at) + 2)
                pool.tensor_tensor(shift[n][0:R, i:i + 1], shift[n][0:R, i:i + 1], rstd[n][0:R, i:i + 1], ALU.mult)\
                    .then_inc(rstd_ready[n], 1)

            def store(at):
                (u, i), j = at, at[1] % TPW
                pool.wait_ge(ht_lo_done, number(at) + 1)
                pool.dma_start(normed_t[u * 2 + i // TPW, :, :, :, 128 * j:128 * j + ROWS[j]],
                             ht[:, i % 3, :, :, 0:ROWS[j]].bitcast(F32)).then_inc(ht_stored[i % 3], 16)

            def step(u, i):
                for n, lag in enumerate((0, PROJ, LN2)):
                    if at := back(u, i, lag):
                        power(n, at)
                if at := back(u, i, HT):
                    store(at)
            tile_steps(pool, HT, step)

        @block.scalar
        def _(act):
            def weights_high():
                act.wait_ge(consts_in, 16 * 5)
                for c in range(XC):
                    act.wait_ge(w_in[c], 16)
                    act.activation(w_hi[:, c, :], w_raw[:, c, :], ACT.Identity, scale=g1_col[:, c:c + 1])\
                        .then_inc(w_hi_ready, 1)

            def normalise(n, at, out, source, done):
                i, R = at[1] % 3, rows_of(at[1])
                act.wait_ge(rstd_ready[n], number(at) + 1)
                act.activation(out, source, ACT.Identity, bias=shift[n][0:R, i:i + 1],
                               scale=rstd[n][0:R, i:i + 1]).then_inc(done, 1)

            def patches_high(at):
                i, R = at[1], rows_of(at[1])
                if not first(at, 2):
                    act.wait_ge(acc_done, number(at) - 1)
                for half in range(2):
                    act.wait_ge(xt_done, 2 * number(at) + half + 1)
                    act.copy(xt_hi[:, i % 2, half * KC:half * KC + KC, 0:R],
                             xt_ps[:, 2 * (i % 2) + half, :, 0:R]).then_inc(xt_hi_done, 1)

            def h_high(at):
                i, R = at[1], rows_of(at[1])
                act.wait_ge(ht_done, number(at) + 1)
                if not first(at, 3):
                    act.wait_ge(ht_stored[i % 3], 16 * (at[0] * 2 + i // 3))
                act.copy(ht[:, i % 3, 0, :, 0:R], ht_ps[:, i % 2, :, 0:R]).then_inc(ht_hi_done, 1)

            def step(u, i):
                if at := back(u, i, XHAT):
                    x = xin[0:rows_of(at[1]), at[1] % 3, :]
                    normalise(0, at, x, x, xhat_ready)
                    if first(at, 1):
                        weights_high()
                if at := back(u, i, LN3):
                    R = rows_of(at[1])
                    if not first(at, 2):
                        act.wait_ge(ht_done, number(at) - 1)
                    normalise(2, at, norm3[0:R, at[1] % 2, :], h_sb[0:R, number(at), :], norm3_ready)
                if at := back(u, i, XHAT):
                    patches_high(at)
                if at := back(u, i, LN3):
                    h_high(at)
            tile_steps(act, LN3, step)

        @block.tensor
        def _(pe):
            pe.wait_ge(b1_spread, XC)
            for c in range(XC):
                pe.wait_ge(w_in[c], 16)
                mm = pe.matmul(acc[:, 0, :], b1_wide[:, c, :], w_raw[:, c, :], start=c == 0, stop=c == XC - 1)
            mm.then_inc(bias_mm, 1)

            def patches_t(at):
                i, R = at[1], rows_of(at[1])
                pe.wait_ge(xhat_ready, number(at) + 1)
                for half in range(2):
                    if not first(at, 2):
                        pe.wait_ge(xt_lo_done, 2 * (number(at) - 2) + half + 1)
                    for c in range(KC):
                        k = half * KC + c
                        mm = pe.transpose(xt_ps[:, 2 * (i % 2) + half, c, 0:R],
                                          xin[0:R, i % 3, k * P:k * P + P], ident[0:R, 0:R])
                    mm.then_inc(xt_done, 1)

            def project(at):
                i, R = at[1], rows_of(at[1])
                pe.wait_ge(xt_lo_done, 2 * number(at) + 2)
                if first(at, 1):
                    pe.wait_ge(bias_ready, 1)
                if not first(at, 2):
                    pe.wait_ge(proj_ready, number(at) - 1)
                for c in range(XC):
                    if first(at, 1):
                        pe.wait_ge(w_ready, c + 1)
                    for lhs, rhs in ((xt_hi, w_hi), (xt_lo, w_hi), (xt_hi, w_lo)):
                        mm = pe.matmul(acc[0:R, i % 2, :], lhs[:, i % 2, c, 0:R], rhs[:, c, :],
                                       start=c == 0 and lhs is xt_hi and rhs is w_hi,
                                       stop=c == XC - 1 and rhs is w_lo)
                mm.then_inc(acc_done, 1)

            def h_t(at):
                i, R = at[1], rows_of(at[1])
                pe.wait_ge(norm3_ready, number(at) + 1)
                if not first(at, 2):
                    pe.wait_ge(ht_lo_done, number(at) - 1)
                for c in range(KC):
                    mm = pe.transpose(ht_ps[:, i % 2, c, 0:R], norm3[0:R, i % 2, c * P:c * P + P],
                                      ident[0:R, 0:R])
                mm.then_inc(ht_done, 1)

            def step(u, i):
                if at := back(u, i, XHAT):
                    patches_t(at)
                if at := back(u, i, XHAT + 1):
                    project(at)
                if at := back(u, i, LN3):
                    h_t(at)
            tile_steps(pe, LN3, step)

        @block.vector
        def _(dve):
            def weights_low():
                for c in range(XC):
                    dve.wait_ge(w_hi_ready, c + 1)
                    dve.scalar_tensor_tensor(w_lo[:, c, :], w_raw[:, c, :], g1_col[:, c:c + 1],
                                             w_hi[:, c, :].bitcast(F32), ALU.mult, ALU.subtract).then_inc(w_ready, 1)
                dve.wait_ge(bias_mm, 1)
                dve.tensor_tensor(bias_row[:], acc[:, 0, :], bias_row[:], ALU.add).then_inc(bias_ready, 1)
                dve.wait_ge(bias_ready, 1)

            def statistics(n, at, source, eps):
                i, R = at[1] % 3, rows_of(at[1])
                halves = source.shape[-1] // DIM
                dve.memset(turnstile[:], 0.0)
                for k in range(halves):
                    dve.bn_stats(st[n][0:R, i, k, :], source[:, k * DIM:k * DIM + DIM]).then_inc(stats_done[n], 1)
                dve.wait_ge(stats_done[n], halves * (number(at) + 1))
                dve.memset(turnstile[:], 0.0)
                dve.bn_aggr(mv[n][0:R, i, :], st[n][0:R, i, 0:halves, :].rearrange("p a b -> p (a b)"))\
                    .then_inc(mv_done[n], 1)
                dve.wait_ge(mv_done[n], number(at) + 1)
                dve.tensor_scalar(ve[n][0:R, i:i + 1], mv[n][0:R, i, 1:2], eps, None, ALU.add)\
                    .then_inc(var_ready[n], 1)

            def step(u, i):
                if (at := back(u, i, XHAT)) and first(at, 1):
                    dve.wait_ge(consts_in, 16 * 5)
                    weights_low()
                if at := back(u, i, XHAT + 1):
                    k, R = at[1] % 2, rows_of(at[1])
                    for half in range(2):
                        dve.wait_ge(xt_hi_done, 2 * number(at) + half + 1)
                        chunks = slice(half * KC, half * KC + KC)
                        dve.tensor_tensor(xt_lo[:, k, chunks, 0:R], xt_ps[:, 2 * k + half, :, 0:R],
                                          xt_hi[:, k, chunks, 0:R].bitcast(F32), ALU.subtract)\
                            .then_inc(xt_lo_done, 1)
                if at := back(u, i, PROJ):
                    k, R = at[1] % 2, rows_of(at[1])
                    dve.wait_ge(acc_done, number(at) + 1)
                    dve.tensor_tensor(proj[0:R, k, :], acc[0:R, k, :], bias_row[0:R, :], ALU.add)\
                        .then_inc(proj_ready, 1)
                    dve.wait_ge(proj_ready, number(at) + 1)
                    statistics(1, at, proj[0:R, k, :], EPS_TOK)
                if at := back(u, i, 0):
                    j, R = at[1] % TPW, rows_of(at[1])
                    whole_windows = at[0] * 2 + at[1] // TPW
                    dve.wait_ge(x_in[j], 16 * len(pieces(j)) * (whole_windows + 1))
                    statistics(0, at, xin[0:R, at[1] % 3, :], EPS_TOK)
                if at := back(u, i, LN2):
                    k, s, R = at[1] % 2, at[1] % 3, rows_of(at[1])
                    h = h_sb[0:R, number(at), :]
                    dve.wait_ge(rstd_ready[1], number(at) + 1)
                    dve.scalar_tensor_tensor(proj[0:R, k, :], proj[0:R, k, :], mv[1][0:R, s, 0:1], g2_row[0:R, :],
                                             ALU.subtract, ALU.mult).then_inc(centred, 1)
                    dve.wait_ge(centred, number(at) + 1)
                    dve.scalar_tensor_tensor(h, proj[0:R, k, :], rstd[1][0:R, s:s + 1], b2_row[0:R, :],
                                             ALU.mult, ALU.add).then_inc(h_ready, 1)
                    dve.wait_ge(h_ready, number(at) + 1)
                    statistics(2, at, h, EPS_LN)
                if at := back(u, i, HT):
                    k, R = at[1], rows_of(at[1])
                    dve.wait_ge(ht_hi_done, number(at) + 1)
                    dve.tensor_tensor(ht[:, k % 3, 1, :, 0:R], ht_ps[:, k % 2, :, 0:R],
                                      ht[:, k % 3, 0, :, 0:R].bitcast(F32), ALU.subtract).then_inc(ht_lo_done, 1)
            tile_steps(dve, HT, step)


HEADS, KV_HEADS, HD = 16, 4, 128
REP = HEADS // KV_HEADS
GSEQ = 4
GT = GSEQ * NPATCH
GPW = WSEQ // GSEQ
QW = REP * HD
WCOLS = QW + 2 * HD + DIM
WPART = WCOLS // 2
EPS_QK = 1e-6
MASKED = -16384.0
BF16 = mybir.dt.bfloat16
TURNS = KV_HEADS * WIN // 2
TURNS_HEAD = WIN // 2


def attend(nc, Wq, Wk, Wv, Wo, ident, h_sb, normed_t):
    with ExitStack() as ctx:
        def sb(name, shape, dt=F32):
            return ctx.enter_context(nc.sbuf_tensor(name, shape, dt))

        def sem(name):
            return ctx.enter_context(nc.semaphore(name))

        w_raw = sb("aw_raw", [P, WPART])
        w_hi = sb("aw_hi", [P, 2, KC, WCOLS], F32R)
        w_lo = sb("aw_lo", [P, 2, KC, WCOLS], F32R)
        hn = sb("hn", [P, 2, 2, KC, WT], F32R)
        squares = sb("squares", [P, QW])
        normed = sb("normed", [P, 2, QW])
        ssq = sb("ssq", [P, 4, REP])
        var = sb("var", [P, 4, REP])
        rs = sb("rs", [P, 4, REP])
        minus_half = sb("aminus_half", [P, REP])
        q_t = sb("q_t", [P, 2, REP, WT], F32R)
        k_t = sb("k_t", [P, 2, WT], F32R)
        v = sb("v", [GT, 2, GPW, HD], F32R)
        e = sb("e", [GT, 2, REP * GT])
        p_hi = sb("p_hi", [GT, 2, REP * GT], F32R)
        p_lo = sb("p_lo", [GT, 2, REP * GT], F32R)
        rden = sb("rden", [P, REP * GT])
        o_norm = sb("o_norm", [P, REP * GT])
        o_t = sb("o_t", [P, 2, REP, WT], F32R)
        ident_b = sb("ident_b", [GT, GT], BF16)
        mask = sb("mask", [GT, REP, GT], BF16)
        ones = sb("ones", [GT, 2], F32R)
        rden_col = sb("rden_col", [GT, REP])
        kv_ps = ctx.enter_context(nc.psum_tensor("kv_ps", [P, GPW, 2 * HD], F32))
        proj_ps = ctx.enter_context(nc.psum_tensor("proj_ps", [P, 2, DIM], F32))
        turn_ps = ctx.enter_context(nc.psum_tensor("turn_ps", [P, 2, DIM], F32))
        o_ps = ctx.enter_context(nc.psum_tensor("o_ps", [P, DIM], F32))
        den_ps = ctx.enter_context(nc.psum_tensor("den_ps", [P, DIM], F32))

        consts = sem("aconsts")
        mask_steps = sem("mask_steps")
        w_in = sem("aw_in")
        w_hi_done = sem("aw_hi_done")
        w_lo_done = sem("aw_lo_done")
        hn_in = [sem(f"hn_in{i}") for i in range(2)]
        raw_done = sem("raw_done")
        squared = sem("squared")
        summed = sem("summed")
        var_ready = sem("avar_ready")
        rs_ready = sem("rs_ready")
        normalised = sem("normalised")
        turned = sem("turned")
        turned_hi = sem("turned_hi")
        turned_lo = sem("turned_lo")
        v_hi_done = sem("v_hi_done")
        v_lo_done = sem("v_lo_done")
        scores_done = sem("scores_done")
        exp_done = sem("exp_done")
        p_hi_done = sem("p_hi_done")
        p_lo_done = sem("p_lo_done")
        pv_done = sem("pv_done")
        den_done = sem("den_done")
        rden_ready = sem("rden_ready")
        rden_spread = sem("rden_spread")
        rden_taken = sem("rden_taken")
        o_norm_ready = sem("o_norm_ready")
        o_hi_done = sem("o_hi_done")
        o_lo_done = sem("o_lo_done")
        out_done = sem("out_done")
        h_added = sem("h_added")

        K = 1
        TILE_AT = [0, None, 1, 2]

        def count(at):
            return at[0] * 2 + at[1]

        def first_step(at, n=1):
            return isinstance(at[0], int) and count(at) < n

        def steps(eng, step):
            def both(u, i):
                step(earlier(u, i, 0, TURNS, 2), earlier(u, i, 1, TURNS, 2))
            run_steps(eng, TURNS, 2, 1, both)

        def slot(at):
            return at[0] // TURNS_HEAD % 2

        def part_source(head, c, half):
            rows = bass.ds(c * P, P)
            if half == 0:
                return [(0, Wq[rows, bass.ds(head * REP, REP), :].rearrange("p h d -> p (h d)"), QW),
                        (QW, Wk[rows, bass.ds(head, 1), :].rearrange("p h d -> p (h d)"), HD)]
            return [(0, Wv[rows, bass.ds(head, 1), :].rearrange("p h d -> p (h d)"), HD),
                    (HD, Wo[bass.ds((head * REP + c) * P, P), :], DIM)]

        def next_part(at):
            u, i = at
            return (u // TURNS_HEAD + 1) % 2, u % TURNS_HEAD, slice(i * WPART, i * WPART + WPART)

        block = ctx.enter_context(nc.Block())

        @block.sync
        def _(sp):
            def load_hn(at):
                u, i = at
                if not first_step(at, 2):
                    sp.wait_ge(raw_done, 4 * (count(at) - 1))
                sp.dma_start(hn[:, i, :, :, :].bitcast(F32), normed_t[bass.ds((u % TURNS_HEAD) * 2 + i, 1)]
                             .rearrange("a p s c t -> (a p) s c t")).then_inc(hn_in[i], 16)

            def load_part(head, c, half):
                for col, src, n in part_source(head, c, half):
                    sp.dma_start(w_raw[:, col:col + n], src).then_inc(w_in, 16)

            load_hn((0, 0))
            for n in range(2 * KC):
                if n:
                    sp.wait_ge(w_lo_done, n)
                load_part(0, n // 2, n % 2)

            def step(front, rear):
                if front:
                    if not first_step(front):
                        load_hn(front)
                    u, i = front
                    sp.wait_ge(w_lo_done, 2 * KC + count(front))
                    load_part((u // TURNS_HEAD + 1) % KV_HEADS, u % TURNS_HEAD, i)
            steps(sp, step)

        @block.gpsimd
        def _(pool):
            pool.memset(minus_half[:], -0.5).then_inc(consts, 1)
            pool.memset(ones[:].bitcast(F32), 1.0).then_inc(consts, 1)
            pool.tensor_copy(ident_b[:], ident[0:GT, 0:GT]).then_inc(consts, 1)
            pool.memset(mask[:], 0.0).then_inc(mask_steps, 1)
            for j in range(GSEQ):
                part = mask[:, :, j * NPATCH:j * NPATCH + NPATCH]
                for side, (base, sign) in enumerate(((-j * NPATCH, 1), (j * NPATCH + NPATCH - 1, -1))):
                    pool.wait_ge(mask_steps, 1 + 2 * j + side)
                    pool.affine_select(out=part, in_=part, compare_op=ALU.is_ge, fill=MASKED, base=base,
                                       pattern=[[0, REP], [0, NPATCH]], channel_multiplier=sign)\
                        .then_inc(mask_steps, 1)
            pool.wait_ge(consts, 3)

            def step(front, rear):
                if front:
                    for s in range(4):
                        R = GT if s == K else ROWS[TILE_AT[s]]
                        pool.wait_ge(var_ready, 4 * count(front) + s + 1)
                        pool.tensor_tensor(rs[0:R, s, :], var[0:R, s, :], minus_half[0:R, :], ALU.pow)\
                            .then_inc(rs_ready, 1)
            steps(pool, step)

        @block.scalar
        def _(act):
            for n in range(2 * KC):
                act.wait_ge(w_in, 32 * (n + 1))
                act.copy(w_hi[:, 0, n // 2, n % 2 * WPART:n % 2 * WPART + WPART], w_raw[:]).then_inc(w_hi_done, 1)

            def step(front, rear):
                f, r = front and count(front), rear and count(rear)

                def exponent(g):
                    act.wait_ge(scores_done, 4 * r + g + 1)
                    if g >= 2 or not first_step(rear):
                        act.wait_ge(p_lo_done, 4 * r + g - 1)
                    act.activation(e[:, g % 2, :], turn_ps[0:GT, g % 2, 0:REP * GT], ACT.Exp,
                                   scale=float(HD) ** -0.5).then_inc(exp_done, 1)
                    if g >= 2 or not first_step(rear):
                        act.wait_ge(pv_done, 4 * r + g - 1)
                    act.wait_ge(exp_done, 4 * r + g + 1)
                    act.copy(p_hi[:, g % 2, :], e[:, g % 2, :]).then_inc(p_hi_done, 1)

                def square(s):
                    act.wait_ge(raw_done, 4 * f + s + 1)
                    if s or not first_step(front):
                        act.wait_ge(summed, 4 * f + s)
                    if s == K:
                        act.activation(squares[0:GT, :].rearrange("p (g d) -> p g d", g=GPW), kv_ps[0:GT, :, 0:HD],
                                       ACT.Square).then_inc(squared, 1)
                    else:
                        j = TILE_AT[s]
                        act.activation(squares[0:ROWS[j], :], proj_ps[0:ROWS[j], j % 2, :], ACT.Square)\
                            .then_inc(squared, 1)

                def values_high():
                    if rear:
                        act.wait_ge(pv_done, 4 * r + 4)
                    act.wait_ge(normalised, 4 * f + K + 1)
                    act.copy(v[:, 0], kv_ps[0:GT, :, HD:2 * HD]).then_inc(v_hi_done, 1)

                def take_reciprocals(g):
                    act.wait_ge(rden_spread, 4 * r + g + 1)
                    if g or not first_step(rear):
                        act.wait_ge(o_norm_ready, 4 * r + g)
                    act.copy(rden[:], den_ps[:, 0:REP * GT]).then_inc(rden_taken, 1)

                def out_high(g):
                    act.wait_ge(o_norm_ready, 4 * r + g + 1)
                    if g == 0 and not first_step(rear):
                        act.wait_ge(out_done, TPW * r)
                    act.copy(o_t[:, 0, :, g * GT:g * GT + GT], o_norm[:].rearrange("p (h t) -> p h t", h=REP))\
                        .then_inc(o_hi_done, 1)

                def turned_high(s):
                    act.wait_ge(turned, 4 * f + s + 1)
                    if rear:
                        act.wait_ge(scores_done, 4 * r + 4)
                    if s == K:
                        act.copy(k_t[:, 0, :], turn_ps[:, s % 2, 0:WT]).then_inc(turned_hi, 1)
                    else:
                        j, R = TILE_AT[s], ROWS[TILE_AT[s]]
                        act.copy(q_t[:, 0, :, j * P:j * P + R],
                                 turn_ps[:, s % 2, 0:REP * R].rearrange("p (h t) -> p h t", h=REP))\
                            .then_inc(turned_hi, 1)

                if rear:
                    exponent(0)
                    exponent(1)
                if front:
                    square(0)
                if rear:
                    exponent(2)
                    take_reciprocals(0)
                    out_high(0)
                    exponent(3)
                    take_reciprocals(1)
                    out_high(1)
                if front:
                    square(K)
                if rear:
                    take_reciprocals(2)
                    out_high(2)
                if front:
                    square(2)
                    turned_high(0)
                if rear:
                    take_reciprocals(3)
                    out_high(3)
                if front:
                    values_high()
                    square(3)
                    for s in range(1, 4):
                        turned_high(s)
                    into, c, cols = next_part(front)
                    act.wait_ge(w_in, 32 * (2 * KC + f + 1))
                    if rear:
                        act.wait_ge(out_done, TPW * (r + 1))
                    act.copy(w_hi[:, bass.ds(into, 1), bass.ds(c, 1), cols].rearrange("p a b n -> p (a b n)"), w_raw[:])\
                        .then_inc(w_hi_done, 1)
            steps(act, step)

        @block.tensor
        def _(pe):
            pe.wait_ge(mask_steps, 1 + 2 * GSEQ)
            pe.wait_ge(consts, 3)

            def products(out, pairs, start, stop):
                for n, (lhs, rhs) in enumerate(pairs):
                    mm = pe.matmul(out, lhs, rhs, start=start and n == 0, stop=stop and n == len(pairs) - 1)
                return mm

            def weights(at, c, cols):
                return [w[:, bass.ds(slot(at), 1), c, cols].rearrange("p a n -> p (a n)") for w in (w_hi, w_lo)]

            def step(front, rear):
                f, r = front and count(front), rear and count(rear)

                def query(j):
                    i, R = front[1], ROWS[j]
                    if j == 0:
                        pe.wait_ge(hn_in[i], 16 * (front[0] + 1))
                        pe.wait_ge(w_lo_done, 2 * KC + (front[0] // TURNS_HEAD) * WIN)
                    if j < 2 and rear and not first_step(rear):
                        pe.wait_ge(h_added, TPW * (r - 1) + 2 + j)
                    if j == 2:
                        pe.wait_ge(normalised, 4 * f + 1)
                    for c in range(KC):
                        hi, lo = (hn[:, i, k, c, j * P:j * P + R] for k in range(2))
                        w, wl = weights(front, c, slice(0, QW))
                        mm = products(proj_ps[0:R, j % 2, :], ((hi, w), (lo, w), (hi, wl)), c == 0, c == KC - 1)
                    mm.then_inc(raw_done, 1)

                def keys_values(groups):
                    i = front[1]
                    if groups[0] == 0 and rear:
                        pe.wait_ge(v_lo_done, f)
                        pe.wait_ge(normalised, 4 * (f - 1) + K + 1)
                    for g in groups:
                        for c in range(KC):
                            hi, lo = (hn[:, i, k, c, g * GT:g * GT + GT] for k in range(2))
                            w, wl = weights(front, c, slice(QW, QW + 2 * HD))
                            mm = products(kv_ps[0:GT, g, :], ((hi, w), (lo, w), (hi, wl)), c == 0, c == KC - 1)
                    if groups[-1] == GPW - 1:
                        mm.then_inc(raw_done, 1)

                def turn(s):
                    R = GT if s == K else ROWS[TILE_AT[s]]
                    pe.wait_ge(normalised, 4 * f + s + 1)
                    if s < 2 and rear:
                        pe.wait_ge(exp_done, 4 * r + 3 + s)
                    if s >= 2:
                        pe.wait_ge(turned_lo, 4 * f + s - 1)
                    for n in range(REP):
                        mm = pe.transpose(turn_ps[:, s % 2, n * R:n * R + R], normed[0:R, s % 2, n * HD:n * HD + HD],
                                          ident[0:R, 0:R])
                    mm.then_inc(turned, 1)

                def scores(g):
                    if g == 0:
                        pe.wait_ge(turned_lo, 4 * r + 4)
                    if g >= 2:
                        pe.wait_ge(exp_done, 4 * r + g - 1)
                    out = turn_ps[0:GT, g % 2, 0:REP * GT]
                    pe.matmul(out, ident_b[:], mask[:].rearrange("p h t -> p (h t)"), start=True, stop=False)
                    k_hi, k_lo = (k_t[:, k, g * GT:g * GT + GT] for k in range(2))
                    q_hi, q_lo = (q_t[:, k, :, g * GT:g * GT + GT] for k in range(2))
                    products(out, ((k_hi, q_hi), (k_lo, q_hi), (k_hi, q_lo)), False, True).then_inc(scores_done, 1)

                def attended(g):
                    pe.wait_ge(p_lo_done, 4 * r + g + 1)
                    if g == 0:
                        pe.wait_ge(v_lo_done, r + 1)
                    if g or not first_step(rear):
                        pe.wait_ge(o_norm_ready, 4 * r + g)
                    hi, lo = p_hi[:, g % 2, :], p_lo[:, g % 2, :]
                    for n in range(REP):
                        head = slice(n * GT, n * GT + GT)
                        mm = products(den_ps[0:GT, REP * GT + 2 * n:REP * GT + 2 * n + 2],
                                      ((hi[:, head], ones[:]), (lo[:, head], ones[:])), True, True)
                    mm.then_inc(den_done, 1)
                    products(o_ps[:, 0:REP * GT], ((v[:, 0, g, :], hi), (v[:, 0, g, :], lo), (v[:, 1, g, :], hi)),
                             True, True).then_inc(pv_done, 1)

                def spread(g):
                    pe.wait_ge(rden_ready, 4 * r + g + 1)
                    for n in range(REP):
                        mm = pe.transpose(den_ps[:, n * GT:n * GT + GT],
                                          rden_col[:, n:n + 1].broadcast_to([GT, P]), ident[0:GT, 0:GT])
                    mm.then_inc(rden_spread, 1)

                def output(j):
                    R = ROWS[j]
                    if j == 0:
                        pe.wait_ge(o_lo_done, 4 * r + 4)
                    if j < 2 and front:
                        pe.wait_ge(normalised, 4 * f + 3 + j)
                    elif j < 2:
                        pe.wait_ge(h_added, TPW * r)
                    else:
                        pe.wait_ge(h_added, TPW * r + 1)
                    for c in range(REP):
                        hi, lo = (o_t[:, k, c, j * P:j * P + R] for k in range(2))
                        w, wl = weights(rear, c, slice(QW + 2 * HD, WCOLS))
                        mm = products(proj_ps[0:R, (j + 1) % 2, :], ((hi, w), (lo, w), (hi, wl)), c == 0, c == REP - 1)
                    mm.then_inc(out_done, 1)

                if rear:
                    scores(0)
                    scores(1)
                if front:
                    query(0)
                if rear:
                    attended(0)
                    scores(2)
                    spread(0)
                if front:
                    keys_values((0, 1))
                if rear:
                    attended(1)
                    scores(3)
                    spread(1)
                if front:
                    keys_values((2, 3))
                if rear:
                    attended(2)
                    spread(2)
                if front:
                    query(1)
                if rear:
                    attended(3)
                if front:
                    turn(0)
                if rear:
                    spread(3)
                if front:
                    query(2)
                    turn(K)
                if rear:
                    output(0)
                if front:
                    turn(2)
                if rear:
                    output(1)
                if front:
                    turn(3)
                if rear:
                    output(2)
            steps(pe, step)

        @block.vector
        def _(dve):
            for n in range(2 * KC):
                cols = slice(n % 2 * WPART, n % 2 * WPART + WPART)
                dve.wait_ge(w_hi_done, n + 1)
                dve.tensor_tensor(w_lo[:, 0, n // 2, cols], w_raw[:], w_hi[:, 0, n // 2, cols].bitcast(F32),
                                  ALU.subtract).then_inc(w_lo_done, 1)

            def step(front, rear):
                f, r = front and count(front), rear and count(rear)

                def probs_low(g):
                    dve.wait_ge(p_hi_done, 4 * r + g + 1)
                    dve.tensor_tensor(p_lo[:, g % 2, :], e[:, g % 2, :], p_hi[:, g % 2, :].bitcast(F32), ALU.subtract)\
                        .then_inc(p_lo_done, 1)

                def sums(s):
                    R = GT if s == K else ROWS[TILE_AT[s]]
                    dve.wait_ge(squared, 4 * f + s + 1)
                    dve.tensor_reduce(ssq[0:R, s, :], squares[0:R, :].rearrange("p (h d) -> p h d", h=REP), AX.X,
                                      ALU.add).then_inc(summed, 1)
                    dve.wait_ge(summed, 4 * f + s + 1)
                    dve.tensor_scalar(var[0:R, s, :], ssq[0:R, s, :], 1.0 / HD, EPS_QK, ALU.mult, ALU.add)\
                        .then_inc(var_ready, 1)

                def normalise(s):
                    R = GT if s == K else ROWS[TILE_AT[s]]
                    dve.wait_ge(rs_ready, 4 * f + s + 1)
                    if s >= 2 or not first_step(front):
                        dve.wait_ge(turned, 4 * f + s - 1)
                    raw = kv_ps[0:GT, :, 0:HD] if s == K else \
                        proj_ps[0:R, TILE_AT[s] % 2, :].rearrange("p (h d) -> p h d", h=REP)
                    dve.tensor_tensor(normed[0:R, s % 2, :].rearrange("p (h d) -> p h d", h=REP), raw,
                                      rs[0:R, s, :].unsqueeze(2).broadcast_to([R, REP, HD]), ALU.mult)\
                        .then_inc(normalised, 1)

                def values_low():
                    dve.wait_ge(v_hi_done, f + 1)
                    dve.tensor_tensor(v[:, 1], kv_ps[0:GT, :, HD:2 * HD], v[:, 0].bitcast(F32), ALU.subtract)\
                        .then_inc(v_lo_done, 1)

                def reciprocals(g):
                    dve.wait_ge(den_done, 4 * r + g + 1)
                    if g or not first_step(rear):
                        dve.wait_ge(rden_spread, 4 * r + g)
                    dve.reciprocal(rden_col[:], den_ps[0:GT, REP * GT:REP * GT + 2 * REP:2]).then_inc(rden_ready, 1)

                def divide(g):
                    dve.wait_ge(pv_done, 4 * r + g + 1)
                    dve.wait_ge(rden_taken, 4 * r + g + 1)
                    if g or not first_step(rear):
                        dve.wait_ge(o_lo_done, 4 * r + g)
                    dve.tensor_tensor(o_norm[:], o_ps[:, 0:REP * GT], rden[:], ALU.mult).then_inc(o_norm_ready, 1)

                def out_low(g):
                    dve.wait_ge(o_hi_done, 4 * r + g + 1)
                    cols = slice(g * GT, g * GT + GT)
                    dve.tensor_tensor(o_t[:, 1, :, cols], o_norm[:].rearrange("p (h t) -> p h t", h=REP),
                                      o_t[:, 0, :, cols].bitcast(F32), ALU.subtract).then_inc(o_lo_done, 1)

                def turned_low(s):
                    dve.wait_ge(turned_hi, 4 * f + s + 1)
                    if s == K:
                        dve.tensor_tensor(k_t[:, 1, :], turn_ps[:, s % 2, 0:WT], k_t[:, 0, :].bitcast(F32),
                                          ALU.subtract).then_inc(turned_lo, 1)
                    else:
                        j, R = TILE_AT[s], ROWS[TILE_AT[s]]
                        cols = slice(j * P, j * P + R)
                        dve.tensor_tensor(q_t[:, 1, :, cols],
                                          turn_ps[:, s % 2, 0:REP * R].rearrange("p (h t) -> p h t", h=REP),
                                          q_t[:, 0, :, cols].bitcast(F32), ALU.subtract).then_inc(turned_lo, 1)

                def add(j):
                    R = ROWS[j]
                    tile = h_sb[0:R, bass.ds((rear[0] % TURNS_HEAD) * TPU + rear[1] * TPW + j, 1), :]\
                        .rearrange("p a n -> p (a n)")
                    dve.wait_ge(out_done, TPW * r + j + 1)
                    dve.tensor_tensor(tile, proj_ps[0:R, (j + 1) % 2, :], tile, ALU.add).then_inc(h_added, 1)

                if rear:
                    probs_low(0)
                    probs_low(1)
                if front:
                    sums(0)
                if rear:
                    reciprocals(0)
                if front:
                    normalise(0)
                if rear:
                    probs_low(2)
                    divide(0)
                    out_low(0)
                    reciprocals(1)
                    probs_low(3)
                    divide(1)
                    out_low(1)
                if front:
                    sums(K)
                if rear:
                    reciprocals(2)
                if front:
                    normalise(K)
                if rear:
                    divide(2)
                    out_low(2)
                if front:
                    sums(2)
                if rear:
                    reciprocals(3)
                if front:
                    normalise(2)
                if rear:
                    divide(3)
                    out_low(3)
                if front:
                    turned_low(0)
                    values_low()
                    sums(3)
                    normalise(3)
                    turned_low(K)
                if rear:
                    add(0)
                if front:
                    turned_low(2)
                if rear:
                    add(1)
                if front:
                    turned_low(3)
                if rear:
                    add(2)
                if front:
                    into, c, cols = next_part(front)
                    dve.wait_ge(w_hi_done, 2 * KC + f + 1)
                    hi, lo = (w[:, bass.ds(into, 1), bass.ds(c, 1), cols].rearrange("p a b n -> p (a b n)")
                              for w in (w_hi, w_lo))
                    dve.tensor_tensor(lo, w_raw[:], hi.bitcast(F32), ALU.subtract).then_inc(w_lo_done, 1)
            steps(dve, step)


EXPERTS, HID = 8, 448
MC = -(-HID // P)
HCS = [min(P, HID - m * P) for m in range(MC)]


MAIN = HID // P * P
LAST = HID - MAIN
assert 2 * LAST == P
GATE_AT = HID + LAST


PARTS = [(0, "up", slice(0, HID)), (HID, "gate", slice(MAIN, HID)), (GATE_AT, "gate", slice(0, MAIN))]


def products_of(m):
    if m == MC - 1:
        return [slice(MAIN, MAIN + P)]
    return [slice(at + m * P, at + m * P + P) for at in (0, GATE_AT)]


def up_of(ps, m):
    return ps[0:HCS[m], 0, :]


def gate_of(ps, m):
    return ps[LAST:P, 0, :] if m == MC - 1 else ps[:, 1, :]


TILES = WIN * TPW
SLOTS = 256
BLOCKS = (2 * TOK + EXPERTS * (SLOTS - 1)) // SLOTS
LIMITS = -(-TOK // SLOTS)


def route_and_share(nc, gate_w, bias, sw1, sw2, sw3, ident, h_sb, normed_t, rows, table, slots, expert_of):
    with ExitStack() as ctx:
        def sb(name, shape, dt=F32):
            return ctx.enter_context(nc.sbuf_tensor(name, shape, dt))

        def sem(name):
            return ctx.enter_context(nc.semaphore(name))

        gate = sb("gate", [P, KC, EXPERTS])
        gate_hi = sb("gate_hi", [P, KC, EXPERTS], F32R)
        gate_lo = sb("gate_lo", [P, KC, EXPERTS], F32R)
        bias_row = sb("fbias_row", [P, EXPERTS])
        minus_half = sb("fminus_half", [P, 1])
        st = sb("fst", [P, 3, 6])
        mv = sb("fmv", [P, 3, 2])
        ve = sb("fve", [P, 3])
        rstd = sb("frstd", [P, 3])
        turnstile = sb("fturnstile", [P, 1])
        norm = sb("norm", [P, 3, DIM])
        ht = sb("fht", [P, 3, 2, KC, P], F32R)
        grid = [P, TILES, EXPERTS]
        logits = sb("logits", grid)
        scores = sb("scores", grid)
        chosen = [sb(f"chosen{k}", grid) for k in range(2)]
        work = sb("work", grid)
        key = sb("key", grid)
        rank = sb("rank", grid)
        falling = sb("falling", [P, EXPERTS])
        valid = sb("valid", [P, TILES])
        best = sb("best", [P, TILES])
        both = sb("both", grid, BF16)
        below = sb("below", [P, P], BF16)
        ones_b = sb("ones_b", [P, P], BF16)
        per_row = sb("per_row", [P, EXPERTS], BF16)
        counts = sb("counts", [P, EXPERTS])
        limits = sb("limits", [P, LIMITS])
        over = sb("over", [P, EXPERTS, LIMITS])
        blocks = sb("blocks", [P, EXPERTS])
        upto = sb("upto", [P, EXPERTS])
        start = sb("start", [P, EXPERTS])
        block_no = sb("block_no", [P, BLOCKS])
        passed = sb("passed", [P, BLOCKS, EXPERTS])
        expert_f = sb("expert_f", [P, BLOCKS])
        payload = sb("payload", [P, TILES, 2, 2], U32)
        slot_f = sb("slot_f", [P, TILES])
        zero_table = sb("zero_table", [P, BLOCKS * SLOTS // P * 2], U32)
        raw = sb("sraw", [P, KC, 2 * HID])
        raw2 = sb("sraw2", [P, MC, DIM])
        w13_hi = sb("sw13_hi", [P, KC, 2 * HID], F32R)
        w13_lo = sb("sw13_lo", [P, KC, 2 * HID], F32R)
        w2_hi = sb("sw2_hi", [P, MC, DIM], F32R)
        w2_lo = sb("sw2_lo", [P, MC, DIM], F32R)
        xt = sb("sxt", [P, 2, 2, KC, WT], F32R)
        gated = sb("gated", [P, 2, WT])
        hidden = sb("hidden", [P, 2, WT])
        hid_hi = sb("hid_hi", [P, MC, WT], F32R)
        hid_lo = sb("hid_lo", [P, MC, WT], F32R)

        ht_ps = ctx.enter_context(nc.psum_tensor("fht_ps", [P, 2, KC, P], F32))
        gu_ps = ctx.enter_context(nc.psum_tensor("gu_ps", [P, 2, 2, DIM], F32))
        y_ps = ctx.enter_context(nc.psum_tensor("y_ps", [P, 2, DIM], F32))

        consts_in = sem("fconsts_in")
        consts = sem("fconsts")
        valid_steps = sem("valid_steps")
        w_in = sem("sw_in")
        gate_hi_done = sem("gate_hi_done")
        gate_ready = sem("gate_ready")
        w_hi_done = sem("sw_hi_done")
        w_lo_done = sem("sw_lo_done")
        stats_done = sem("fstats_done")
        mv_done = sem("fmv_done")
        var_ready = sem("fvar_ready")
        rstd_ready = sem("frstd_ready")
        norm_ready = sem("fnorm_ready")
        rows_stored = [sem(f"rows_stored{k}") for k in range(3)]
        ht_done = sem("fht_done")
        ht_hi_done = sem("fht_hi_done")
        ht_lo_done = sem("fht_lo_done")
        ht_stored = [sem(f"fht_stored{k}") for k in range(3)]
        gate_done = sem("gate_done")
        logits_ready = sem("logits_ready")
        table_zeroed = sem("table_zeroed")
        routed = sem("routed")
        centred = sem("fcentred")
        exp_done = sem("fexp_done")
        counts_ready = sem("counts_ready")
        ranks_done = sem("ranks_done")
        counts_done = sem("counts_done")
        slots_ready = sem("slots_ready")
        scattered = sem("scattered")
        xt_in = [sem(f"sxt_in{k}") for k in range(2)]
        gu_done = sem("gu_done")
        silu_done = sem("silu_done")
        hidden_ready = sem("hidden_ready")
        hid_hi_done = sem("hid_hi_done")
        hid_lo_done = sem("hid_lo_done")
        y_done = sem("y_done")
        h_added = sem("fh_added")

        NORM, LOW, LOGITS = 1, 2, 3
        block = ctx.enter_context(nc.Block())

        @block.sync
        def _(sp):
            sp.dma_start(gate[:], gate_w.rearrange("(c p) e -> p c e", p=P)).then_inc(consts_in, 16)
            sp.dma_start(bias_row[:], bias.partition_broadcast(P)).then_inc(consts_in, 16)
            for at, w, cols in PARTS:
                sp.dma_start(raw[:, :, at:at + cols.stop - cols.start],
                             {"up": sw3, "gate": sw1}[w][:, cols].rearrange("(c p) n -> p c n", p=P)).then_inc(w_in, 16)
            whole = HID // P
            sp.dma_start(raw2[:, 0:whole, :], sw2[0:whole * P, :].rearrange("(c p) n -> p c n", p=P)).then_inc(w_in, 16)
            sp.dma_start(raw2[0:HCS[-1], MC - 1, :], sw2[whole * P:HID, :]).then_inc(w_in, 16)

            def store_rows(at):
                (u, i), j, R = at, at[1] % TPW, rows_of(at[1])
                sp.wait_ge(norm_ready, number(at) + 1)
                sp.dma_start(rows[bass.ds((u * 2 + i // TPW) * WT + P * j, R), :], norm[0:R, i % 3, :])\
                    .then_inc(rows_stored[i % 3], 16)

            def store_turned(at):
                (u, i), j, R = at, at[1] % TPW, rows_of(at[1])
                sp.wait_ge(ht_lo_done, number(at) + 1)
                sp.dma_start(normed_t[u * 2 + i // TPW, :, :, :, P * j:P * j + R],
                             ht[:, i % 3, :, :, 0:R].bitcast(F32)).then_inc(ht_stored[i % 3], 16)

            def step(u, i):
                if at := back(u, i, NORM):
                    store_rows(at)
                if at := back(u, i, LOW):
                    store_turned(at)
            tile_steps(sp, LOW, step)
            for k in range(3):
                sp.wait_ge(rows_stored[k], 16 * TILES // 3)
                sp.wait_ge(ht_stored[k], 16 * TILES // 3)

            def load(u, i):
                if not (isinstance(u, int) and u == 0):
                    sp.wait_ge(gu_done, MC * ((u - 1) * 2 + i + 1))
                sp.dma_start(xt[:, i].bitcast(F32), normed_t[bass.ds(u * 2 + i, 1)]
                             .rearrange("a p s c t -> (a p) s c t")).then_inc(xt_in[i], 16)
            run_steps(sp, WIN // 2, 2, 0, load)

        @block.gpsimd
        def _(pool):
            pool.memset(zero_table[:], 0).then_inc(consts, 1)
            pool.memset(minus_half[:], -0.5).then_inc(consts, 1)
            pool.memset(logits[:], 0.0).then_inc(consts, 1)
            pool.memset(ones_b[:], 1.0).then_inc(consts, 1)
            pool.memset(below[:], 1.0).then_inc(consts, 1)
            pool.memset(valid[:], 1.0).then_inc(consts, 1)
            for n in range(EXPERTS):
                pool.memset(falling[:, n:n + 1], float(EXPERTS - n)).then_inc(consts, 1)
            for n in range(LIMITS):
                pool.memset(limits[:, n:n + 1], float(n * SLOTS)).then_inc(consts, 1)
            for n in range(BLOCKS):
                pool.memset(block_no[:, n:n + 1], float(n)).then_inc(consts, 1)
            made = 6 + EXPERTS + LIMITS + BLOCKS
            pool.wait_ge(consts, made)
            pool.dma_start(table.rearrange("(p n) w -> p (n w)", p=P), zero_table[:]).then_inc(table_zeroed, 16)
            pool.affine_select(out=below[:], in_=below[:], compare_op=ALU.is_gt, fill=0.0, base=0, pattern=[[1, P]],
                               channel_multiplier=-1).then_inc(consts, 1)
            last = valid[:].rearrange("p (w j) -> p w j", j=TPW)[:, :, TPW - 1]
            pool.affine_select(out=last, in_=last, compare_op=ALU.is_gt, fill=0.0, base=ROWS[-1], pattern=[[0, WIN]],
                               channel_multiplier=-1).then_inc(consts, 1)
            for k in range(2):
                for j in range(TPW):
                    pool.iota(payload[:].rearrange("p (w j) k n -> p j k n w", j=TPW)[:, j, k, 0, :],
                              pattern=[[WT, WIN]], base=P * j, channel_multiplier=1).then_inc(consts, 1)

            def step(u, i):
                at = back(u, i, 0)
                if at:
                    k, R = at[1] % 3, rows_of(at[1])
                    pool.wait_ge(var_ready, number(at) + 1)
                    pool.tensor_tensor(rstd[0:R, k:k + 1], ve[0:R, k:k + 1], minus_half[0:R, :], ALU.pow)\
                        .then_inc(rstd_ready, 1)
            tile_steps(pool, 0, step)

            pool.wait_ge(table_zeroed, 16)
            pool.wait_ge(slots_ready, 4)
            for n in range(TILES):
                R = ROWS[n % TPW]
                for k in range(2):
                    pool.indirect_dma_start(out=table[:, :],
                                            out_offset=bass.IndirectOffsetOnAxis(ap=slots[0:R, k, n:n + 1], axis=0),
                                            in_=payload[0:R, n, k, :], in_offset=None).then_inc(scattered, 16)
            pool.wait_ge(scattered, 16 * 2 * TILES)

        @block.scalar
        def _(act):
            act.wait_ge(consts_in, 32)
            act.copy(gate_hi[:], gate[:]).then_inc(gate_hi_done, 1)

            def high(at):
                i, R = at[1], rows_of(at[1])
                act.wait_ge(ht_done, number(at) + 1)
                if not first(at, 3):
                    act.wait_ge(ht_stored[i % 3], 16 * (at[0] * 2 + i // 3))
                    act.wait_ge(gate_done, number(at) - 2)
                act.copy(ht[:, i % 3, 0, :, 0:R], ht_ps[:, i % 2, :, 0:R]).then_inc(ht_hi_done, 1)

            def step(u, i):
                if at := back(u, i, NORM):
                    high(at)
            tile_steps(act, NORM, step)

            act.wait_ge(w_in, 16 * 5)
            act.copy(w13_hi[:], raw[:]).then_inc(w_hi_done, 1)
            for c in range(MC):
                act.copy(w2_hi[0:HCS[c], c, :], raw2[0:HCS[c], c, :]).then_inc(w_hi_done, 1)
            act.wait_ge(centred, 1)
            act.activation(scores[:], work[:], ACT.Exp).then_inc(exp_done, 1)

            def window(u, i):
                n = u * 2 + i
                for m in range(MC):
                    known = isinstance(u, int)
                    act.wait_ge(gu_done, MC * n + m + 1)
                    if not (known and MC * n + m < 2):
                        act.wait_ge(hidden_ready, MC * n + m - 1)
                    act.activation(gated[0:HCS[m], m % 2, :], gate_of(gu_ps[:, m % 2, :, 0:WT], m), ACT.Silu).then_inc(silu_done, 1)
                    act.wait_ge(hidden_ready, MC * n + m + 1)
                    if m == 0 and not (known and n == 0):
                        act.wait_ge(y_done, TPW * n)
                    act.copy(hid_hi[0:HCS[m], m, :], hidden[0:HCS[m], m % 2, :]).then_inc(hid_hi_done, 1)
            run_steps(act, WIN // 2, 2, 0, window)

        @block.tensor
        def _(pe):
            pe.wait_ge(gate_ready, 1)

            def turn(at):
                i, R = at[1], rows_of(at[1])
                pe.wait_ge(norm_ready, number(at) + 1)
                if not first(at, 2):
                    pe.wait_ge(ht_lo_done, number(at) - 1)
                for c in range(KC):
                    mm = pe.transpose(ht_ps[:, i % 2, c, 0:R], norm[0:R, i % 3, c * P:c * P + P], ident[0:R, 0:R])
                mm.then_inc(ht_done, 1)

            def gates(at):
                i, R = at[1], rows_of(at[1])
                pe.wait_ge(ht_lo_done, number(at) + 1)
                if not first(at, 2):
                    pe.wait_ge(logits_ready, number(at) - 1)
                for c in range(KC):
                    hi, lo = (ht[:, i % 3, k, c, 0:R] for k in range(2))
                    for n, (lhs, rhs) in enumerate(((hi, gate_hi), (lo, gate_hi), (hi, gate_lo))):
                        mm = pe.matmul(y_ps[0:R, i % 2, 0:EXPERTS], lhs, rhs[:, c, :], start=c == 0 and n == 0,
                                       stop=c == KC - 1 and n == 2)
                mm.then_inc(gate_done, 1)

            def step(u, i):
                if at := back(u, i, NORM):
                    turn(at)
                if at := back(u, i, LOW):
                    gates(at)
            tile_steps(pe, LOW, step)

            pe.wait_ge(consts, 8 + EXPERTS + LIMITS + BLOCKS)
            pe.wait_ge(counts_ready, 2)
            ranks = gu_ps[:, 0, 0, 0:TILES * EXPERTS].rearrange("p (t e) -> p t e", e=EXPERTS)
            pe.matmul(ranks, below[:], both[:], start=True, stop=False)
            for t in range(TILES - 1):
                after = TILES - 1 - t
                mm = pe.matmul(ranks[:, t + 1:TILES, :], ones_b[:],
                               both[:, t, :].unsqueeze(1).broadcast_to([P, after, EXPERTS]), start=False,
                               stop=t == TILES - 2)
            mm.then_inc(ranks_done, 1)
            pe.matmul(gu_ps[:, 0, 1, 0:EXPERTS], ones_b[:], per_row[:], start=True, stop=True).then_inc(counts_done, 1)

            def window(u, i):
                n, known = u * 2 + i, isinstance(u, int)
                pe.wait_ge(xt_in[i], 16 * (u + 1))
                if known and n == 0:
                    pe.wait_ge(w_lo_done, 1 + MC)
                    pe.wait_ge(slots_ready, 4)
                for m in range(MC):
                    if not (known and MC * n + m < 2):
                        pe.wait_ge(hidden_ready, MC * n + m - 1)
                    for k, cols in enumerate(products_of(m)):
                        for c in range(KC):
                            x_hi, x_lo = (xt[:, i, s, c, :] for s in range(2))
                            w, wl = w13_hi[:, c, cols], w13_lo[:, c, cols]
                            for q, (lhs, rhs) in enumerate(((w, x_hi), (wl, x_hi), (w, x_lo))):
                                mm = pe.matmul(gu_ps[:, m % 2, k, 0:WT], lhs, rhs, start=c == 0 and q == 0,
                                               stop=c == KC - 1 and q == 2)
                    mm.then_inc(gu_done, 1)
                for j in range(TPW):
                    R = ROWS[j]
                    slot = (TPW * i + j) % 2
                    if not (known and TPW * n + j < 2):
                        pe.wait_ge(h_added, TPW * n + j - 1)
                    for c in range(MC):
                        if j == 0:
                            pe.wait_ge(hid_lo_done, MC * n + c + 1)
                        tok = slice(j * P, j * P + R)
                        h, hl = hid_hi[0:HCS[c], c, tok], hid_lo[0:HCS[c], c, tok]
                        for q, (lhs, rhs) in enumerate(((h, w2_hi), (hl, w2_hi), (h, w2_lo))):
                            mm = pe.matmul(y_ps[0:R, slot, :], lhs, rhs[0:HCS[c], c, :], start=c == 0 and q == 0,
                                           stop=c == MC - 1 and q == 2)
                    mm.then_inc(y_done, 1)
            run_steps(pe, WIN // 2, 2, 0, window)

        @block.vector
        def _(dve):
            dve.wait_ge(gate_hi_done, 1)
            dve.tensor_tensor(gate_lo[:], gate[:], gate_hi[:].bitcast(F32), ALU.subtract).then_inc(gate_ready, 1)
            dve.wait_ge(consts, 6)

            def step(u, i):
                if at := back(u, i, 0):
                    k, R = at[1] % 3, rows_of(at[1])
                    h = h_sb[0:R, bass.ds(number(at), 1), :].rearrange("p a n -> p (a n)")
                    dve.bn_stats(st[0:R, k, :], h).then_inc(stats_done, 1)
                    dve.wait_ge(stats_done, number(at) + 1)
                    dve.memset(turnstile[:], 0.0)
                    dve.bn_aggr(mv[0:R, k, :], st[0:R, k, :]).then_inc(mv_done, 1)
                    dve.wait_ge(mv_done, number(at) + 1)
                    dve.tensor_scalar(ve[0:R, k:k + 1], mv[0:R, k, 1:2], EPS_LN, None, ALU.add).then_inc(var_ready, 1)
                if at := back(u, i, NORM):
                    k, R = at[1] % 3, rows_of(at[1])
                    h = h_sb[0:R, bass.ds(number(at), 1), :].rearrange("p a n -> p (a n)")
                    if not first(at, 3):
                        dve.wait_ge(rows_stored[k], 16 * (at[0] * 2 + at[1] // 3))
                        dve.wait_ge(ht_done, number(at) - 2)
                    dve.wait_ge(rstd_ready, number(at) + 1)
                    dve.tensor_scalar(norm[0:R, k, :], h, mv[0:R, k, 0:1], rstd[0:R, k:k + 1], ALU.subtract,
                                      ALU.mult).then_inc(norm_ready, 1)
                if at := back(u, i, LOW):
                    k, R = at[1], rows_of(at[1])
                    dve.wait_ge(ht_hi_done, number(at) + 1)
                    dve.tensor_tensor(ht[:, k % 3, 1, :, 0:R], ht_ps[:, k % 2, :, 0:R],
                                      ht[:, k % 3, 0, :, 0:R].bitcast(F32), ALU.subtract).then_inc(ht_lo_done, 1)
                if at := back(u, i, LOGITS):
                    k, R = at[1], rows_of(at[1])
                    dve.wait_ge(gate_done, number(at) + 1)
                    dve.tensor_copy(logits[0:R, bass.ds(number(at), 1), :].rearrange("p a e -> p (a e)"),
                                    y_ps[0:R, k % 2, 0:EXPERTS]).then_inc(logits_ready, 1)
            tile_steps(dve, LOGITS, step)

            dve.wait_ge(logits_ready, TILES)
            dve.wait_ge(consts_in, 32)
            dve.wait_ge(consts, 14 + EXPERTS + LIMITS + BLOCKS)
            done = 0

            def over_experts(a):
                return a.unsqueeze(2).broadcast_to(grid)

            def over_tiles(a):
                return a.unsqueeze(1).broadcast_to(grid)

            def then(instruction):
                nonlocal done
                done += 1
                instruction.then_inc(routed, 1)
                dve.wait_ge(routed, done)

            then(dve.tensor_reduce(best[:], logits[:], AX.X, ALU.max))
            dve.tensor_tensor(work[:], logits[:], over_experts(best[:]), ALU.subtract).then_inc(centred, 1)
            dve.wait_ge(exp_done, 1)
            then(dve.tensor_reduce(best[:], scores[:], AX.X, ALU.add))
            then(dve.reciprocal(slot_f[:], best[:]))
            then(dve.tensor_tensor(scores[:], scores[:], over_experts(slot_f[:]), ALU.mult))
            then(dve.tensor_tensor(work[:], scores[:], over_tiles(bias_row[:]), ALU.add))
            for k in range(2):
                then(dve.tensor_reduce(best[:], work[:], AX.X, ALU.max))
                then(dve.tensor_tensor(key[:], work[:], over_experts(best[:]), ALU.is_equal))
                then(dve.tensor_tensor(key[:], key[:], over_tiles(falling[:]), ALU.mult))
                then(dve.tensor_reduce(best[:], key[:], AX.X, ALU.max))
                then(dve.tensor_tensor(chosen[k][:], key[:], over_experts(best[:]), ALU.is_equal))
                if k == 0:
                    then(dve.scalar_tensor_tensor(work[:], chosen[0][:], -3e38, work[:], ALU.mult, ALU.add))
                then(dve.tensor_tensor(chosen[k][:], chosen[k][:], over_experts(valid[:]), ALU.mult))
            then(dve.tensor_tensor(key[:], chosen[0][:], chosen[1][:], ALU.add))
            dve.tensor_copy(both[:], key[:]).then_inc(counts_ready, 1)
            then(dve.tensor_reduce(counts[:], key[:].rearrange("p t e -> p e t"), AX.X, ALU.add))
            dve.tensor_copy(per_row[:], counts[:]).then_inc(counts_ready, 1)
            for k in range(2):
                then(dve.tensor_tensor(work[:], chosen[k][:], scores[:], ALU.mult))
                then(dve.tensor_reduce(payload[:, :, k, 1].bitcast(F32), work[:], AX.X, ALU.add))
            dve.wait_ge(ranks_done, 1)
            dve.wait_ge(counts_done, 1)
            then(dve.tensor_copy(counts[:], gu_ps[:, 0, 1, 0:EXPERTS]))
            wide = [P, EXPERTS, LIMITS]
            then(dve.tensor_tensor(over[:], counts[:].unsqueeze(2).broadcast_to(wide),
                                   limits[:].unsqueeze(1).broadcast_to(wide), ALU.is_gt))
            then(dve.tensor_reduce(blocks[:], over[:], AX.X, ALU.add))
            then(dve.tensor_copy(upto[:], blocks[:]))
            for n in range(1, EXPERTS):
                then(dve.tensor_tensor(upto[:, n:n + 1], upto[:, n - 1:n], blocks[:, n:n + 1], ALU.add))
            then(dve.tensor_tensor(start[:], upto[:], blocks[:], ALU.subtract))
            then(dve.tensor_scalar(start[:], start[:], float(SLOTS), None, ALU.mult))
            then(dve.tensor_tensor(rank[:], gu_ps[:, 0, 0, 0:TILES * EXPERTS].rearrange("p (t e) -> p t e", e=EXPERTS),
                                   over_tiles(start[:]), ALU.add))
            for k in range(2):
                then(dve.tensor_tensor(work[:], chosen[k][:], rank[:], ALU.mult))
                then(dve.tensor_reduce(slot_f[:], work[:], AX.X, ALU.add))
                dve.tensor_copy(slots[:, k, :], slot_f[:]).then_inc(slots_ready, 1)
                dve.wait_ge(slots_ready, k + 1)
            wide = [P, BLOCKS, EXPERTS]
            then(dve.tensor_tensor(passed[:], block_no[:].unsqueeze(2).broadcast_to(wide),
                                   upto[:].unsqueeze(1).broadcast_to(wide), ALU.is_ge))
            then(dve.tensor_reduce(expert_f[:], passed[:], AX.X, ALU.add))
            dve.tensor_scalar(expert_of[:], expert_f[0:1, :], float(EXPERTS - 1), None, ALU.min).then_inc(slots_ready, 1)
            dve.tensor_scalar(turnstile[:], turnstile[:], 1.0, None, ALU.mult).then_inc(slots_ready, 1)

            dve.wait_ge(w_hi_done, 1 + MC)
            dve.tensor_tensor(w13_lo[:], raw[:], w13_hi[:].bitcast(F32), ALU.subtract).then_inc(w_lo_done, 1)
            for c in range(MC):
                dve.tensor_tensor(w2_lo[0:HCS[c], c, :], raw2[0:HCS[c], c, :], w2_hi[0:HCS[c], c, :].bitcast(F32),
                                  ALU.subtract).then_inc(w_lo_done, 1)

            def window(u, i):
                n, known = u * 2 + i, isinstance(u, int)

                def low(m):
                    dve.wait_ge(hid_hi_done, MC * n + m + 1)
                    dve.tensor_tensor(hid_lo[0:HCS[m], m, :], hidden[0:HCS[m], m % 2, :],
                                      hid_hi[0:HCS[m], m, :].bitcast(F32), ALU.subtract)\
                        .then_inc(hid_lo_done, 1)

                for m in range(MC):
                    dve.wait_ge(silu_done, MC * n + m + 1)
                    dve.tensor_tensor(hidden[0:HCS[m], m % 2, :], up_of(gu_ps[:, m % 2, :, 0:WT], m),
                                      gated[0:HCS[m], m % 2, :], ALU.mult)\
                        .then_inc(hidden_ready, 1)
                    low(m)
                for j in range(TPW):
                    R = ROWS[j]
                    tile = h_sb[0:R, bass.ds(n * TPW + j, 1), :].rearrange("p a n -> p (a n)")
                    dve.wait_ge(y_done, TPW * n + j + 1)
                    dve.tensor_tensor(tile, y_ps[0:R, (TPW * i + j) % 2, :], tile, ALU.add).then_inc(h_added, 1)
            run_steps(dve, WIN // 2, 2, 0, window)


def run_experts(nc, w1, w2, w3, ident, rows, table, expert_of, routed_out):
    with ExitStack() as ctx:
        def sb(name, shape, dt=F32):
            return ctx.enter_context(nc.sbuf_tensor(name, shape, dt))

        def sem(name):
            return ctx.enter_context(nc.semaphore(name))

        HALVES = SLOTS // P
        w13 = {"up": w3, "gate": w1}
        raw = sb("eraw", [P, KC, 2 * HID])
        raw2 = sb("eraw2", [P, MC, DIM])
        w13_hi = sb("ew13_hi", [P, 2, KC, 2 * HID], F32R)
        w13_lo = sb("ew13_lo", [P, 2, KC, 2 * HID], F32R)
        w2_hi = sb("ew2_hi", [P, 2, MC, DIM], F32R)
        w2_lo = sb("ew2_lo", [P, 2, MC, DIM], F32R)
        entry = sb("entry", [P, 2, HALVES, 2], U32)
        gathered = sb("gathered", [P, 2, HALVES, DIM])
        xt_hi = sb("ext_hi", [P, 2, KC, SLOTS], F32R)
        xt_lo = sb("ext_lo", [P, 2, KC, SLOTS], F32R)
        gated = sb("egated", [P, 2, SLOTS])
        hidden = sb("ehidden", [P, 2, SLOTS])
        hid_hi = sb("ehid_hi", [P, MC, SLOTS], F32R)
        hid_lo = sb("ehid_lo", [P, MC, SLOTS], F32R)
        y = sb("y", [P, HALVES, DIM])
        turnstile = sb("eturnstile", [P, 2])
        xt_ps = ctx.enter_context(nc.psum_tensor("ext_ps", [P, HALVES, KC, P], F32))
        gu_ps = ctx.enter_context(nc.psum_tensor("egu_ps", [P, MC, 2, SLOTS], F32))
        y_ps = ctx.enter_context(nc.psum_tensor("ey_ps", [P, HALVES, DIM], F32))

        w_in = [sem(f"ew_in{c}") for c in range(KC)]
        w_hi_done = sem("ew_hi_done")
        w_lo_done = sem("ew_lo_done")
        entry_in = sem("entry_in")
        turnstile_set = sem("turnstile_set")
        gathered_in = [sem(f"gathered_in{k}") for k in range(2)]
        scaled = sem("scaled")
        turned = sem("eturned")
        turned_hi = sem("eturned_hi")
        turned_lo = sem("eturned_lo")
        gu_done = sem("egu_done")
        silu_done = sem("esilu_done")
        hidden_ready = sem("ehidden_ready")
        hid_hi_done = sem("ehid_hi_done")
        hid_lo_done = sem("ehid_lo_done")
        down_done = sem("edown_done")
        y_done = sem("ey_done")
        y_taken = sem("y_taken")
        y_stored = [sem(f"y_stored{k}") for k in range(HALVES)]

        BTURNS = BLOCKS // 2
        assert BLOCKS % 2 == 0

        def steps(eng, step):
            def three(u, i):
                step(*(earlier(u, i, n, BTURNS, 2) for n in range(3)))
            run_steps(eng, BTURNS, 2, 2, three, peeled=2)

        def count(at):
            return at[0] * 2 + at[1]

        def is_first(at, n=1):
            return isinstance(at[0], int) and count(at) < n

        block = ctx.enter_context(nc.Block())

        @block.sync
        def _(sp):
            def step(after, front, rear):
                if after:
                    f = count(after)
                    e = sp.value_load(expert_of[0:1, bass.ds(f, 1)], min_val=0, max_val=EXPERTS - 1)
                    for c in range(KC):
                        if not is_first(after):
                            sp.wait_ge(w_lo_done, KC * (f - 1) + c + 1)
                        for at, w, cols in PARTS:
                            sp.dma_start(raw[:, c, at:at + cols.stop - cols.start],
                                         w13[w][bass.ds(e, 1), c * P:c * P + P, cols]
                                         .rearrange("a p n -> (a p) n")).then_inc(w_in[c], 16)
                        sp.dma_start(raw2[0:HCS[c], c, :], w2[bass.ds(e, 1), c * P:c * P + HCS[c], :]
                                     .rearrange("a p n -> (a p) n")).then_inc(w_in[c], 16)
            steps(sp, step)

        @block.gpsimd
        def _(pool):
            pool.memset(turnstile[:], 0.0).then_inc(turnstile_set, 1)
            pool.wait_ge(turnstile_set, 1)

            def step(after, front, rear):
                if front:
                    (u, i), f = front, count(front)
                    if not is_first(front, 2):
                        pool.wait_ge(turned, HALVES * (f - 1))
                    pool.dma_start(entry[:, i], table[bass.ds(f * SLOTS, SLOTS), :]
                                   .rearrange("(h p) w -> p h w", p=P)).then_inc(entry_in, 16)
                    pool.wait_ge(entry_in, 16 * (f + 1))
                    if not is_first(front):
                        pool.wait_ge(turnstile_set, f + 1)
                    pool.tensor_tensor(turnstile[:, 0:1], turnstile[:, 1:2], turnstile[:, 1:2], ALU.mult)\
                        .then_inc(turnstile_set, 1)
                    for half in range(HALVES):
                        pool.indirect_dma_start(out=gathered[:, i, half, :], out_offset=None, in_=rows[:, :],
                                                in_offset=bass.IndirectOffsetOnAxis(ap=entry[:, i, half, 0:1], axis=0))\
                            .then_inc(gathered_in[i], 16)
            steps(pool, step)

        @block.scalar
        def _(act):
            def step(after, front, rear):
                f, r = front and count(front), rear and count(rear)

                def weights(at, c):
                    i, n = at[1], count(at)
                    act.wait_ge(w_in[c], 64 * (n + 1))
                    if c == 0 and not is_first(at, 2):
                        act.wait_ge(gu_done, MC * (n - 1))
                    act.copy(w13_hi[:, i, c], raw[:, c]).then_inc(w_hi_done, 1)
                    if c == 0 and not is_first(at, 2):
                        act.wait_ge(down_done, (MC - 1) * (n - 2) + 1)
                    if c == 1 and not is_first(at, 2):
                        act.wait_ge(y_done, HALVES * (n - 1))
                    act.copy(w2_hi[0:HCS[c], i, c, :], raw2[0:HCS[c], c, :]).then_inc(w_hi_done, 1)

                def rows_high(half):
                    act.wait_ge(turned, HALVES * f + half + 1)
                    act.copy(xt_hi[:, front[1], :, half * P:half * P + P], xt_ps[:, half]).then_inc(turned_hi, 1)

                def silu(m):
                    act.wait_ge(gu_done, MC * r + m + 1)
                    if m >= 2 or not is_first(rear):
                        act.wait_ge(hidden_ready, MC * r + m - 1)
                    act.activation(gated[0:HCS[m], m % 2, :], gate_of(gu_ps[:, m], m), ACT.Silu).then_inc(silu_done, 1)

                def hidden_high(m):
                    act.wait_ge(hidden_ready, MC * r + m + 1)
                    if m == 0 and not is_first(rear):
                        act.wait_ge(y_done, HALVES * r)
                    act.copy(hid_hi[0:HCS[m], m, :], hidden[0:HCS[m], m % 2, :]).then_inc(hid_hi_done, 1)

                def take(half):
                    act.wait_ge(y_done, HALVES * r + half + 1)
                    if not is_first(rear):
                        act.wait_ge(y_stored[half], 16 * r)
                    act.copy(y[:, half, :], y_ps[:, half, :]).then_inc(y_taken, 1)

                def store(half):
                    act.wait_ge(y_taken, HALVES * r + half + 1)
                    act.dma_start(routed_out[bass.ds(r * SLOTS + half * P, P), :], y[:, half, :])\
                        .then_inc(y_stored[half], 16)

                for m in range(MC):
                    if rear:
                        silu(m)
                    if front and m + 1 < MC:
                        weights(front, m + 1)
                    if rear:
                        hidden_high(m)
                if front:
                    for half in range(HALVES):
                        rows_high(half)
                if after:
                    weights(after, 0)
                if rear:
                    for half in range(HALVES):
                        take(half)
                        store(half)
            steps(act, step)
            for stored in y_stored:
                act.wait_ge(stored, 16 * BLOCKS)

        @block.tensor
        def _(pe):
            def step(after, front, rear):
                f, r = front and count(front), rear and count(rear)

                def gate_and_up(m):
                    i = rear[1]
                    if m == 0:
                        pe.wait_ge(turned_lo, HALVES * (r + 1))
                    if not is_first(rear):
                        pe.wait_ge(hidden_ready, MC * (r - 1) + m + 1)
                    for k, cols in enumerate(products_of(m)):
                        for c in range(KC):
                            if m == 0 and k == 0:
                                pe.wait_ge(w_lo_done, KC * r + c + 1)
                            w, wl = w13_hi[:, i, c, cols], w13_lo[:, i, c, cols]
                            for q, (lhs, rhs) in enumerate(((w, xt_hi), (wl, xt_hi), (w, xt_lo))):
                                mm = pe.matmul(gu_ps[:, m, k, :], lhs, rhs[:, i, c, :], start=c == 0 and q == 0,
                                               stop=c == KC - 1 and q == 2)
                    mm.then_inc(gu_done, 1)

                def turn(half):
                    i = front[1]
                    pe.wait_ge(scaled, HALVES * f + half + 1)
                    if rear:
                        pe.wait_ge(turned_lo, HALVES * (f - 1) + half + 1)
                    for c in range(KC):
                        mm = pe.transpose(xt_ps[:, half, c, :], gathered[:, i, half, c * P:c * P + P], ident[:])
                    mm.then_inc(turned, 1)

                def down(c):
                    i = rear[1]
                    if c == 0 and not is_first(rear):
                        pe.wait_ge(y_taken, HALVES * r)
                    pe.wait_ge(hid_lo_done, MC * r + c + 1)
                    for half in range(HALVES):
                        tok = slice(half * P, half * P + P)
                        h, hl = hid_hi[0:HCS[c], c, tok], hid_lo[0:HCS[c], c, tok]
                        for q, (lhs, rhs) in enumerate(((h, w2_hi), (hl, w2_hi), (h, w2_lo))):
                            mm = pe.matmul(y_ps[:, half, :], lhs, rhs[0:HCS[c], i, c, :], start=c == 0 and q == 0,
                                           stop=c == MC - 1 and q == 2)
                        if c == MC - 1:
                            mm.then_inc(y_done, 1)
                    if c < MC - 1:
                        mm.then_inc(down_done, 1)

                for m in range(MC):
                    if rear:
                        gate_and_up(m)
                if front:
                    for half in range(HALVES):
                        turn(half)
                if rear:
                    for c in range(MC):
                        down(c)
            steps(pe, step)

        @block.vector
        def _(dve):
            def step(after, front, rear):
                f, r = front and count(front), rear and count(rear)

                def weights(at, c):
                    i = at[1]
                    dve.wait_ge(w_hi_done, 2 * (KC * count(at) + c + 1))
                    dve.tensor_tensor(w13_lo[:, i, c], raw[:, c], w13_hi[:, i, c].bitcast(F32), ALU.subtract)
                    dve.tensor_tensor(w2_lo[0:HCS[c], i, c, :], raw2[0:HCS[c], c, :],
                                      w2_hi[0:HCS[c], i, c, :].bitcast(F32), ALU.subtract)\
                        .then_inc(w_lo_done, 1)

                def scale(half):
                    i = front[1]
                    if half == 0:
                        dve.wait_ge(gathered_in[i], 16 * HALVES * (front[0] + 1))
                    x = gathered[:, i, half, :]
                    dve.tensor_scalar(x, x, entry[:, i, half, 1:2].bitcast(F32), None, ALU.mult).then_inc(scaled, 1)

                def rows_low(half):
                    dve.wait_ge(turned_hi, HALVES * f + half + 1)
                    i, cols = front[1], slice(half * P, half * P + P)
                    dve.tensor_tensor(xt_lo[:, i, :, cols], xt_ps[:, half], xt_hi[:, i, :, cols].bitcast(F32),
                                      ALU.subtract).then_inc(turned_lo, 1)

                def multiply(m):
                    dve.wait_ge(silu_done, MC * r + m + 1)
                    dve.tensor_tensor(hidden[0:HCS[m], m % 2, :], up_of(gu_ps[:, m], m), gated[0:HCS[m], m % 2, :], ALU.mult)\
                        .then_inc(hidden_ready, 1)

                def hidden_low(m):
                    dve.wait_ge(hid_hi_done, MC * r + m + 1)
                    dve.tensor_tensor(hid_lo[0:HCS[m], m, :], hidden[0:HCS[m], m % 2, :],
                                      hid_hi[0:HCS[m], m, :].bitcast(F32), ALU.subtract).then_inc(hid_lo_done, 1)

                for m in range(MC):
                    if rear:
                        multiply(m)
                    if front and m + 1 < MC:
                        weights(front, m + 1)
                    if front and m == 1:
                        for half in range(HALVES):
                            scale(half)
                    if rear:
                        hidden_low(m)
                if front:
                    for half in range(HALVES):
                        rows_low(half)
                if after:
                    weights(after, 0)
            steps(dve, step)


def combine(nc, h_sb, slots, routed_out, out):
    RING = 6
    flat = out.rearrange("b p d -> (b p) d")
    with ExitStack() as ctx:
        picked = ctx.enter_context(nc.sbuf_tensor("picked", [P, RING, 2, DIM], F32))
        picked_in = [ctx.enter_context(nc.semaphore(f"picked_in{k}")) for k in range(RING)]
        added = ctx.enter_context(nc.semaphore("added"))
        stored = ctx.enter_context(nc.semaphore("out_stored"))
        block = ctx.enter_context(nc.Block())

        @block.gpsimd
        def _(pool):
            for n in range(TILES):
                R = ROWS[n % TPW]
                if n >= RING:
                    pool.wait_ge(added, 2 * (n - RING + 1))
                for k in range(2):
                    pool.indirect_dma_start(out=picked[0:R, n % RING, k, :], out_offset=None, in_=routed_out[:, :],
                                            in_offset=bass.IndirectOffsetOnAxis(ap=slots[0:R, k, n:n + 1], axis=0))\
                        .then_inc(picked_in[n % RING], 16)

        @block.vector
        def _(dve):
            for n in range(TILES):
                R = ROWS[n % TPW]
                dve.wait_ge(picked_in[n % RING], 32 * (n // RING + 1))
                for k in range(2):
                    if k:
                        dve.wait_ge(added, 2 * n + 1)
                    dve.tensor_tensor(h_sb[0:R, n, :], h_sb[0:R, n, :], picked[0:R, n % RING, k, :], ALU.add)\
                        .then_inc(added, 1)

        @block.sync
        def _(sp):
            for n in range(TILES):
                w, j = divmod(n, TPW)
                sp.wait_ge(added, 2 * n + 2)
                sp.dma_start(flat[w * WT + P * j:w * WT + P * j + ROWS[j], :], h_sb[0:ROWS[j], n, :])\
                    .then_inc(stored, 16)
            sp.wait_ge(stored, 16 * TILES)


def build(nc, x, W, b, g1, b1, g2, b2, Wq, Wk, Wv, Wo, gate_w, w1, w2, w3, sw1, sw2, sw3, bias, out):
    normed_t = nc.dram_tensor("normed_t", (WIN, P, 2, KC, WT), F32).ap()
    rows = nc.dram_tensor("rows", (TOK, DIM), F32).ap()
    table = nc.dram_tensor("table", (BLOCKS * SLOTS, 2), U32).ap()
    routed_out = nc.dram_tensor("routed_out", (BLOCKS * SLOTS, DIM), F32).ap()
    with ExitStack() as ctx:
        ident = ctx.enter_context(nc.sbuf_tensor("ident", [P, P], F32))
        h_sb = ctx.enter_context(nc.sbuf_tensor("h_sb", [P, WIN * TPW, DIM], F32))
        constants(nc, ident)
        tokenise(nc, x, W, b, g1, b1, g2, b2, ident, h_sb, normed_t)
        attend(nc, Wq, Wk, Wv, Wo, ident, h_sb, normed_t)
        slots = ctx.enter_context(nc.sbuf_tensor("slots", [P, 2, TILES], U32))
        expert_of = ctx.enter_context(nc.sbuf_tensor("expert_of", [1, BLOCKS], U32))
        route_and_share(nc, gate_w, bias, sw1, sw2, sw3, ident, h_sb, normed_t, rows, table, slots, expert_of)
        run_experts(nc, w1, w2, w3, ident, rows, table, expert_of, routed_out)
        combine(nc, h_sb, slots, routed_out, out)


def constants(nc, ident):
    with nc.semaphore("cleared") as cleared, nc.Block() as block:
        @block.gpsimd
        def _(pool):
            pool.memset(ident[:], 0.0).then_inc(cleared, 1)
            pool.wait_ge(cleared, 1)
            pool.affine_select(out=ident[:], in_=ident[:], compare_op=ALU.not_equal, fill=1.0, base=0,
                               pattern=[[-1, P]], channel_multiplier=1)


_INS = ['x', 'L0_tok_W', 'L0_tok_b', 'L0_tok_g1', 'L0_tok_b1', 'L0_tok_g2', 'L0_tok_b2', 'L0_attn_Wq', 'L0_attn_Wk',
        'L0_attn_Wv', 'L0_attn_Wo', 'L0_ffn_gate_w', 'L0_ffn_w1', 'L0_ffn_w2', 'L0_ffn_w3', 'L0_ffn_sw1',
        'L0_ffn_sw2', 'L0_ffn_sw3', 'L0_ffn_expert_bias']


def kernel(**inputs):
    import numpy as _np
    import concourse.bacc as _bacc
    from concourse.bass_utils import run_bass_kernel_spmd as _run

    nc = _bacc.Bacc("TRN2", target_bir_lowering=False, num_devices=1)
    arrays, args = {}, []
    for name in _INS:
        a = _np.ascontiguousarray(inputs[name])
        arrays[f"in_{name}"] = a
        args.append(nc.dram_tensor(f"in_{name}", a.shape, mybir.dt.from_np(a.dtype), kind="ExternalInput").ap())
    args.append(nc.dram_tensor("out_dram", (BATCH, NPATCH, DIM), F32, kind="ExternalOutput").ap())
    build(nc, *args)
    return _run(nc, [arrays], core_ids=[0]).results[0]["out_dram"]
```

```python
from contextlib import ExitStack
import numpy as np
import concourse.bass as bass
from concourse import mybir

ALU = mybir.AluOpType
ACT = mybir.ActivationFunctionType
AX = mybir.AxisListType
F32 = mybir.dt.float32
F32R = mybir.dt.float32r
U32 = mybir.dt.uint32

P = 128
BATCH, FRAMES, FEAT, TIN = 128, 375, 64, 16
NPATCH = FRAMES // TIN
IN_DIM = TIN * FEAT
DIM = 512
TOK = BATCH * NPATCH
WSEQ = 16
WT = WSEQ * NPATCH
WIN = TOK // WT
ROWS = [128, 128, WT - 256]
TPW = len(ROWS)
KC = DIM // P
XC = IN_DIM // P
EPS_TOK = 1e-6
EPS_LN = 1e-5


def pieces(j):
    out, n, end = [], 128 * j, 128 * j + ROWS[j]
    while n < end:
        s, p = divmod(n, NPATCH)
        whole = (end - n) // NPATCH if p == 0 else 0
        k = whole * NPATCH if whole else min(NPATCH - p, end - n)
        out.append((n - 128 * j, s, p, whole, k))
        n += k
    return out


TPU = 2 * TPW
UNITS = WIN // 2


def rows_of(i):
    return ROWS[i % TPW]


def run_steps(eng, turns, per, lag, step, peeled=1):
    for n in range(peeled * per):
        step(n // per, n % per)
    with eng.Fori(peeled, turns) as u:
        for i in range(per):
            step(u, i)
    for i in range(lag):
        step(turns + i // per, i % per)


def earlier(u, i, n, turns, per):
    d, i = divmod(i - n, per)
    if isinstance(u, int) and not 0 <= u + d < turns:
        return None
    return u + d, i


def tile_steps(eng, lag, step):
    run_steps(eng, UNITS, TPU, lag, step)


def back(u, i, n):
    return earlier(u, i, n, UNITS, TPU)


def number(at):
    return at[0] * TPU + at[1]


def first(at, n):
    return isinstance(at[0], int) and number(at) < n


def tokenise(nc, x, W, b, g1, b1, g2, b2, ident, h_sb, normed_t):
    with ExitStack() as ctx:
        def sb(name, shape, dt=F32):
            return ctx.enter_context(nc.sbuf_tensor(name, shape, dt))

        def sem(name):
            return ctx.enter_context(nc.semaphore(name))

        w_raw = sb("w_raw", [P, XC, DIM])
        w_hi = sb("w_hi", [P, XC, DIM], F32R)
        w_lo = sb("w_lo", [P, XC, DIM], F32R)
        g1_col = sb("g1_col", [P, XC])
        b1_col = sb("b1_col", [P, XC])
        zeros = sb("zeros", [P, P])
        b1_wide = sb("b1_wide", [P, XC, P])
        g2_row = sb("g2_row", [P, DIM])
        b2_row = sb("b2_row", [P, DIM])
        bias_row = sb("bias_row", [P, DIM])
        turnstile = sb("turnstile", [P, 6])
        minus_half = sb("minus_half", [P, 1])
        minus_one = sb("minus_one", [P, 1])
        eps = sb("eps", [P, 3])
        xin = sb("xin", [P, 3, IN_DIM])
        xt_hi = sb("xt_hi", [P, 2, XC, P], F32R)
        xt_lo = sb("xt_lo", [P, 2, XC, P], F32R)
        proj = sb("proj", [P, 2, DIM])
        norm3 = sb("norm3", [P, 2, DIM])
        ht = sb("ht", [P, 3, 2, KC, P], F32R)
        st = [sb(f"st{i}", [P, 3, 2, 6]) for i in range(3)]
        mv = [sb(f"mv{i}", [P, 3, 2]) for i in range(3)]
        ve = [sb(f"ve{i}", [P, 3]) for i in range(3)]
        rstd = [sb(f"rstd{i}", [P, 3]) for i in range(3)]
        shift = [sb(f"shift{i}", [P, 3]) for i in range(3)]
        xt_ps = ctx.enter_context(nc.psum_tensor("xt_ps", [P, 4, KC, P], F32))
        acc = ctx.enter_context(nc.psum_tensor("acc", [P, 2, DIM], F32))
        ht_ps = ctx.enter_context(nc.psum_tensor("ht_ps", [P, 2, KC, P], F32))

        consts_in = sem("consts_in")
        w_in = [sem(f"w_in{c}") for c in range(XC)]
        x_in = [sem(f"x_in{j}") for j in range(TPW)]
        b1_spread = sem("b1_spread")
        w_hi_ready = sem("w_hi_ready")
        w_ready = sem("w_ready")
        bias_mm = sem("bias_mm")
        bias_ready = sem("bias_ready")
        consts_set = sem("consts_set")
        stats_done = [sem(f"stats_done{i}") for i in range(3)]
        mv_done = [sem(f"mv_done{i}") for i in range(3)]
        var_ready = [sem(f"var_ready{i}") for i in range(3)]
        shift_steps = [sem(f"shift_steps{i}") for i in range(2)]
        rstd_ready = [sem(f"rstd_ready{i}") for i in range(3)]
        xhat_ready = sem("xhat_ready")
        xt_done = sem("xt_done")
        xt_hi_done = sem("xt_hi_done")
        xt_lo_done = sem("xt_lo_done")
        acc_done = sem("acc_done")
        proj_ready = sem("proj_ready")
        centred = sem("centred")
        h_ready = sem("h_ready")
        norm3_ready = sem("norm3_ready")
        ht_done = sem("ht_done")
        ht_hi_done = sem("ht_hi_done")
        ht_lo_done = sem("ht_lo_done")
        ht_stored = [sem(f"ht_stored{k}") for k in range(3)]

        flat = x.rearrange("b t f -> b (t f)")
        XHAT, PROJ, LN2, LN3, HT = 1, 3, 4, 5, 6
        block = ctx.enter_context(nc.Block())

        @block.sync
        def _(sp):
            with nc.allow_non_contiguous_dma("columns of two short vectors"):
                sp.dma_start(g1_col[:], g1.rearrange("(c p) -> p c", p=P)).then_inc(consts_in, 16)
                sp.dma_start(b1_col[:], b1.rearrange("(c p) -> p c", p=P)).then_inc(consts_in, 16)
            for row, vector in ((g2_row, g2), (b2_row, b2), (bias_row, b)):
                sp.dma_start(row[:], vector.partition_broadcast(P)).then_inc(consts_in, 16)

            def load_weights():
                for c in range(XC):
                    sp.dma_start(w_raw[:, c, :], W[c * P:c * P + P, :]).then_inc(w_in[c], 16)

            def load(at):
                (u, i), j = at, at[1] % TPW
                if not first(at, 3):
                    sp.wait_ge(xt_done, 2 * (number(at) - 2))
                seq = u * 2 * WSEQ + i // TPW * WSEQ
                for row, s, p, whole, k in pieces(j):
                    src = flat[bass.ds(seq + s, whole or 1), p * IN_DIM:(p + (NPATCH if whole else k)) * IN_DIM]
                    sp.dma_start(xin[row:row + k, i % 3, :], src.rearrange("s (p d) -> s p d", d=IN_DIM))\
                        .then_inc(x_in[j], 16)

            def step(u, i):
                if at := back(u, i, 0):
                    load(at)
                    if first(at, 1):
                        load_weights()
            tile_steps(sp, 0, step)
            for stored in ht_stored:
                sp.wait_ge(stored, 16 * UNITS * TPU // 3)

        @block.gpsimd
        def _(pool):
            pool.memset(minus_half[:], -0.5).then_inc(consts_set, 1)
            pool.memset(minus_one[:], -1.0).then_inc(consts_set, 1)
            pool.memset(zeros[:], 0.0).then_inc(consts_set, 1)
            for n, value in enumerate((EPS_TOK, EPS_TOK, EPS_LN)):
                pool.memset(eps[:, n:n + 1], value).then_inc(consts_set, 1)
            pool.wait_ge(consts_set, 6)
            pool.wait_ge(consts_in, 16 * 5)
            for c in range(XC):
                pool.tensor_scalar(b1_wide[:, c, :], zeros[:], b1_col[:, c:c + 1], None, ALU.add)\
                    .then_inc(b1_spread, 1)

            def power(n, at):
                i, R, N = at[1] % 3, rows_of(at[1]), number(at)
                col = slice(i, i + 1)
                pool.wait_ge(mv_done[n], N + 1)
                pool.tensor_tensor(ve[n][0:R, col], mv[n][0:R, i, 1:2], eps[0:R, n:n + 1], ALU.add)\
                    .then_inc(var_ready[n], 1)
                if n != 1:
                    pool.tensor_tensor(shift[n][0:R, col], mv[n][0:R, i, 0:1], minus_one[0:R, :], ALU.mult)\
                        .then_inc(shift_steps[n // 2], 1)
                pool.wait_ge(var_ready[n], N + 1)
                power = pool.tensor_tensor(rstd[n][0:R, col], ve[n][0:R, col], minus_half[0:R, :], ALU.pow)
                if n == 1:
                    power.then_inc(rstd_ready[n], 1)
                    return
                power.then_inc(shift_steps[n // 2], 1)
                pool.wait_ge(shift_steps[n // 2], 2 * N + 2)
                pool.tensor_tensor(shift[n][0:R, col], shift[n][0:R, col], rstd[n][0:R, col], ALU.mult)\
                    .then_inc(rstd_ready[n], 1)

            def store(at):
                (u, i), j = at, at[1] % TPW
                pool.wait_ge(ht_lo_done, number(at) + 1)
                pool.dma_start(normed_t[u * 2 + i // TPW, :, :, :, 128 * j:128 * j + ROWS[j]],
                             ht[:, i % 3, :, :, 0:ROWS[j]].bitcast(F32)).then_inc(ht_stored[i % 3], 16)

            def step(u, i):
                for n, lag in enumerate((0, PROJ, LN2)):
                    if at := back(u, i, lag):
                        power(n, at)
                if at := back(u, i, HT):
                    store(at)
            tile_steps(pool, HT, step)

        @block.scalar
        def _(act):
            def weights_high():
                act.wait_ge(consts_in, 16 * 5)
                for c in range(XC):
                    act.wait_ge(w_in[c], 16)
                    act.activation(w_hi[:, c, :], w_raw[:, c, :], ACT.Identity, scale=g1_col[:, c:c + 1])\
                        .then_inc(w_hi_ready, 1)

            def normalise(n, at, out, source, done):
                i, R = at[1] % 3, rows_of(at[1])
                act.wait_ge(rstd_ready[n], number(at) + 1)
                act.activation(out, source, ACT.Identity, bias=shift[n][0:R, i:i + 1],
                               scale=rstd[n][0:R, i:i + 1]).then_inc(done, 1)

            def patches_high(at):
                i, R = at[1], rows_of(at[1])
                if not first(at, 2):
                    act.wait_ge(acc_done, number(at) - 1)
                for half in range(2):
                    act.wait_ge(xt_done, 2 * number(at) + half + 1)
                    act.copy(xt_hi[:, i % 2, half * KC:half * KC + KC, 0:R],
                             xt_ps[:, 2 * (i % 2) + half, :, 0:R]).then_inc(xt_hi_done, 1)

            def h_high(at):
                i, R = at[1], rows_of(at[1])
                act.wait_ge(ht_done, number(at) + 1)
                if not first(at, 3):
                    act.wait_ge(ht_stored[i % 3], 16 * (at[0] * 2 + i // 3))
                act.copy(ht[:, i % 3, 0, :, 0:R], ht_ps[:, i % 2, :, 0:R]).then_inc(ht_hi_done, 1)

            def step(u, i):
                if at := back(u, i, XHAT):
                    x = xin[0:rows_of(at[1]), at[1] % 3, :]
                    normalise(0, at, x, x, xhat_ready)
                    if first(at, 1):
                        weights_high()
                if at := back(u, i, LN3):
                    R = rows_of(at[1])
                    if not first(at, 2):
                        act.wait_ge(ht_done, number(at) - 1)
                    normalise(2, at, norm3[0:R, at[1] % 2, :], h_sb[0:R, number(at), :], norm3_ready)
                if at := back(u, i, XHAT):
                    patches_high(at)
                if at := back(u, i, LN3):
                    h_high(at)
            tile_steps(act, LN3, step)

        @block.tensor
        def _(pe):
            pe.wait_ge(b1_spread, XC)
            for c in range(XC):
                pe.wait_ge(w_in[c], 16)
                mm = pe.matmul(acc[:, 0, :], b1_wide[:, c, :], w_raw[:, c, :], start=c == 0, stop=c == XC - 1)
            mm.then_inc(bias_mm, 1)

            def patches_t(at):
                i, R = at[1], rows_of(at[1])
                pe.wait_ge(xhat_ready, number(at) + 1)
                for half in range(2):
                    if not first(at, 2):
                        pe.wait_ge(xt_lo_done, 2 * (number(at) - 2) + half + 1)
                    for c in range(KC):
                        k = half * KC + c
                        mm = pe.transpose(xt_ps[:, 2 * (i % 2) + half, c, 0:R],
                                          xin[0:R, i % 3, k * P:k * P + P], ident[0:R, 0:R])
                    mm.then_inc(xt_done, 1)

            def project(at):
                i, R = at[1], rows_of(at[1])
                pe.wait_ge(xt_lo_done, 2 * number(at) + 2)
                if first(at, 1):
                    pe.wait_ge(bias_ready, 1)
                if not first(at, 2):
                    pe.wait_ge(proj_ready, number(at) - 1)
                for c in range(XC):
                    if first(at, 1):
                        pe.wait_ge(w_ready, c + 1)
                    for lhs, rhs in ((xt_hi, w_hi), (xt_lo, w_hi), (xt_hi, w_lo)):
                        mm = pe.matmul(acc[0:R, i % 2, :], lhs[:, i % 2, c, 0:R], rhs[:, c, :],
                                       start=c == 0 and lhs is xt_hi and rhs is w_hi,
                                       stop=c == XC - 1 and rhs is w_lo)
                mm.then_inc(acc_done, 1)

            def h_t(at):
                i, R = at[1], rows_of(at[1])
                pe.wait_ge(norm3_ready, number(at) + 1)
                if not first(at, 2):
                    pe.wait_ge(ht_lo_done, number(at) - 1)
                for c in range(KC):
                    mm = pe.transpose(ht_ps[:, i % 2, c, 0:R], norm3[0:R, i % 2, c * P:c * P + P],
                                      ident[0:R, 0:R])
                mm.then_inc(ht_done, 1)

            def step(u, i):
                if at := back(u, i, XHAT):
                    patches_t(at)
                if at := back(u, i, LN3):
                    h_t(at)
                if at := back(u, i, XHAT + 1):
                    project(at)
            tile_steps(pe, LN3, step)

        @block.vector
        def _(dve):
            def weights_low():
                for c in range(XC):
                    dve.wait_ge(w_hi_ready, c + 1)
                    dve.scalar_tensor_tensor(w_lo[:, c, :], w_raw[:, c, :], g1_col[:, c:c + 1],
                                             w_hi[:, c, :].bitcast(F32), ALU.mult, ALU.subtract).then_inc(w_ready, 1)
                dve.wait_ge(bias_mm, 1)
                dve.tensor_tensor(bias_row[:], acc[:, 0, :], bias_row[:], ALU.add).then_inc(bias_ready, 1)
                dve.wait_ge(bias_ready, 1)

            def statistics(n, at, source):
                i, R = at[1] % 3, rows_of(at[1])
                dve.memset(turnstile[:, n:n + 1], 0.0)
                for k in range(source.shape[-1] // DIM):
                    dve.bn_stats(st[n][0:R, i, k, :], source[:, k * DIM:k * DIM + DIM]).then_inc(stats_done[n], 1)

            def mean_and_variance(n, at):
                i, R, halves = at[1] % 3, rows_of(at[1]), 2 if n == 0 else 1
                dve.wait_ge(stats_done[n], halves * (number(at) + 1))
                dve.memset(turnstile[:, 3 + n:4 + n], 0.0)
                dve.bn_aggr(mv[n][0:R, i, :], st[n][0:R, i, 0:halves, :].rearrange("p a b -> p (a b)"))\
                    .then_inc(mv_done[n], 1)

            def step(u, i):
                new, to_h = back(u, i, 0), back(u, i, LN2)
                if (at := back(u, i, XHAT)) and first(at, 1):
                    dve.wait_ge(consts_in, 16 * 5)
                    weights_low()
                if at := back(u, i, XHAT + 1):
                    k, R = at[1] % 2, rows_of(at[1])
                    for half in range(2):
                        dve.wait_ge(xt_hi_done, 2 * number(at) + half + 1)
                        chunks = slice(half * KC, half * KC + KC)
                        dve.tensor_tensor(xt_lo[:, k, chunks, 0:R], xt_ps[:, 2 * k + half, :, 0:R],
                                          xt_hi[:, k, chunks, 0:R].bitcast(F32), ALU.subtract)\
                            .then_inc(xt_lo_done, 1)
                projected = back(u, i, PROJ)
                if at := projected:
                    k, R = at[1] % 2, rows_of(at[1])
                    dve.wait_ge(acc_done, number(at) + 1)
                    dve.tensor_tensor(proj[0:R, k, :], acc[0:R, k, :], bias_row[0:R, :], ALU.add)\
                        .then_inc(proj_ready, 1)
                if at := new:
                    dve.wait_ge(x_in[at[1] % TPW], 16 * len(pieces(at[1] % TPW)) * (at[0] * 2 + at[1] // TPW + 1))
                    statistics(0, at, xin[0:rows_of(at[1]), at[1] % 3, :])
                if at := projected:
                    dve.wait_ge(proj_ready, number(at) + 1)
                    statistics(1, at, proj[0:rows_of(at[1]), at[1] % 2, :])
                if new:
                    mean_and_variance(0, new)
                if at := to_h:
                    k, s, R = at[1] % 2, at[1] % 3, rows_of(at[1])
                    dve.wait_ge(rstd_ready[1], number(at) + 1)
                    dve.scalar_tensor_tensor(proj[0:R, k, :], proj[0:R, k, :], mv[1][0:R, s, 0:1], g2_row[0:R, :],
                                             ALU.subtract, ALU.mult).then_inc(centred, 1)
                if projected:
                    mean_and_variance(1, projected)
                if at := to_h:
                    k, s, R = at[1] % 2, at[1] % 3, rows_of(at[1])
                    dve.wait_ge(centred, number(at) + 1)
                    dve.scalar_tensor_tensor(h_sb[0:R, number(at), :], proj[0:R, k, :], rstd[1][0:R, s:s + 1],
                                             b2_row[0:R, :], ALU.mult, ALU.add).then_inc(h_ready, 1)
                    dve.wait_ge(h_ready, number(at) + 1)
                    statistics(2, at, h_sb[0:R, number(at), :])
                if at := back(u, i, HT):
                    k, R = at[1], rows_of(at[1])
                    dve.wait_ge(ht_hi_done, number(at) + 1)
                    dve.tensor_tensor(ht[:, k % 3, 1, :, 0:R], ht_ps[:, k % 2, :, 0:R],
                                      ht[:, k % 3, 0, :, 0:R].bitcast(F32), ALU.subtract).then_inc(ht_lo_done, 1)
                if to_h:
                    mean_and_variance(2, to_h)
            tile_steps(dve, HT, step)


HEADS, KV_HEADS, HD = 16, 4, 128
REP = HEADS // KV_HEADS
GSEQ = 4
GT = GSEQ * NPATCH
GPW = WSEQ // GSEQ
QW = REP * HD
WCOLS = QW + 2 * HD + DIM
WPART = WCOLS // 2
EPS_QK = 1e-6
MASKED = -16384.0
BF16 = mybir.dt.bfloat16
TURNS = KV_HEADS * WIN // 2
TURNS_HEAD = WIN // 2


def attend(nc, Wq, Wk, Wv, Wo, ident, h_sb, normed_t):
    with ExitStack() as ctx:
        def sb(name, shape, dt=F32):
            return ctx.enter_context(nc.sbuf_tensor(name, shape, dt))

        def sem(name):
            return ctx.enter_context(nc.semaphore(name))

        w_raw = sb("aw_raw", [P, WPART])
        w_hi = sb("aw_hi", [P, 2, KC, WCOLS], F32R)
        w_lo = sb("aw_lo", [P, 2, KC, WCOLS], F32R)
        hn = sb("hn", [P, 2, 2, KC, WT], F32R)
        scratch = sb("scratch", [P, 2 * WPART])
        squares = scratch[:, 0:QW]
        rden = scratch[:, QW:QW + REP * GT]
        o_norm = scratch[:, QW + REP * GT:QW + 2 * REP * GT]
        normed = sb("normed", [P, 2, QW])
        ssq = sb("ssq", [P, 4, REP])
        var = sb("var", [P, 4, REP])
        rs = sb("rs", [P, 4, REP])
        minus_half = sb("aminus_half", [P, REP])
        q_t = sb("q_t", [P, 2, REP, WT], F32R)
        k_t = sb("k_t", [P, 2, WT], F32R)
        v = sb("v", [GT, 2, GPW, HD], F32R)
        e = sb("e", [GT, 2, REP * GT])
        p_hi = sb("p_hi", [GT, 2, REP * GT], F32R)
        p_lo = sb("p_lo", [GT, 2, REP * GT], F32R)
        o_t = sb("o_t", [P, 2, REP, WT], F32R)
        ident_b = sb("ident_b", [GT, GT], BF16)
        mask = sb("mask", [GT, REP, GT], BF16)
        ones = sb("ones", [GT, 2], F32R)
        rden_col = sb("rden_col", [GT, REP])
        kv_ps = ctx.enter_context(nc.psum_tensor("kv_ps", [P, GPW, 2 * HD], F32))
        proj_ps = ctx.enter_context(nc.psum_tensor("proj_ps", [P, 2, DIM], F32))
        turn_ps = ctx.enter_context(nc.psum_tensor("turn_ps", [P, 2, DIM], F32))
        o_ps = ctx.enter_context(nc.psum_tensor("o_ps", [P, DIM], F32))
        den_ps = ctx.enter_context(nc.psum_tensor("den_ps", [P, DIM], F32))

        consts = sem("aconsts")
        mask_steps = sem("mask_steps")
        first_in = [sem(f"afirst_in{c}") for c in range(4)]
        w_in = sem("aw_in")
        w_hi_done = sem("aw_hi_done")
        w_lo_done = sem("aw_lo_done")
        hn_in = [sem(f"hn_in{i}") for i in range(2)]
        raw_done = sem("raw_done")
        squared = sem("squared")
        summed = sem("summed")
        var_ready = sem("avar_ready")
        rs_ready = sem("rs_ready")
        normalised = sem("normalised")
        turned = sem("turned")
        turned_hi = sem("turned_hi")
        turned_lo = sem("turned_lo")
        v_hi_done = sem("v_hi_done")
        v_lo_done = sem("v_lo_done")
        scores_done = sem("scores_done")
        exp_done = sem("exp_done")
        p_hi_done = sem("p_hi_done")
        p_lo_done = sem("p_lo_done")
        pv_done = sem("pv_done")
        den_done = sem("den_done")
        rden_ready = sem("rden_ready")
        rden_spread = sem("rden_spread")
        rden_taken = sem("rden_taken")
        o_norm_ready = sem("o_norm_ready")
        o_hi_done = sem("o_hi_done")
        o_lo_done = sem("o_lo_done")
        out_done = sem("out_done")
        h_added = sem("h_added")

        first_raw = [w_raw[:], normed[:].rearrange("p a n -> p (a n)")[:, 0:WPART], scratch[:, 0:WPART],
                     scratch[:, WPART:2 * WPART]]
        RAWS = len(first_raw)
        FIRST_PARTS = [(c, half) for half in range(2) for c in range(KC)]
        K = 1
        TILE_AT = [0, None, 1, 2]

        def count(at):
            return at[0] * 2 + at[1]

        def first_step(at, n=1):
            return isinstance(at[0], int) and count(at) < n

        def steps(eng, step):
            def both(u, i):
                step(earlier(u, i, 0, TURNS, 2), earlier(u, i, 1, TURNS, 2))
            run_steps(eng, TURNS, 2, 1, both)

        def slot(at):
            return at[0] // TURNS_HEAD % 2

        def part_source(head, c, half):
            rows = bass.ds(c * P, P)
            if half == 0:
                return [(0, Wq[rows, bass.ds(head * REP, REP), :].rearrange("p h d -> p (h d)"), QW),
                        (QW, Wk[rows, bass.ds(head, 1), :].rearrange("p h d -> p (h d)"), HD)]
            return [(0, Wv[rows, bass.ds(head, 1), :].rearrange("p h d -> p (h d)"), HD),
                    (HD, Wo[bass.ds((head * REP + c) * P, P), :], DIM)]

        def next_part(at):
            u, i = at
            return (u // TURNS_HEAD + 1) % 2, u % TURNS_HEAD, slice(i * WPART, i * WPART + WPART)

        block = ctx.enter_context(nc.Block())

        @block.sync
        def _(sp):
            def load_hn(at):
                u, i = at
                if not first_step(at, 2):
                    sp.wait_ge(raw_done, 4 * (count(at) - 1))
                sp.dma_start(hn[:, i, :, :, :].bitcast(F32), normed_t[bass.ds((u % TURNS_HEAD) * 2 + i, 1)]
                             .rearrange("a p s c t -> (a p) s c t")).then_inc(hn_in[i], 16)

            load_hn((0, 0))
            for n, (c, half) in enumerate(FIRST_PARTS):
                if n >= RAWS:
                    sp.wait_ge(w_lo_done, n - RAWS + 1)
                for col, src, width in part_source(0, c, half):
                    sp.dma_start(first_raw[n % RAWS][:, col:col + width], src).then_inc(first_in[n % RAWS], 16)

            def load_part(head, c, half):
                for col, src, n in part_source(head, c, half):
                    sp.dma_start(w_raw[:, col:col + n], src).then_inc(w_in, 16)

            def step(front, rear):
                if front:
                    if not first_step(front):
                        load_hn(front)
                    u, i = front
                    sp.wait_ge(w_lo_done, 2 * KC + count(front))
                    load_part((u // TURNS_HEAD + 1) % KV_HEADS, u % TURNS_HEAD, i)
            steps(sp, step)

        @block.gpsimd
        def _(pool):
            pool.memset(minus_half[:], -0.5).then_inc(consts, 1)
            pool.memset(ones[:].bitcast(F32), 1.0).then_inc(consts, 1)
            pool.tensor_copy(ident_b[:], ident[0:GT, 0:GT]).then_inc(consts, 1)
            pool.memset(mask[:], 0.0).then_inc(mask_steps, 1)
            for j in range(GSEQ):
                part = mask[:, :, j * NPATCH:j * NPATCH + NPATCH]
                for side, (base, sign) in enumerate(((-j * NPATCH, 1), (j * NPATCH + NPATCH - 1, -1))):
                    pool.wait_ge(mask_steps, 1 + 2 * j + side)
                    pool.affine_select(out=part, in_=part, compare_op=ALU.is_ge, fill=MASKED, base=base,
                                       pattern=[[0, REP], [0, NPATCH]], channel_multiplier=sign)\
                        .then_inc(mask_steps, 1)
            pool.wait_ge(consts, 3)

            def step(front, rear):
                if front:
                    for s in range(4):
                        R = GT if s == K else ROWS[TILE_AT[s]]
                        pool.wait_ge(var_ready, 4 * count(front) + s + 1)
                        pool.tensor_tensor(rs[0:R, s, :], var[0:R, s, :], minus_half[0:R, :], ALU.pow)\
                            .then_inc(rs_ready, 1)
            steps(pool, step)

        @block.scalar
        def _(act):
            for n, (c, half) in enumerate(FIRST_PARTS):
                cols = slice(half * WPART, half * WPART + WPART)
                act.wait_ge(first_in[n % RAWS], 32 * (n // RAWS + 1))
                act.copy(w_hi[:, 0, c, cols], first_raw[n % RAWS]).then_inc(w_hi_done, 1)

            def step(front, rear):
                f, r = front and count(front), rear and count(rear)

                def exponent(g):
                    act.wait_ge(scores_done, 4 * r + g + 1)
                    if g >= 2 or not first_step(rear):
                        act.wait_ge(p_lo_done, 4 * r + g - 1)
                    act.activation(e[:, g % 2, :], turn_ps[0:GT, g % 2, 0:REP * GT], ACT.Exp,
                                   scale=float(HD) ** -0.5).then_inc(exp_done, 1)
                    if g >= 2 or not first_step(rear):
                        act.wait_ge(pv_done, 4 * r + g - 1)
                    act.wait_ge(exp_done, 4 * r + g + 1)
                    act.copy(p_hi[:, g % 2, :], e[:, g % 2, :]).then_inc(p_hi_done, 1)

                def square(s):
                    act.wait_ge(raw_done, 4 * f + s + 1)
                    if s or not first_step(front):
                        act.wait_ge(summed, 4 * f + s)
                    else:
                        act.wait_ge(w_lo_done, 2 * KC)
                    if s == K:
                        act.activation(squares[0:GT, :].rearrange("p (g d) -> p g d", g=GPW), kv_ps[0:GT, :, 0:HD],
                                       ACT.Square).then_inc(squared, 1)
                    else:
                        j = TILE_AT[s]
                        act.activation(squares[0:ROWS[j], :], proj_ps[0:ROWS[j], j % 2, :], ACT.Square)\
                            .then_inc(squared, 1)

                def values_high():
                    if rear:
                        act.wait_ge(pv_done, 4 * r + 4)
                    act.wait_ge(normalised, 4 * f + K + 1)
                    act.copy(v[:, 0], kv_ps[0:GT, :, HD:2 * HD]).then_inc(v_hi_done, 1)

                def take_reciprocals(g):
                    act.wait_ge(rden_spread, 4 * r + g + 1)
                    if g or not first_step(rear):
                        act.wait_ge(o_norm_ready, 4 * r + g)
                    act.copy(rden[:], den_ps[:, 0:REP * GT]).then_inc(rden_taken, 1)

                def out_high(g):
                    act.wait_ge(o_norm_ready, 4 * r + g + 1)
                    if g == 0 and not first_step(rear):
                        act.wait_ge(out_done, TPW * r)
                    act.copy(o_t[:, 0, :, g * GT:g * GT + GT], o_norm[:].rearrange("p (h t) -> p h t", h=REP))\
                        .then_inc(o_hi_done, 1)

                def turned_high(s):
                    act.wait_ge(turned, 4 * f + s + 1)
                    if rear:
                        act.wait_ge(scores_done, 4 * r + 4)
                    if s == K:
                        act.copy(k_t[:, 0, :], turn_ps[:, s % 2, 0:WT]).then_inc(turned_hi, 1)
                    else:
                        j, R = TILE_AT[s], ROWS[TILE_AT[s]]
                        act.copy(q_t[:, 0, :, j * P:j * P + R],
                                 turn_ps[:, s % 2, 0:REP * R].rearrange("p (h t) -> p h t", h=REP))\
                            .then_inc(turned_hi, 1)

                if rear:
                    exponent(0)
                    exponent(1)
                if front:
                    square(0)
                if rear:
                    exponent(2)
                    take_reciprocals(0)
                    out_high(0)
                    exponent(3)
                    take_reciprocals(1)
                    out_high(1)
                if front:
                    square(K)
                if rear:
                    take_reciprocals(2)
                    out_high(2)
                if front:
                    square(2)
                    turned_high(0)
                if rear:
                    take_reciprocals(3)
                    out_high(3)
                if front:
                    square(3)
                    values_high()
                    for s in range(1, 4):
                        turned_high(s)
                    into, c, cols = next_part(front)
                    act.wait_ge(w_in, 32 * (f + 1))
                    if rear:
                        act.wait_ge(out_done, TPW * (r + 1))
                    act.copy(w_hi[:, bass.ds(into, 1), bass.ds(c, 1), cols].rearrange("p a b n -> p (a b n)"), w_raw[:])\
                        .then_inc(w_hi_done, 1)
            steps(act, step)

        @block.tensor
        def _(pe):
            pe.wait_ge(mask_steps, 1 + 2 * GSEQ)
            pe.wait_ge(consts, 3)

            def products(out, pairs, start, stop):
                for n, (lhs, rhs) in enumerate(pairs):
                    mm = pe.matmul(out, lhs, rhs, start=start and n == 0, stop=stop and n == len(pairs) - 1)
                return mm

            def weights(at, c, cols):
                return [w[:, bass.ds(slot(at), 1), c, cols].rearrange("p a n -> p (a n)") for w in (w_hi, w_lo)]

            def step(front, rear):
                f, r = front and count(front), rear and count(rear)

                def query(j, chunks=range(KC)):
                    i, R = front[1], ROWS[j]
                    if j == 0:
                        pe.wait_ge(hn_in[i], 16 * (front[0] + 1))
                        if not first_step(front):
                            pe.wait_ge(w_lo_done, 2 * KC + (front[0] // TURNS_HEAD) * WIN)
                    if j < 2 and rear and not first_step(rear):
                        pe.wait_ge(h_added, TPW * (r - 1) + 2 + j)
                    if j == 2:
                        pe.wait_ge(normalised, 4 * f + 1)
                    for c in chunks:
                        if j == 0 and first_step(front):
                            pe.wait_ge(w_lo_done, c + 1)
                        hi, lo = (hn[:, i, k, c, j * P:j * P + R] for k in range(2))
                        w, wl = weights(front, c, slice(0, QW))
                        mm = products(proj_ps[0:R, j % 2, :], ((hi, w), (lo, w), (hi, wl)), c == 0, c == KC - 1)
                    if KC - 1 in chunks:
                        mm.then_inc(raw_done, 1)

                def keys_values(g, chunks=range(KC)):
                    i = front[1]
                    if g == 0 and 0 in chunks and rear:
                        pe.wait_ge(v_lo_done, f)
                        pe.wait_ge(normalised, 4 * (f - 1) + K + 1)
                    if g == 0 and first_step(front):
                        pe.wait_ge(w_lo_done, 2 * KC)
                    for c in chunks:
                        hi, lo = (hn[:, i, k, c, g * GT:g * GT + GT] for k in range(2))
                        w, wl = weights(front, c, slice(QW, QW + 2 * HD))
                        mm = products(kv_ps[0:GT, g, :], ((hi, w), (lo, w), (hi, wl)), c == 0, c == KC - 1)
                    if g == GPW - 1:
                        mm.then_inc(raw_done, 1)

                def turn(s):
                    R = GT if s == K else ROWS[TILE_AT[s]]
                    pe.wait_ge(normalised, 4 * f + s + 1)
                    if s < 2 and rear:
                        pe.wait_ge(exp_done, 4 * r + 3 + s)
                    if s >= 2:
                        pe.wait_ge(turned_lo, 4 * f + s - 1)
                    for n in range(REP):
                        mm = pe.transpose(turn_ps[:, s % 2, n * R:n * R + R], normed[0:R, s % 2, n * HD:n * HD + HD],
                                          ident[0:R, 0:R])
                    mm.then_inc(turned, 1)

                def scores(g):
                    if g == 0:
                        pe.wait_ge(turned_lo, 4 * r + 4)
                    if g >= 2:
                        pe.wait_ge(exp_done, 4 * r + g - 1)
                    out = turn_ps[0:GT, g % 2, 0:REP * GT]
                    pe.matmul(out, ident_b[:], mask[:].rearrange("p h t -> p (h t)"), start=True, stop=False)
                    k_hi, k_lo = (k_t[:, k, g * GT:g * GT + GT] for k in range(2))
                    q_hi, q_lo = (q_t[:, k, :, g * GT:g * GT + GT] for k in range(2))
                    products(out, ((k_hi, q_hi), (k_lo, q_hi), (k_hi, q_lo)), False, True).then_inc(scores_done, 1)

                def attended(g):
                    pe.wait_ge(p_lo_done, 4 * r + g + 1)
                    if g == 0:
                        pe.wait_ge(v_lo_done, r + 1)
                    if g or not first_step(rear):
                        pe.wait_ge(o_norm_ready, 4 * r + g)
                    hi, lo = p_hi[:, g % 2, :], p_lo[:, g % 2, :]
                    for n in range(REP):
                        head = slice(n * GT, n * GT + GT)
                        mm = products(den_ps[0:GT, REP * GT + 2 * n:REP * GT + 2 * n + 2],
                                      ((hi[:, head], ones[:]), (lo[:, head], ones[:])), True, True)
                    mm.then_inc(den_done, 1)
                    products(o_ps[:, 0:REP * GT], ((v[:, 0, g, :], hi), (v[:, 0, g, :], lo), (v[:, 1, g, :], hi)),
                             True, True).then_inc(pv_done, 1)

                def spread(g):
                    pe.wait_ge(rden_ready, 4 * r + g + 1)
                    for n in range(REP):
                        mm = pe.transpose(den_ps[:, n * GT:n * GT + GT],
                                          rden_col[:, n:n + 1].broadcast_to([GT, P]), ident[0:GT, 0:GT])
                    mm.then_inc(rden_spread, 1)

                def output(j):
                    R = ROWS[j]
                    if j == 0:
                        pe.wait_ge(o_lo_done, 4 * r + 4)
                    if j < 2 and front:
                        pe.wait_ge(normalised, 4 * f + 3 + j)
                    elif j < 2:
                        pe.wait_ge(h_added, TPW * r)
                    else:
                        pe.wait_ge(h_added, TPW * r + 1)
                    for c in range(REP):
                        hi, lo = (o_t[:, k, c, j * P:j * P + R] for k in range(2))
                        w, wl = weights(rear, c, slice(QW + 2 * HD, WCOLS))
                        mm = products(proj_ps[0:R, (j + 1) % 2, :], ((hi, w), (lo, w), (hi, wl)), c == 0, c == REP - 1)
                    mm.then_inc(out_done, 1)

                if rear:
                    scores(0)
                    scores(1)
                if front:
                    query(0)
                if rear:
                    attended(0)
                    scores(2)
                if front:
                    keys_values(0, range(0, 1))
                if rear:
                    spread(0)
                if front:
                    keys_values(0, range(1, KC))
                    keys_values(1)
                if rear:
                    attended(1)
                    scores(3)
                if front:
                    keys_values(2, range(0, 1))
                if rear:
                    spread(1)
                if front:
                    keys_values(2, range(1, KC))
                    keys_values(3)
                if rear:
                    attended(2)
                if front:
                    query(1, range(0, 2))
                if rear:
                    spread(2)
                if front:
                    query(1, range(2, KC))
                if rear:
                    attended(3)
                if front:
                    turn(0)
                if rear:
                    spread(3)
                if front:
                    query(2)
                    turn(K)
                if rear:
                    output(0)
                if front:
                    turn(2)
                if rear:
                    output(1)
                if front:
                    turn(3)
                if rear:
                    output(2)
            steps(pe, step)

        @block.vector
        def _(dve):
            for n, (c, half) in enumerate(FIRST_PARTS):
                cols = slice(half * WPART, half * WPART + WPART)
                dve.wait_ge(w_hi_done, n + 1)
                dve.tensor_tensor(w_lo[:, 0, c, cols], first_raw[n % RAWS],
                                  w_hi[:, 0, c, cols].bitcast(F32), ALU.subtract).then_inc(w_lo_done, 1)

            def step(front, rear):
                f, r = front and count(front), rear and count(rear)

                def probs_low(g):
                    dve.wait_ge(p_hi_done, 4 * r + g + 1)
                    dve.tensor_tensor(p_lo[:, g % 2, :], e[:, g % 2, :], p_hi[:, g % 2, :].bitcast(F32), ALU.subtract)\
                        .then_inc(p_lo_done, 1)

                def sums(s):
                    R = GT if s == K else ROWS[TILE_AT[s]]
                    dve.wait_ge(squared, 4 * f + s + 1)
                    dve.tensor_reduce(ssq[0:R, s, :], squares[0:R, :].rearrange("p (h d) -> p h d", h=REP), AX.X,
                                      ALU.add).then_inc(summed, 1)
                    dve.wait_ge(summed, 4 * f + s + 1)
                    dve.tensor_scalar(var[0:R, s, :], ssq[0:R, s, :], 1.0 / HD, EPS_QK, ALU.mult, ALU.add)\
                        .then_inc(var_ready, 1)

                def normalise(s):
                    R = GT if s == K else ROWS[TILE_AT[s]]
                    dve.wait_ge(rs_ready, 4 * f + s + 1)
                    if s >= 2 or not first_step(front):
                        dve.wait_ge(turned, 4 * f + s - 1)
                    raw = kv_ps[0:GT, :, 0:HD] if s == K else \
                        proj_ps[0:R, TILE_AT[s] % 2, :].rearrange("p (h d) -> p h d", h=REP)
                    dve.tensor_tensor(normed[0:R, s % 2, :].rearrange("p (h d) -> p h d", h=REP), raw,
                                      rs[0:R, s, :].unsqueeze(2).broadcast_to([R, REP, HD]), ALU.mult)\
                        .then_inc(normalised, 1)

                def values_low():
                    dve.wait_ge(v_hi_done, f + 1)
                    dve.tensor_tensor(v[:, 1], kv_ps[0:GT, :, HD:2 * HD], v[:, 0].bitcast(F32), ALU.subtract)\
                        .then_inc(v_lo_done, 1)

                def reciprocals(g):
                    dve.wait_ge(den_done, 4 * r + g + 1)
                    if g or not first_step(rear):
                        dve.wait_ge(rden_spread, 4 * r + g)
                    dve.reciprocal(rden_col[:], den_ps[0:GT, REP * GT:REP * GT + 2 * REP:2]).then_inc(rden_ready, 1)

                def divide(g):
                    dve.wait_ge(pv_done, 4 * r + g + 1)
                    dve.wait_ge(rden_taken, 4 * r + g + 1)
                    if g or not first_step(rear):
                        dve.wait_ge(o_lo_done, 4 * r + g)
                    dve.tensor_tensor(o_norm[:], o_ps[:, 0:REP * GT], rden[:], ALU.mult).then_inc(o_norm_ready, 1)

                def out_low(g):
                    dve.wait_ge(o_hi_done, 4 * r + g + 1)
                    cols = slice(g * GT, g * GT + GT)
                    dve.tensor_tensor(o_t[:, 1, :, cols], o_norm[:].rearrange("p (h t) -> p h t", h=REP),
                                      o_t[:, 0, :, cols].bitcast(F32), ALU.subtract).then_inc(o_lo_done, 1)

                def turned_low(s):
                    dve.wait_ge(turned_hi, 4 * f + s + 1)
                    if s == K:
                        dve.tensor_tensor(k_t[:, 1, :], turn_ps[:, s % 2, 0:WT], k_t[:, 0, :].bitcast(F32),
                                          ALU.subtract).then_inc(turned_lo, 1)
                    else:
                        j, R = TILE_AT[s], ROWS[TILE_AT[s]]
                        cols = slice(j * P, j * P + R)
                        dve.tensor_tensor(q_t[:, 1, :, cols],
                                          turn_ps[:, s % 2, 0:REP * R].rearrange("p (h t) -> p h t", h=REP),
                                          q_t[:, 0, :, cols].bitcast(F32), ALU.subtract).then_inc(turned_lo, 1)

                def add(j):
                    R = ROWS[j]
                    tile = h_sb[0:R, bass.ds((rear[0] % TURNS_HEAD) * TPU + rear[1] * TPW + j, 1), :]\
                        .rearrange("p a n -> p (a n)")
                    dve.wait_ge(out_done, TPW * r + j + 1)
                    dve.tensor_tensor(tile, proj_ps[0:R, (j + 1) % 2, :], tile, ALU.add).then_inc(h_added, 1)

                if rear:
                    probs_low(0)
                    probs_low(1)
                if front:
                    sums(0)
                if rear:
                    reciprocals(0)
                if front:
                    normalise(0)
                if rear:
                    probs_low(2)
                    divide(0)
                    out_low(0)
                    reciprocals(1)
                    probs_low(3)
                    divide(1)
                    out_low(1)
                if front:
                    sums(K)
                if rear:
                    reciprocals(2)
                if front:
                    normalise(K)
                if rear:
                    divide(2)
                    out_low(2)
                if front:
                    sums(2)
                if rear:
                    reciprocals(3)
                if front:
                    normalise(2)
                if rear:
                    divide(3)
                    out_low(3)
                if front:
                    turned_low(0)
                    sums(3)
                    values_low()
                    normalise(3)
                    turned_low(K)
                if rear:
                    add(0)
                if front:
                    turned_low(2)
                if rear:
                    add(1)
                if front:
                    turned_low(3)
                if rear:
                    add(2)
                if front:
                    into, c, cols = next_part(front)
                    dve.wait_ge(w_hi_done, 2 * KC + f + 1)
                    hi, lo = (w[:, bass.ds(into, 1), bass.ds(c, 1), cols].rearrange("p a b n -> p (a b n)")
                              for w in (w_hi, w_lo))
                    dve.tensor_tensor(lo, w_raw[:], hi.bitcast(F32), ALU.subtract).then_inc(w_lo_done, 1)
            steps(dve, step)


EXPERTS, HID = 8, 448
MC = -(-HID // P)
HCS = [min(P, HID - m * P) for m in range(MC)]

MAIN = HID // P * P
LAST = HID - MAIN
assert 2 * LAST == P
GATE_AT = HID + LAST
PARTS = [(0, "up", slice(0, HID)), (HID, "gate", slice(MAIN, HID)), (GATE_AT, "gate", slice(0, MAIN))]


def products_of(m):
    if m == MC - 1:
        return [slice(MAIN, MAIN + P)]
    return [slice(at + m * P, at + m * P + P) for at in (0, GATE_AT)]


def up_of(ps, m):
    return ps[0:HCS[m], 0, :]


def gate_of(ps, m):
    return ps[LAST:P, 0, :] if m == MC - 1 else ps[:, 1, :]


TILES = WIN * TPW
SLOTS = 256
BLOCKS = (2 * TOK + EXPERTS * (SLOTS - 1)) // SLOTS
LIMITS = -(-TOK // SLOTS)


def route_and_share(nc, gate_w, bias, sw1, sw2, sw3, ident, h_sb, normed_t, rows, table, slots, expert_of):
    with ExitStack() as ctx:
        def sb(name, shape, dt=F32):
            return ctx.enter_context(nc.sbuf_tensor(name, shape, dt))

        def sem(name):
            return ctx.enter_context(nc.semaphore(name))

        gate = sb("gate", [P, KC, EXPERTS])
        gate_parts = sb("gate_parts", [P, KC, 2, EXPERTS], F32R)
        bias_row = sb("fbias_row", [P, EXPERTS])
        minus_half = sb("fminus_half", [P, 1])
        minus_one = sb("fminus_one", [P, 1])
        eps = sb("feps", [P, 1])
        st = sb("fst", [P, 3, 6])
        mv = sb("fmv", [P, 3, 2])
        ve = sb("fve", [P, 3])
        rstd = sb("frstd", [P, 3])
        shift = sb("fshift", [P, 3])
        turnstile = sb("fturnstile", [P, 2])
        norm = sb("norm", [P, 3, DIM])
        ht = sb("fht", [P, 3, 2, KC, P], F32R)
        grid = [P, TILES, EXPERTS]
        logits = sb("logits", grid)
        scores = sb("scores", grid)
        chosen = [sb(f"chosen{k}", grid) for k in range(2)]
        work = sb("work", grid)
        key = sb("key", grid)
        rank = sb("rank", grid)
        falling = sb("falling", [P, EXPERTS])
        valid = sb("valid", [P, TILES])
        best = sb("best", [P, TILES])
        both = sb("both", grid, BF16)
        below = sb("below", [P, P], BF16)
        ones_b = sb("ones_b", [P, P], BF16)
        per_row = sb("per_row", [P, EXPERTS], BF16)
        counts = sb("counts", [P, EXPERTS])
        limits = sb("limits", [P, LIMITS])
        over = sb("over", [P, EXPERTS, LIMITS])
        blocks = sb("blocks", [P, EXPERTS])
        upto = sb("upto", [P, EXPERTS])
        start = sb("start", [P, EXPERTS])
        block_no = sb("block_no", [P, BLOCKS])
        passed = sb("passed", [P, BLOCKS, EXPERTS])
        expert_f = sb("expert_f", [P, BLOCKS])
        payload = sb("payload", [P, TILES, 2, 2], U32)
        slot_f = sb("slot_f", [P, TILES])
        zero_table = sb("zero_table", [P, BLOCKS * SLOTS // P * 2], U32)
        raw = sb("sraw", [P, KC, 2 * HID])
        raw2 = sb("sraw2", [P, MC, DIM])
        w13_hi = sb("sw13_hi", [P, KC, 2 * HID], F32R)
        w13_lo = sb("sw13_lo", [P, KC, 2 * HID], F32R)
        w2_hi = sb("sw2_hi", [P, MC, DIM], F32R)
        w2_lo = sb("sw2_lo", [P, MC, DIM], F32R)
        xt = sb("sxt", [P, 2, 2, KC, WT], F32R)
        gated = sb("gated", [P, 2, WT])
        hidden = sb("hidden", [P, 2, WT])
        hid_hi = sb("hid_hi", [P, MC, WT], F32R)
        hid_lo = sb("hid_lo", [P, MC, WT], F32R)

        ht_ps = ctx.enter_context(nc.psum_tensor("fht_ps", [P, KC, P], F32))
        gate_ps = ctx.enter_context(nc.psum_tensor("gate_ps", [P, DIM], F32))
        gu_ps = ctx.enter_context(nc.psum_tensor("gu_ps", [P, 2, 2, DIM], F32))
        y_ps = ctx.enter_context(nc.psum_tensor("y_ps", [P, 2, DIM], F32))

        consts_in = sem("fconsts_in")
        consts = sem("fconsts")
        w_in = sem("sw_in")
        gate_hi_done = sem("gate_hi_done")
        gate_ready = sem("gate_ready")
        w_hi_done = sem("sw_hi_done")
        w_lo_done = sem("sw_lo_done")
        stats_done = sem("fstats_done")
        mv_done = sem("fmv_done")
        var_ready = sem("fvar_ready")
        shift_steps = sem("fshift_steps")
        rstd_ready = sem("frstd_ready")
        norm_ready = sem("fnorm_ready")
        rows_stored = [sem(f"rows_stored{k}") for k in range(3)]
        ht_done = sem("fht_done")
        ht_hi_done = sem("fht_hi_done")
        ht_lo_done = sem("fht_lo_done")
        ht_stored = [sem(f"fht_stored{k}") for k in range(3)]
        gate_done = sem("gate_done")
        logits_ready = sem("logits_ready")
        table_zeroed = sem("table_zeroed")
        routed = sem("routed")
        centred = sem("fcentred")
        exp_done = sem("fexp_done")
        counts_ready = sem("counts_ready")
        ranks_done = sem("ranks_done")
        counts_done = sem("counts_done")
        slots_ready = sem("slots_ready")
        scattered = sem("scattered")
        xt_in = [sem(f"sxt_in{k}") for k in range(2)]
        gu_done = sem("gu_done")
        silu_done = sem("silu_done")
        hidden_ready = sem("hidden_ready")
        hid_hi_done = sem("hid_hi_done")
        hid_lo_done = sem("hid_lo_done")
        y_done = sem("y_done")
        h_added = sem("fh_added")

        APPLY, TURN, GATES, LOGITS = 1, 2, 3, 4
        SHARED = UNITS

        def shared_steps(eng, step):
            def with_window(u, i):
                step(u, i, None if isinstance(u, int) and u == 0 else u - 1)
            run_steps(eng, UNITS, TPU, TPU, with_window, peeled=2)

        def known(v):
            return isinstance(v, int)

        def slot_of(v):
            return (v + 1) % 2 if known(v) and v >= SHARED else 0

        def loads_until(v):
            return v + 1 if not known(v) or v < SHARED else 1 + (v - SHARED) // 2 + (SHARED if slot_of(v) == 0 else 0)

        ranks_ps = gate_ps[:, 0:TILES * EXPERTS].rearrange("p (t e) -> p t e", e=EXPERTS)
        counts_ps = ht_ps[:, 0, 0:EXPERTS]

        block = ctx.enter_context(nc.Block())

        @block.sync
        def _(sp):
            sp.dma_start(gate[:], gate_w.rearrange("(c p) e -> p c e", p=P)).then_inc(consts_in, 16)
            sp.dma_start(bias_row[:], bias.partition_broadcast(P)).then_inc(consts_in, 16)
            for at, w, cols in PARTS:
                sp.dma_start(raw[:, :, at:at + cols.stop - cols.start],
                             {"up": sw3, "gate": sw1}[w][:, cols].rearrange("(c p) n -> p c n", p=P)).then_inc(w_in, 16)
            whole = HID // P
            sp.dma_start(raw2[:, 0:whole, :], sw2[0:whole * P, :].rearrange("(c p) n -> p c n", p=P)).then_inc(w_in, 16)
            sp.dma_start(raw2[0:HCS[-1], MC - 1, :], sw2[whole * P:HID, :]).then_inc(w_in, 16)

            def store_rows(at):
                (u, i), j, R = at, at[1] % TPW, rows_of(at[1])
                sp.wait_ge(norm_ready, number(at) + 1)
                sp.dma_start(rows[bass.ds((u * 2 + i // TPW) * WT + P * j, R), :], norm[0:R, i % 3, :])\
                    .then_inc(rows_stored[i % 3], 16)

            def store_turned(at):
                (u, i), j, R = at, at[1] % TPW, rows_of(at[1])
                sp.wait_ge(ht_lo_done, number(at) + 1)
                sp.dma_start(normed_t[u * 2 + i // TPW, :, :, :, P * j:P * j + R],
                             ht[:, i % 3, :, :, 0:R].bitcast(F32)).then_inc(ht_stored[i % 3], 16)

            def load(v):
                slot = slot_of(v)
                sp.dma_start(xt[:, slot].bitcast(F32), normed_t[bass.ds(v, 1)].rearrange("a p s c t -> (a p) s c t"))\
                    .then_inc(xt_in[slot], 16)

            def step(u, i, v):
                if at := back(u, i, APPLY):
                    store_rows(at)
                if at := back(u, i, TURN):
                    store_turned(at)
                if known(u) and u == 0:
                    if i == TPU - 1:
                        for stored in ht_stored:
                            sp.wait_ge(stored, 16)
                        load(0)
                elif not (known(u) and u == SHARED) and i == MC:
                    sp.wait_ge(gu_done, MC * u)
                    load(u)
            shared_steps(sp, step)
            for k in range(3):
                sp.wait_ge(rows_stored[k], 16 * TILES // 3)
                sp.wait_ge(ht_stored[k], 16 * TILES // 3)
            for v in range(SHARED, WIN):
                if v > SHARED:
                    sp.wait_ge(gu_done, MC * (v - 1))
                load(v)

        @block.gpsimd
        def _(pool):
            pool.memset(zero_table[:], 0).then_inc(consts, 1)
            pool.memset(minus_half[:], -0.5).then_inc(consts, 1)
            pool.memset(minus_one[:], -1.0).then_inc(consts, 1)
            pool.memset(eps[:], EPS_LN).then_inc(consts, 1)
            pool.memset(logits[:], 0.0).then_inc(consts, 1)
            pool.memset(ones_b[:], 1.0).then_inc(consts, 1)
            pool.memset(below[:], 1.0).then_inc(consts, 1)
            pool.memset(valid[:], 1.0).then_inc(consts, 1)
            for n in range(EXPERTS):
                pool.memset(falling[:, n:n + 1], float(EXPERTS - n)).then_inc(consts, 1)
            for n in range(LIMITS):
                pool.memset(limits[:, n:n + 1], float(n * SLOTS)).then_inc(consts, 1)
            for n in range(BLOCKS):
                pool.memset(block_no[:, n:n + 1], float(n)).then_inc(consts, 1)
            made = 8 + EXPERTS + LIMITS + BLOCKS
            pool.wait_ge(consts, made)
            pool.dma_start(table.rearrange("(p n) w -> p (n w)", p=P), zero_table[:]).then_inc(table_zeroed, 16)
            pool.affine_select(out=below[:], in_=below[:], compare_op=ALU.is_gt, fill=0.0, base=0, pattern=[[1, P]],
                               channel_multiplier=-1).then_inc(consts, 1)
            last = valid[:].rearrange("p (w j) -> p w j", j=TPW)[:, :, TPW - 1]
            pool.affine_select(out=last, in_=last, compare_op=ALU.is_gt, fill=0.0, base=ROWS[-1], pattern=[[0, WIN]],
                               channel_multiplier=-1).then_inc(consts, 1)
            for k in range(2):
                for j in range(TPW):
                    pool.iota(payload[:].rearrange("p (w j) k n -> p j k n w", j=TPW)[:, j, k, 0, :],
                              pattern=[[WT, WIN]], base=P * j, channel_multiplier=1).then_inc(consts, 1)

            def step(u, i, v):
                if at := back(u, i, 0):
                    k, R, N = at[1] % 3, rows_of(at[1]), number(at)
                    col = slice(k, k + 1)
                    pool.wait_ge(mv_done, N + 1)
                    pool.tensor_tensor(ve[0:R, col], mv[0:R, k, 1:2], eps[0:R, :], ALU.add).then_inc(var_ready, 1)
                    pool.tensor_tensor(shift[0:R, col], mv[0:R, k, 0:1], minus_one[0:R, :], ALU.mult)\
                        .then_inc(shift_steps, 1)
                    pool.wait_ge(var_ready, N + 1)
                    pool.tensor_tensor(rstd[0:R, col], ve[0:R, col], minus_half[0:R, :], ALU.pow)\
                        .then_inc(shift_steps, 1)
                    pool.wait_ge(shift_steps, 2 * N + 2)
                    pool.tensor_tensor(shift[0:R, col], shift[0:R, col], rstd[0:R, col], ALU.mult)\
                        .then_inc(rstd_ready, 1)
            shared_steps(pool, step)

            pool.wait_ge(table_zeroed, 16)
            pool.wait_ge(slots_ready, 4)
            for n in range(TILES):
                R = ROWS[n % TPW]
                for k in range(2):
                    pool.indirect_dma_start(out=table[:, :],
                                            out_offset=bass.IndirectOffsetOnAxis(ap=slots[0:R, k, n:n + 1], axis=0),
                                            in_=payload[0:R, n, k, :], in_offset=None).then_inc(scattered, 16)
            pool.wait_ge(scattered, 16 * 2 * TILES)

        @block.scalar
        def _(act):
            act.wait_ge(consts_in, 32)
            act.copy(gate_parts[:, :, 0, :], gate[:]).then_inc(gate_hi_done, 1)

            def normalise(at):
                k, R = at[1] % 3, rows_of(at[1])
                if not first(at, 3):
                    act.wait_ge(rows_stored[k], 16 * (at[0] * 2 + at[1] // 3))
                    act.wait_ge(ht_done, number(at) - 2)
                act.wait_ge(rstd_ready, number(at) + 1)
                act.activation(norm[0:R, k, :], h_sb[0:R, number(at), :], ACT.Identity, bias=shift[0:R, k:k + 1],
                               scale=rstd[0:R, k:k + 1]).then_inc(norm_ready, 1)

            def high(at):
                i, R = at[1], rows_of(at[1])
                act.wait_ge(ht_done, number(at) + 1)
                if not first(at, 3):
                    act.wait_ge(ht_stored[i % 3], 16 * (at[0] * 2 + i // 3))
                    act.wait_ge(gate_done, number(at) - 2)
                act.copy(ht[:, i % 3, 0, :, 0:R], ht_ps[:, :, 0:R]).then_inc(ht_hi_done, 1)

            def silu(v, m):
                act.wait_ge(gu_done, MC * v + m + 1)
                if not (known(v) and MC * v + m < 2):
                    act.wait_ge(hidden_ready, MC * v + m - 1)
                act.activation(gated[0:HCS[m], m % 2, :], gate_of(gu_ps[:, m % 2, :, 0:WT], m), ACT.Silu)\
                    .then_inc(silu_done, 1)

            def hidden_high(v, m):
                act.wait_ge(hidden_ready, MC * v + m + 1)
                if m == 0 and not (known(v) and v == 0):
                    act.wait_ge(y_done, TPW * v)
                act.copy(hid_hi[0:HCS[m], m, :], hidden[0:HCS[m], m % 2, :]).then_inc(hid_hi_done, 1)

            def step(u, i, v):
                m = i - 1
                piece = v is not None and 0 <= m < MC
                if piece:
                    silu(v, m)
                if at := back(u, i, TURN):
                    high(at)
                if piece:
                    hidden_high(v, m)
                if at := back(u, i, APPLY):
                    normalise(at)
                if known(u) and u == 0 and i >= TPU - 2:
                    if i == TPU - 2:
                        act.wait_ge(w_in, 16 * 5)
                    for c in ((0, 1), (2, 3))[i - (TPU - 2)]:
                        act.copy(w13_hi[:, c, :], raw[:, c, :]).then_inc(w_hi_done, 1)
                if known(u) and u == 1 and i < MC:
                    act.copy(w2_hi[0:HCS[i], i, :], raw2[0:HCS[i], i, :]).then_inc(w_hi_done, 1)
            shared_steps(act, step)

            act.wait_ge(centred, 1)
            act.activation(scores[:], work[:], ACT.Exp).then_inc(exp_done, 1)
            for v in range(SHARED, WIN):
                for m in range(MC):
                    silu(v, m)
                    hidden_high(v, m)

        @block.tensor
        def _(pe):
            pe.wait_ge(gate_ready, 1)

            def turn(at):
                i, R = at[1], rows_of(at[1])
                pe.wait_ge(norm_ready, number(at) + 1)
                if not first(at, 1):
                    pe.wait_ge(ht_lo_done, number(at))
                for c in range(KC):
                    mm = pe.transpose(ht_ps[:, c, 0:R], norm[0:R, i % 3, c * P:c * P + P], ident[0:R, 0:R])
                mm.then_inc(ht_done, 1)

            def gates(at):
                i, R = at[1], rows_of(at[1])
                pe.wait_ge(ht_lo_done, number(at) + 1)
                if not first(at, 1):
                    pe.wait_ge(logits_ready, number(at))
                for c in range(KC):
                    for k in range(2):
                        mm = pe.matmul(gate_ps[0:R, 0:2 * EXPERTS], ht[:, i % 3, k, c, 0:R],
                                       gate_parts[:, c].rearrange("p k e -> p (k e)"), start=c == 0 and k == 0,
                                       stop=c == KC - 1 and k == 1)
                mm.then_inc(gate_done, 1)

            def gate_and_up(v, m):
                if m == 0:
                    pe.wait_ge(xt_in[slot_of(v)], 16 * loads_until(v))
                    if known(v) and v == 0:
                        pe.wait_ge(w_lo_done, KC)
                if not (known(v) and MC * v + m < 2):
                    pe.wait_ge(hidden_ready, MC * v + m - 1)
                for k, cols in enumerate(products_of(m)):
                    for c in range(KC):
                        x_hi, x_lo = (xt[:, slot_of(v), s, c, :] for s in range(2))
                        w, wl = w13_hi[:, c, cols], w13_lo[:, c, cols]
                        for q, (lhs, rhs) in enumerate(((w, x_hi), (wl, x_hi), (w, x_lo))):
                            mm = pe.matmul(gu_ps[:, m % 2, k, 0:WT], lhs, rhs, start=c == 0 and q == 0,
                                           stop=c == KC - 1 and q == 2)
                mm.then_inc(gu_done, 1)

            def down(v, j):
                R, tok = ROWS[j], slice(j * P, j * P + ROWS[j])
                if not (known(v) and v == 0 and j < 2):
                    pe.wait_ge(h_added, TPW * v + (j == 2))
                if known(v) and v == 0 and j == 0:
                    pe.wait_ge(w_lo_done, KC + MC)
                for c in range(MC):
                    if j == 0:
                        pe.wait_ge(hid_lo_done, MC * v + c + 1)
                    h, hl = hid_hi[0:HCS[c], c, tok], hid_lo[0:HCS[c], c, tok]
                    for q, (lhs, rhs) in enumerate(((h, w2_hi), (hl, w2_hi), (h, w2_lo))):
                        mm = pe.matmul(y_ps[0:R, j % 2, :], lhs, rhs[0:HCS[c], c, :], start=c == 0 and q == 0,
                                       stop=c == MC - 1 and q == 2)
                mm.then_inc(y_done, 1)

            def step(u, i, v):
                if at := back(u, i, TURN):
                    turn(at)
                if at := back(u, i, GATES):
                    gates(at)
                if v is not None:
                    if i < MC:
                        gate_and_up(v, i)
                    elif i == MC:
                        down(v, 0)
                    else:
                        down(v, 1)
                        down(v, 2)
            shared_steps(pe, step)

            def count_ranks():
                pe.wait_ge(consts, 10 + EXPERTS + LIMITS + BLOCKS)
                pe.wait_ge(counts_ready, 2)
                pe.matmul(ranks_ps, below[:], both[:], start=True, stop=False)
                for t in range(TILES - 1):
                    after = TILES - 1 - t
                    mm = pe.matmul(ranks_ps[:, t + 1:TILES, :], ones_b[:],
                                   both[:, t, :].unsqueeze(1).broadcast_to([P, after, EXPERTS]), start=False,
                                   stop=t == TILES - 2)
                mm.then_inc(ranks_done, 1)
                pe.matmul(counts_ps, ones_b[:], per_row[:], start=True, stop=True).then_inc(counts_done, 1)

            for v in range(SHARED, WIN):
                for m in range(MC):
                    gate_and_up(v, m)
                for j in range(TPW):
                    down(v, j)
                    if v == SHARED and j == 0:
                        count_ranks()

        @block.vector
        def _(dve):
            dve.wait_ge(gate_hi_done, 1)
            dve.tensor_tensor(gate_parts[:, :, 1, :], gate[:], gate_parts[:, :, 0, :].bitcast(F32), ALU.subtract)\
               .then_inc(gate_ready, 1)
            dve.wait_ge(consts, 6)

            def multiply(v, m):
                dve.wait_ge(silu_done, MC * v + m + 1)
                dve.tensor_tensor(hidden[0:HCS[m], m % 2, :], up_of(gu_ps[:, m % 2, :, 0:WT], m),
                                  gated[0:HCS[m], m % 2, :], ALU.mult).then_inc(hidden_ready, 1)

            def hidden_low(v, m):
                dve.wait_ge(hid_hi_done, MC * v + m + 1)
                dve.tensor_tensor(hid_lo[0:HCS[m], m, :], hidden[0:HCS[m], m % 2, :],
                                  hid_hi[0:HCS[m], m, :].bitcast(F32), ALU.subtract).then_inc(hid_lo_done, 1)

            def add(v, j):
                R = ROWS[j]
                tile = h_sb[0:R, bass.ds(v * TPW + j, 1), :].rearrange("p a n -> p (a n)")
                dve.wait_ge(y_done, TPW * v + j + 1)
                dve.tensor_tensor(tile, y_ps[0:R, j % 2, :], tile, ALU.add).then_inc(h_added, 1)

            def step(u, i, v):
                m = i - 1
                piece = v is not None and 0 <= m < MC
                if at := back(u, i, LOGITS):
                    dve.wait_ge(gate_done, number(at) + 1)
                    R = rows_of(at[1])
                    dve.tensor_reduce(logits[0:R, bass.ds(number(at), 1), :].rearrange("p a e -> p (a e)"),
                                      gate_ps[0:R, 0:2 * EXPERTS].rearrange("p (k e) -> p e k", k=2), AX.X, ALU.add)\
                        .then_inc(logits_ready, 1)
                if v is not None and i == 0 and not (known(v) and v == 0):
                    add(v - 1, 1)
                    add(v - 1, 2)
                if v is not None and i == TPU - 1:
                    add(v, 0)
                if piece:
                    multiply(v, m)
                if at := back(u, i, TURN):
                    k, R = at[1], rows_of(at[1])
                    dve.wait_ge(ht_hi_done, number(at) + 1)
                    dve.tensor_tensor(ht[:, k % 3, 1, :, 0:R], ht_ps[:, :, 0:R], ht[:, k % 3, 0, :, 0:R].bitcast(F32),
                                      ALU.subtract).then_inc(ht_lo_done, 1)
                if piece:
                    hidden_low(v, m)
                if at := back(u, i, 0):
                    k, R = at[1] % 3, rows_of(at[1])
                    dve.memset(turnstile[:, 0:1], 0.0)
                    dve.bn_stats(st[0:R, k, :], h_sb[0:R, bass.ds(number(at), 1), :].rearrange("p a n -> p (a n)"))\
                        .then_inc(stats_done, 1)
                    dve.wait_ge(stats_done, number(at) + 1)
                    dve.memset(turnstile[:, 1:2], 0.0)
                    dve.bn_aggr(mv[0:R, k, :], st[0:R, k, :]).then_inc(mv_done, 1)
                if known(u) and u == 0 and i >= TPU - 2:
                    for c in ((0, 1), (2, 3))[i - (TPU - 2)]:
                        dve.wait_ge(w_hi_done, c + 1)
                        dve.tensor_tensor(w13_lo[:, c, :], raw[:, c, :], w13_hi[:, c, :].bitcast(F32), ALU.subtract)\
                            .then_inc(w_lo_done, 1)
                if known(u) and u == 1 and i < MC:
                    dve.wait_ge(w_hi_done, KC + i + 1)
                    dve.tensor_tensor(w2_lo[0:HCS[i], i, :], raw2[0:HCS[i], i, :], w2_hi[0:HCS[i], i, :].bitcast(F32),
                                      ALU.subtract).then_inc(w_lo_done, 1)
            shared_steps(dve, step)

            dve.wait_ge(logits_ready, TILES)
            dve.wait_ge(consts_in, 32)
            dve.wait_ge(consts, 16 + EXPERTS + LIMITS + BLOCKS)
            done = 0

            def over_experts(a):
                return a.unsqueeze(2).broadcast_to(grid)

            def over_tiles(a):
                return a.unsqueeze(1).broadcast_to(grid)

            def then(instruction):
                nonlocal done
                done += 1
                instruction.then_inc(routed, 1)
                dve.wait_ge(routed, done)

            then(dve.tensor_reduce(best[:], logits[:], AX.X, ALU.max))
            dve.tensor_tensor(work[:], logits[:], over_experts(best[:]), ALU.subtract).then_inc(centred, 1)
            dve.wait_ge(exp_done, 1)
            then(dve.tensor_reduce(best[:], scores[:], AX.X, ALU.add))
            then(dve.reciprocal(slot_f[:], best[:]))
            then(dve.tensor_tensor(scores[:], scores[:], over_experts(slot_f[:]), ALU.mult))
            then(dve.tensor_tensor(work[:], scores[:], over_tiles(bias_row[:]), ALU.add))
            add(SHARED - 1, 1)
            add(SHARED - 1, 2)

            def hidden_parts(v, m):
                multiply(v, m)
                hidden_low(v, m)

            for k in range(2):
                hidden_parts(SHARED, k)
                then(dve.tensor_reduce(best[:], work[:], AX.X, ALU.max))
                then(dve.tensor_tensor(key[:], work[:], over_experts(best[:]), ALU.is_equal))
                then(dve.tensor_tensor(key[:], key[:], over_tiles(falling[:]), ALU.mult))
                then(dve.tensor_reduce(best[:], key[:], AX.X, ALU.max))
                then(dve.tensor_tensor(chosen[k][:], key[:], over_experts(best[:]), ALU.is_equal))
                if k == 0:
                    then(dve.scalar_tensor_tensor(work[:], chosen[0][:], -3e38, work[:], ALU.mult, ALU.add))
                then(dve.tensor_tensor(chosen[k][:], chosen[k][:], over_experts(valid[:]), ALU.mult))
            hidden_parts(SHARED, 2)
            then(dve.tensor_tensor(key[:], chosen[0][:], chosen[1][:], ALU.add))
            dve.tensor_copy(both[:], key[:]).then_inc(counts_ready, 1)
            then(dve.tensor_reduce(counts[:], key[:].rearrange("p t e -> p e t"), AX.X, ALU.add))
            dve.tensor_copy(per_row[:], counts[:]).then_inc(counts_ready, 1)
            hidden_parts(SHARED, 3)
            for k in range(2):
                then(dve.tensor_tensor(work[:], chosen[k][:], scores[:], ALU.mult))
                then(dve.tensor_reduce(payload[:, :, k, 1].bitcast(F32), work[:], AX.X, ALU.add))
            add(SHARED, 0)
            dve.wait_ge(ranks_done, 1)
            dve.wait_ge(counts_done, 1)
            then(dve.tensor_copy(counts[:], counts_ps))
            wide = [P, EXPERTS, LIMITS]
            then(dve.tensor_tensor(over[:], counts[:].unsqueeze(2).broadcast_to(wide),
                                   limits[:].unsqueeze(1).broadcast_to(wide), ALU.is_gt))
            then(dve.tensor_reduce(blocks[:], over[:], AX.X, ALU.add))
            then(dve.tensor_copy(upto[:], blocks[:]))
            for n in range(1, EXPERTS):
                then(dve.tensor_tensor(upto[:, n:n + 1], upto[:, n - 1:n], blocks[:, n:n + 1], ALU.add))
            then(dve.tensor_tensor(start[:], upto[:], blocks[:], ALU.subtract))
            then(dve.tensor_scalar(start[:], start[:], float(SLOTS), None, ALU.mult))
            then(dve.tensor_tensor(rank[:], ranks_ps,
                                   over_tiles(start[:]), ALU.add))
            for k in range(2):
                then(dve.tensor_tensor(work[:], chosen[k][:], rank[:], ALU.mult))
                then(dve.tensor_reduce(slot_f[:], work[:], AX.X, ALU.add))
                dve.tensor_copy(slots[:, k, :], slot_f[:]).then_inc(slots_ready, 1)
                dve.wait_ge(slots_ready, k + 1)
            wide = [P, BLOCKS, EXPERTS]
            then(dve.tensor_tensor(passed[:], block_no[:].unsqueeze(2).broadcast_to(wide),
                                   upto[:].unsqueeze(1).broadcast_to(wide), ALU.is_ge))
            then(dve.tensor_reduce(expert_f[:], passed[:], AX.X, ALU.add))
            dve.tensor_scalar(expert_of[:], expert_f[0:1, :], float(EXPERTS - 1), None, ALU.min).then_inc(slots_ready, 1)
            dve.tensor_scalar(turnstile[:, 0:1], turnstile[:, 0:1], 1.0, None, ALU.mult).then_inc(slots_ready, 1)

            add(SHARED, 1)
            add(SHARED, 2)
            for v in range(SHARED + 1, WIN):
                for m in range(MC):
                    hidden_parts(v, m)
                for j in range(TPW):
                    add(v, j)


def run_experts(nc, w1, w2, w3, ident, rows, table, expert_of, routed_out):
    with ExitStack() as ctx:
        def sb(name, shape, dt=F32):
            return ctx.enter_context(nc.sbuf_tensor(name, shape, dt))

        def sem(name):
            return ctx.enter_context(nc.semaphore(name))

        HALVES = SLOTS // P
        w13 = {"up": w3, "gate": w1}
        raw = sb("eraw", [P, KC, 2 * HID])
        raw2 = sb("eraw2", [P, MC, DIM])
        w13_hi = sb("ew13_hi", [P, 2, KC, 2 * HID], F32R)
        w13_lo = sb("ew13_lo", [P, 2, KC, 2 * HID], F32R)
        w2_hi = sb("ew2_hi", [P, 2, MC, DIM], F32R)
        w2_lo = sb("ew2_lo", [P, 2, MC, DIM], F32R)
        entry = sb("entry", [P, 2, HALVES, 2], U32)
        gathered = sb("gathered", [P, 2, HALVES, DIM])
        xt_hi = sb("ext_hi", [P, 2, KC, SLOTS], F32R)
        xt_lo = sb("ext_lo", [P, 2, KC, SLOTS], F32R)
        gated = sb("egated", [P, 2, SLOTS])
        hidden = sb("ehidden", [P, 2, SLOTS])
        hid_hi = sb("ehid_hi", [P, MC, SLOTS], F32R)
        hid_lo = sb("ehid_lo", [P, MC, SLOTS], F32R)
        y = sb("y", [P, HALVES, DIM])
        turnstile = sb("eturnstile", [P, 2])
        xt_ps = ctx.enter_context(nc.psum_tensor("ext_ps", [P, HALVES, KC, P], F32))
        gu_ps = ctx.enter_context(nc.psum_tensor("egu_ps", [P, MC, 2, SLOTS], F32))
        y_ps = ctx.enter_context(nc.psum_tensor("ey_ps", [P, HALVES, DIM], F32))

        w_in = [sem(f"ew_in{c}") for c in range(KC)]
        w_hi_done = sem("ew_hi_done")
        w_lo_done = sem("ew_lo_done")
        entry_in = sem("entry_in")
        turnstile_set = sem("turnstile_set")
        gathered_in = [sem(f"gathered_in{k}") for k in range(2)]
        scaled = sem("scaled")
        turned = sem("eturned")
        turned_hi = sem("eturned_hi")
        turned_lo = sem("eturned_lo")
        gu_done = sem("egu_done")
        silu_done = sem("esilu_done")
        hidden_ready = sem("ehidden_ready")
        hid_hi_done = sem("ehid_hi_done")
        hid_lo_done = sem("ehid_lo_done")
        down_done = sem("edown_done")
        y_done = sem("ey_done")
        y_taken = sem("y_taken")
        y_stored = [sem(f"y_stored{k}") for k in range(HALVES)]

        BTURNS = BLOCKS // 2
        assert BLOCKS % 2 == 0

        def steps(eng, step):
            def three(u, i):
                step(*(earlier(u, i, n, BTURNS, 2) for n in range(3)))
            run_steps(eng, BTURNS, 2, 2, three, peeled=2)

        def count(at):
            return at[0] * 2 + at[1]

        def is_first(at, n=1):
            return isinstance(at[0], int) and count(at) < n

        block = ctx.enter_context(nc.Block())

        @block.sync
        def _(sp):
            def step(after, front, rear):
                if after:
                    f = count(after)
                    e = sp.value_load(expert_of[0:1, bass.ds(f, 1)], min_val=0, max_val=EXPERTS - 1)
                    for c in range(KC):
                        if not is_first(after):
                            sp.wait_ge(w_lo_done, KC * (f - 1) + c + 1)
                        for at, w, cols in PARTS:
                            sp.dma_start(raw[:, c, at:at + cols.stop - cols.start],
                                         w13[w][bass.ds(e, 1), c * P:c * P + P, cols]
                                         .rearrange("a p n -> (a p) n")).then_inc(w_in[c], 16)
                        sp.dma_start(raw2[0:HCS[c], c, :], w2[bass.ds(e, 1), c * P:c * P + HCS[c], :]
                                     .rearrange("a p n -> (a p) n")).then_inc(w_in[c], 16)
            steps(sp, step)

        @block.gpsimd
        def _(pool):
            pool.memset(turnstile[:], 0.0).then_inc(turnstile_set, 1)
            pool.wait_ge(turnstile_set, 1)

            def step(after, front, rear):
                if front:
                    (u, i), f = front, count(front)
                    if not is_first(front, 2):
                        pool.wait_ge(turned, HALVES * (f - 1))
                    pool.dma_start(entry[:, i], table[bass.ds(f * SLOTS, SLOTS), :]
                                   .rearrange("(h p) w -> p h w", p=P)).then_inc(entry_in, 16)
                    pool.wait_ge(entry_in, 16 * (f + 1))
                    if not is_first(front):
                        pool.wait_ge(turnstile_set, f + 1)
                    pool.tensor_tensor(turnstile[:, 0:1], turnstile[:, 1:2], turnstile[:, 1:2], ALU.mult)\
                        .then_inc(turnstile_set, 1)
                    for half in range(HALVES):
                        pool.indirect_dma_start(out=gathered[:, i, half, :], out_offset=None, in_=rows[:, :],
                                                in_offset=bass.IndirectOffsetOnAxis(ap=entry[:, i, half, 0:1], axis=0))\
                            .then_inc(gathered_in[i], 16)
            steps(pool, step)

        @block.scalar
        def _(act):
            def step(after, front, rear):
                f, r = front and count(front), rear and count(rear)

                def weights(at, c):
                    i, n = at[1], count(at)
                    act.wait_ge(w_in[c], 64 * (n + 1))
                    if c == 0 and not is_first(at, 2):
                        act.wait_ge(gu_done, MC * (n - 1))
                    act.copy(w13_hi[:, i, c], raw[:, c]).then_inc(w_hi_done, 1)
                    if c == 0 and not is_first(at, 2):
                        act.wait_ge(down_done, (MC - 1) * (n - 2) + 1)
                    if c == 1 and not is_first(at, 2):
                        act.wait_ge(y_done, HALVES * (n - 1))
                    act.copy(w2_hi[0:HCS[c], i, c, :], raw2[0:HCS[c], c, :]).then_inc(w_hi_done, 1)

                def rows_high(half):
                    act.wait_ge(turned, HALVES * f + half + 1)
                    act.copy(xt_hi[:, front[1], :, half * P:half * P + P], xt_ps[:, half]).then_inc(turned_hi, 1)

                def silu(m):
                    act.wait_ge(gu_done, MC * r + m + 1)
                    if m >= 2 or not is_first(rear):
                        act.wait_ge(hidden_ready, MC * r + m - 1)
                    act.activation(gated[0:HCS[m], m % 2, :], gate_of(gu_ps[:, m], m), ACT.Silu).then_inc(silu_done, 1)

                def hidden_high(m):
                    act.wait_ge(hidden_ready, MC * r + m + 1)
                    if m == 0 and not is_first(rear):
                        act.wait_ge(y_done, HALVES * r)
                    act.copy(hid_hi[0:HCS[m], m, :], hidden[0:HCS[m], m % 2, :]).then_inc(hid_hi_done, 1)

                def take(half):
                    act.wait_ge(y_done, HALVES * r + half + 1)
                    if not is_first(rear):
                        act.wait_ge(y_stored[half], 16 * r)
                    act.copy(y[:, half, :], y_ps[:, half, :]).then_inc(y_taken, 1)

                def store(half):
                    act.wait_ge(y_taken, HALVES * r + half + 1)
                    act.dma_start(routed_out[bass.ds(r * SLOTS + half * P, P), :], y[:, half, :])\
                        .then_inc(y_stored[half], 16)

                for m in range(MC):
                    if rear:
                        silu(m)
                    if front and m + 1 < MC:
                        weights(front, m + 1)
                    if rear:
                        hidden_high(m)
                if front:
                    for half in range(HALVES):
                        rows_high(half)
                if after:
                    weights(after, 0)
                if rear:
                    for half in range(HALVES):
                        take(half)
                        store(half)
            steps(act, step)
            for stored in y_stored:
                act.wait_ge(stored, 16 * BLOCKS)

        @block.tensor
        def _(pe):
            def step(after, front, rear):
                f, r = front and count(front), rear and count(rear)

                def gate_and_up(m):
                    i = rear[1]
                    if m == 0:
                        pe.wait_ge(turned_lo, HALVES * (r + 1))
                    if not is_first(rear):
                        pe.wait_ge(hidden_ready, MC * (r - 1) + m + 1)
                    for k, cols in enumerate(products_of(m)):
                        for c in range(KC):
                            if m == 0 and k == 0:
                                pe.wait_ge(w_lo_done, KC * r + c + 1)
                            w, wl = w13_hi[:, i, c, cols], w13_lo[:, i, c, cols]
                            for q, (lhs, rhs) in enumerate(((w, xt_hi), (wl, xt_hi), (w, xt_lo))):
                                mm = pe.matmul(gu_ps[:, m, k, :], lhs, rhs[:, i, c, :], start=c == 0 and q == 0,
                                               stop=c == KC - 1 and q == 2)
                    mm.then_inc(gu_done, 1)

                def turn(half):
                    i = front[1]
                    pe.wait_ge(scaled, HALVES * f + half + 1)
                    if rear:
                        pe.wait_ge(turned_lo, HALVES * (f - 1) + half + 1)
                    for c in range(KC):
                        mm = pe.transpose(xt_ps[:, half, c, :], gathered[:, i, half, c * P:c * P + P], ident[:])
                    mm.then_inc(turned, 1)

                def down(c):
                    i = rear[1]
                    if c == 0 and not is_first(rear):
                        pe.wait_ge(y_taken, HALVES * r)
                    pe.wait_ge(hid_lo_done, MC * r + c + 1)
                    for half in range(HALVES):
                        tok = slice(half * P, half * P + P)
                        h, hl = hid_hi[0:HCS[c], c, tok], hid_lo[0:HCS[c], c, tok]
                        for q, (lhs, rhs) in enumerate(((h, w2_hi), (hl, w2_hi), (h, w2_lo))):
                            mm = pe.matmul(y_ps[:, half, :], lhs, rhs[0:HCS[c], i, c, :], start=c == 0 and q == 0,
                                           stop=c == MC - 1 and q == 2)
                        if c == MC - 1:
                            mm.then_inc(y_done, 1)
                    if c < MC - 1:
                        mm.then_inc(down_done, 1)

                for m in range(MC):
                    if rear:
                        gate_and_up(m)
                if front:
                    for half in range(HALVES):
                        turn(half)
                if rear:
                    for c in range(MC):
                        down(c)
            steps(pe, step)

        @block.vector
        def _(dve):
            def step(after, front, rear):
                f, r = front and count(front), rear and count(rear)

                def weights(at, c):
                    i = at[1]
                    dve.wait_ge(w_hi_done, 2 * (KC * count(at) + c + 1))
                    dve.tensor_tensor(w13_lo[:, i, c], raw[:, c], w13_hi[:, i, c].bitcast(F32), ALU.subtract)
                    dve.tensor_tensor(w2_lo[0:HCS[c], i, c, :], raw2[0:HCS[c], c, :],
                                      w2_hi[0:HCS[c], i, c, :].bitcast(F32), ALU.subtract)\
                        .then_inc(w_lo_done, 1)

                def scale(half):
                    i = front[1]
                    if half == 0:
                        dve.wait_ge(gathered_in[i], 16 * HALVES * (front[0] + 1))
                    x = gathered[:, i, half, :]
                    dve.tensor_scalar(x, x, entry[:, i, half, 1:2].bitcast(F32), None, ALU.mult).then_inc(scaled, 1)

                def rows_low(half):
                    dve.wait_ge(turned_hi, HALVES * f + half + 1)
                    i, cols = front[1], slice(half * P, half * P + P)
                    dve.tensor_tensor(xt_lo[:, i, :, cols], xt_ps[:, half], xt_hi[:, i, :, cols].bitcast(F32),
                                      ALU.subtract).then_inc(turned_lo, 1)

                def multiply(m):
                    dve.wait_ge(silu_done, MC * r + m + 1)
                    dve.tensor_tensor(hidden[0:HCS[m], m % 2, :], up_of(gu_ps[:, m], m), gated[0:HCS[m], m % 2, :], ALU.mult)\
                        .then_inc(hidden_ready, 1)

                def hidden_low(m):
                    dve.wait_ge(hid_hi_done, MC * r + m + 1)
                    dve.tensor_tensor(hid_lo[0:HCS[m], m, :], hidden[0:HCS[m], m % 2, :],
                                      hid_hi[0:HCS[m], m, :].bitcast(F32), ALU.subtract).then_inc(hid_lo_done, 1)

                for m in range(MC):
                    if rear:
                        multiply(m)
                    if front and m + 1 < MC:
                        weights(front, m + 1)
                    if front and m == (1 if rear else 0):
                        for half in range(HALVES):
                            scale(half)
                    if rear:
                        hidden_low(m)
                if front:
                    for half in range(HALVES):
                        rows_low(half)
                if after:
                    weights(after, 0)
            steps(dve, step)


def combine(nc, h_sb, slots, routed_out, out):
    RING = 4
    flat = out.rearrange("b p d -> (b p) d")
    with ExitStack() as ctx:
        picked = ctx.enter_context(nc.sbuf_tensor("picked", [P, RING, 2, DIM], F32))
        picked_in = [ctx.enter_context(nc.semaphore(f"picked_in{k}")) for k in range(RING)]
        added = ctx.enter_context(nc.semaphore("added"))
        stored = ctx.enter_context(nc.semaphore("out_stored"))
        block = ctx.enter_context(nc.Block())

        @block.gpsimd
        def _(pool):
            for n in range(TILES):
                R = ROWS[n % TPW]
                if n >= RING:
                    pool.wait_ge(added, 2 * (n - RING + 1))
                for k in range(2):
                    pool.indirect_dma_start(out=picked[0:R, n % RING, k, :], out_offset=None, in_=routed_out[:, :],
                                            in_offset=bass.IndirectOffsetOnAxis(ap=slots[0:R, k, n:n + 1], axis=0))\
                        .then_inc(picked_in[n % RING], 16)

        @block.vector
        def _(dve):
            for n in range(TILES):
                R = ROWS[n % TPW]
                dve.wait_ge(picked_in[n % RING], 32 * (n // RING + 1))
                for k in range(2):
                    if k:
                        dve.wait_ge(added, 2 * n + 1)
                    dve.tensor_tensor(h_sb[0:R, n, :], h_sb[0:R, n, :], picked[0:R, n % RING, k, :], ALU.add)\
                        .then_inc(added, 1)

        @block.sync
        def _(sp):
            for n in range(TILES):
                w, j = divmod(n, TPW)
                sp.wait_ge(added, 2 * n + 2)
                sp.dma_start(flat[w * WT + P * j:w * WT + P * j + ROWS[j], :], h_sb[0:ROWS[j], n, :])\
                    .then_inc(stored, 16)
            sp.wait_ge(stored, 16 * TILES)


def build(nc, x, W, b, g1, b1, g2, b2, Wq, Wk, Wv, Wo, gate_w, w1, w2, w3, sw1, sw2, sw3, bias, out):
    normed_t = nc.dram_tensor("normed_t", (WIN, P, 2, KC, WT), F32).ap()
    rows = nc.dram_tensor("rows", (TOK, DIM), F32).ap()
    table = nc.dram_tensor("table", (BLOCKS * SLOTS, 2), U32).ap()
    routed_out = nc.dram_tensor("routed_out", (BLOCKS * SLOTS, DIM), F32).ap()
    with ExitStack() as ctx:
        ident = ctx.enter_context(nc.sbuf_tensor("ident", [P, P], F32))
        h_sb = ctx.enter_context(nc.sbuf_tensor("h_sb", [P, WIN * TPW, DIM], F32))
        constants(nc, ident)
        tokenise(nc, x, W, b, g1, b1, g2, b2, ident, h_sb, normed_t)
        attend(nc, Wq, Wk, Wv, Wo, ident, h_sb, normed_t)
        slots = ctx.enter_context(nc.sbuf_tensor("slots", [P, 2, TILES], U32))
        expert_of = ctx.enter_context(nc.sbuf_tensor("expert_of", [1, BLOCKS], U32))
        route_and_share(nc, gate_w, bias, sw1, sw2, sw3, ident, h_sb, normed_t, rows, table, slots, expert_of)
        run_experts(nc, w1, w2, w3, ident, rows, table, expert_of, routed_out)
        combine(nc, h_sb, slots, routed_out, out)


def constants(nc, ident):
    with nc.semaphore("cleared") as cleared, nc.Block() as block:
        @block.gpsimd
        def _(pool):
            pool.memset(ident[:], 0.0).then_inc(cleared, 1)
            pool.wait_ge(cleared, 1)
            pool.affine_select(out=ident[:], in_=ident[:], compare_op=ALU.not_equal, fill=1.0, base=0,
                               pattern=[[-1, P]], channel_multiplier=1)


_INS = ['x', 'L0_tok_W', 'L0_tok_b', 'L0_tok_g1', 'L0_tok_b1', 'L0_tok_g2', 'L0_tok_b2', 'L0_attn_Wq', 'L0_attn_Wk',
        'L0_attn_Wv', 'L0_attn_Wo', 'L0_ffn_gate_w', 'L0_ffn_w1', 'L0_ffn_w2', 'L0_ffn_w3', 'L0_ffn_sw1',
        'L0_ffn_sw2', 'L0_ffn_sw3', 'L0_ffn_expert_bias']


def kernel(**inputs):
    import numpy as _np
    import concourse.bacc as _bacc
    from concourse.bass_utils import run_bass_kernel_spmd as _run

    nc = _bacc.Bacc("TRN2", target_bir_lowering=False, num_devices=1)
    arrays, args = {}, []
    for name in _INS:
        a = _np.ascontiguousarray(inputs[name])
        arrays[f"in_{name}"] = a
        args.append(nc.dram_tensor(f"in_{name}", a.shape, mybir.dt.from_np(a.dtype), kind="ExternalInput").ap())
    args.append(nc.dram_tensor("out_dram", (BATCH, NPATCH, DIM), F32, kind="ExternalOutput").ap())
    build(nc, *args)
    return _run(nc, [arrays], core_ids=[0]).results[0]["out_dram"]
```
